# Optimizing a Trainium2 kernel written in Bass

```python
import numpy as np
import jax
import jax.numpy as jnp

def _softmax(x, axis=-1):
    return jax.nn.softmax(x, axis=axis)

def _gelu(x):
    return jax.nn.gelu(x, approximate=True)

def _silu(x):
    return jax.nn.silu(x)

def _sigmoid(x):
    return jax.nn.sigmoid(x)

def _layernorm(x, axis=-1, eps=1e-05):
    m = jnp.mean(x, axis=axis, keepdims=True)
    v = jnp.var(x, axis=axis, keepdims=True)
    return (x - m) / jnp.sqrt(v + eps)

def _scatter_add(tgt, idx, src, axis=0):
    return tgt.at[idx].add(src)

def _segment_sum(src, seg, n):
    return jax.ops.segment_sum(src, seg, n)
kernel_name = 'mk_gnn_ffn_d1_gnn_r32_2986a3'

def setup_inputs(seed: int=0):
    np.random.seed(seed)
    _w = jnp.asarray

    def _rec_inputs():
        import jax
        import jax.numpy as jnp
        _gk = jax.random.key(seed)
        x = -0.0001126 + 1 * jax.random.normal(jax.random.fold_in(_gk, 1), (10000, 768), jnp.float32)
        src = jax.random.randint(jax.random.fold_in(_gk, 2), (10000,), 0, 10000, jnp.int32)
        dst = jax.random.randint(jax.random.fold_in(_gk, 3), (10000,), 0, 10000, jnp.int32)
        _o = jnp.argsort(dst, stable=True)
        src = src[_o]
        dst = dst[_o]
        return (x, src, dst)
    x, src, dst = _rec_inputs()

    def _L0_gnn_setup():
        import jax, jax.numpy as jnp
        import numpy as np
        N_NODES = 10000
        N_EDGES = 2500
        IN_DIM, HID, OUT_DIM, HEADS = (768, 512, 768, 4)
        NEG_SLOPE = 0.2

        def _gat_layer(x, src, dst, W, a_src, a_dst, b, heads, d_out, concat):
            N = x.shape[0]
            h = (x @ W).reshape(N, heads, d_out)
            as_n = jnp.einsum('nhd,hd->nh', h, a_src)
            ad_n = jnp.einsum('nhd,hd->nh', h, a_dst)
            e = jax.nn.leaky_relu(as_n[src] + ad_n[dst], NEG_SLOPE)
            e_max = jax.lax.stop_gradient(jax.ops.segment_max(e, dst, num_segments=N))
            ex = jnp.exp(e - e_max[dst])
            denom = jax.ops.segment_sum(ex, dst, num_segments=N)
            alpha = ex / (denom[dst] + 1e-16)
            msg = alpha[:, :, None] * h[src]
            out = jax.ops.segment_sum(msg, dst, num_segments=N)
            out = out.reshape(N, heads * d_out) if concat else out.mean(axis=1)
            return out + b
        key = jax.random.key(seed)
        ks = jax.random.split(key, 10)
        g = 0.05
        return {'x': jax.random.normal(ks[0], (N_NODES, IN_DIM), jnp.float32), 'edge_index': jax.random.randint(ks[1], (2, N_EDGES), 0, N_NODES, jnp.int64), 'W1': jax.random.normal(ks[2], (IN_DIM, HEADS * HID), jnp.float32) * g, 'a1_src': jax.random.normal(ks[3], (HEADS, HID), jnp.float32) * g, 'a1_dst': jax.random.normal(ks[4], (HEADS, HID), jnp.float32) * g, 'b1': jnp.zeros((HEADS * HID,), jnp.float32), 'W2': jax.random.normal(ks[5], (HEADS * HID, OUT_DIM), jnp.float32) * g, 'a2_src': jax.random.normal(ks[6], (1, OUT_DIM), jnp.float32) * g, 'a2_dst': jax.random.normal(ks[7], (1, OUT_DIM), jnp.float32) * g, 'b2': jnp.zeros((OUT_DIM,), jnp.float32)}
    _L0_gnn_all = _L0_gnn_setup()
    _L0_gnn_in = {k: v for k, v in _L0_gnn_all.items() if k in ('W1', 'a1_src', 'a1_dst', 'b1', 'W2', 'a2_src', 'a2_dst', 'b2')}
    del _L0_gnn_all

    def _L0_ffn_setup():
        import math
        import jax, jax.numpy as jnp
        import numpy as np
        EMBED_CHOICES = [384, 576, 768]
        RATIO_CHOICES = [2, 3, 4]
        E_MAX = 768
        H_MAX = 96

        def new_gelu(x):
            c = math.sqrt(2.0 / math.pi)
            return 0.5 * x * (1.0 + jnp.tanh(c * (x + 0.044715 * x * x * x)))

        def _mixed_coeffs(alpha_e, alpha_r):
            h_idx = jnp.arange(H_MAX)
            d_idx = jnp.arange(E_MAX)
            C0 = jnp.zeros((H_MAX, E_MAX), jnp.float32)
            c0b = jnp.zeros((H_MAX,), jnp.float32)
            C1 = jnp.zeros((E_MAX, H_MAX), jnp.float32)
            c1b = jnp.zeros((E_MAX,), jnp.float32)
            for i, e in enumerate(EMBED_CHOICES):
                m_in = (d_idx < e).astype(jnp.float32)
                for j, r in enumerate(RATIO_CHOICES):
                    a = alpha_e[i] * alpha_r[j]
                    m_out = (h_idx < r * e).astype(jnp.float32)
                    C0 = C0 + a * (m_out[:, None] * m_in[None, :])
                    c0b = c0b + a * m_out
                    C1 = C1 + a * (m_in[:, None] * m_out[None, :])
                    c1b = c1b + a * m_in
            return (C0, c0b, C1, c1b)
        key = jax.random.key(seed)
        ks = jax.random.split(key, 6)
        x = jax.random.normal(ks[0], (8, 64, E_MAX), jnp.float32)
        w_fc = jax.random.normal(ks[1], (H_MAX, E_MAX), jnp.float32) * 0.02
        b_fc = jnp.zeros((H_MAX,), jnp.float32)
        w_proj = jax.random.normal(ks[2], (E_MAX, H_MAX), jnp.float32) * 0.02
        b_proj = jnp.zeros((E_MAX,), jnp.float32)
        alpha_e = jax.nn.softmax(jax.random.normal(ks[3], (3,), jnp.float32))
        alpha_r = jax.nn.softmax(jax.random.normal(ks[4], (3,), jnp.float32))
        return {'x': x, 'w_fc': w_fc, 'b_fc': b_fc, 'w_proj': w_proj, 'b_proj': b_proj, 'alpha_e': alpha_e, 'alpha_r': alpha_r}
    _L0_ffn_all = _L0_ffn_setup()
    _L0_ffn_in = {k: v for k, v in _L0_ffn_all.items() if k in ('w_fc', 'b_fc', 'w_proj', 'b_proj', 'alpha_e', 'alpha_r')}
    del _L0_ffn_all
    return {'x': x, 'src': src, 'dst': dst, 'L0_gnn_W1': _L0_gnn_in['W1'], 'L0_gnn_a1_src': _L0_gnn_in['a1_src'], 'L0_gnn_a1_dst': _L0_gnn_in['a1_dst'], 'L0_gnn_b1': _L0_gnn_in['b1'], 'L0_gnn_W2': _L0_gnn_in['W2'], 'L0_gnn_a2_src': _L0_gnn_in['a2_src'], 'L0_gnn_a2_dst': _L0_gnn_in['a2_dst'], 'L0_gnn_b2': _L0_gnn_in['b2'], 'L0_ffn_w_fc': _L0_ffn_in['w_fc'], 'L0_ffn_b_fc': _L0_ffn_in['b_fc'], 'L0_ffn_w_proj': _L0_ffn_in['w_proj'], 'L0_ffn_b_proj': _L0_ffn_in['b_proj'], 'L0_ffn_alpha_e': _L0_ffn_in['alpha_e'], 'L0_ffn_alpha_r': _L0_ffn_in['alpha_r']}

def reference(x, src, dst, L0_gnn_W1, L0_gnn_a1_src, L0_gnn_a1_dst, L0_gnn_b1, L0_gnn_W2, L0_gnn_a2_src, L0_gnn_a2_dst, L0_gnn_b2, L0_ffn_w_fc, L0_ffn_b_fc, L0_ffn_w_proj, L0_ffn_b_proj, L0_ffn_alpha_e, L0_ffn_alpha_r):
    import jax
    import jax.numpy as jnp

    def _L0_gnn_ref(x, edge_index, W1, a1_src, a1_dst, b1, W2, a2_src, a2_dst, b2):
        import jax, jax.numpy as jnp
        import numpy as np
        N_NODES = 10000
        N_EDGES = 2500
        IN_DIM, HID, OUT_DIM, HEADS = (768, 512, 768, 4)
        NEG_SLOPE = 0.2

        def _gat_layer(x, src, dst, W, a_src, a_dst, b, heads, d_out, concat):
            N = x.shape[0]
            h = (x @ W).reshape(N, heads, d_out)
            as_n = jnp.einsum('nhd,hd->nh', h, a_src)
            ad_n = jnp.einsum('nhd,hd->nh', h, a_dst)
            e = jax.nn.leaky_relu(as_n[src] + ad_n[dst], NEG_SLOPE)
            e_max = jax.lax.stop_gradient(jax.ops.segment_max(e, dst, num_segments=N))
            ex = jnp.exp(e - e_max[dst])
            denom = jax.ops.segment_sum(ex, dst, num_segments=N)
            alpha = ex / (denom[dst] + 1e-16)
            msg = alpha[:, :, None] * h[src]
            out = jax.ops.segment_sum(msg, dst, num_segments=N)
            out = out.reshape(N, heads * d_out) if concat else out.mean(axis=1)
            return out + b
        N = x.shape[0]
        loops = jnp.arange(N, dtype=edge_index.dtype)
        src = jnp.concatenate([edge_index[0], loops])
        dst = jnp.concatenate([edge_index[1], loops])
        h = _gat_layer(x, src, dst, W1, a1_src, a1_dst, b1, HEADS, HID, True)
        h = jax.nn.elu(h)
        out = _gat_layer(h, src, dst, W2, a2_src, a2_dst, b2, 1, OUT_DIM, False)
        return out

    def _L0_ffn_ref(x, w_fc, b_fc, w_proj, b_proj, alpha_e, alpha_r):
        import math
        import jax, jax.numpy as jnp
        import numpy as np
        EMBED_CHOICES = [384, 576, 768]
        RATIO_CHOICES = [2, 3, 4]
        E_MAX = 768
        H_MAX = 96

        def new_gelu(x):
            c = math.sqrt(2.0 / math.pi)
            return 0.5 * x * (1.0 + jnp.tanh(c * (x + 0.044715 * x * x * x)))

        def _mixed_coeffs(alpha_e, alpha_r):
            h_idx = jnp.arange(H_MAX)
            d_idx = jnp.arange(E_MAX)
            C0 = jnp.zeros((H_MAX, E_MAX), jnp.float32)
            c0b = jnp.zeros((H_MAX,), jnp.float32)
            C1 = jnp.zeros((E_MAX, H_MAX), jnp.float32)
            c1b = jnp.zeros((E_MAX,), jnp.float32)
            for i, e in enumerate(EMBED_CHOICES):
                m_in = (d_idx < e).astype(jnp.float32)
                for j, r in enumerate(RATIO_CHOICES):
                    a = alpha_e[i] * alpha_r[j]
                    m_out = (h_idx < r * e).astype(jnp.float32)
                    C0 = C0 + a * (m_out[:, None] * m_in[None, :])
                    c0b = c0b + a * m_out
                    C1 = C1 + a * (m_in[:, None] * m_out[None, :])
                    c1b = c1b + a * m_in
            return (C0, c0b, C1, c1b)
        C0, c0b, C1, c1b = _mixed_coeffs(alpha_e, alpha_r)
        W0 = w_fc * C0
        b0 = b_fc * c0b
        h = jnp.einsum('bte,he->bth', x, W0) + b0
        h = new_gelu(h)
        W1 = w_proj * C1
        b1 = b_proj * c1b
        out = jnp.einsum('bth,eh->bte', h, W1) + b1
        return out
    edge_index = jnp.stack([src, dst])
    x = x + _L0_gnn_ref(_layernorm(x, axis=-1), edge_index, L0_gnn_W1, L0_gnn_a1_src, L0_gnn_a1_dst, L0_gnn_b1, L0_gnn_W2, L0_gnn_a2_src, L0_gnn_a2_dst, L0_gnn_b2)
    x = x + _L0_ffn_ref(_layernorm(x, axis=-1)[None], L0_ffn_w_fc, L0_ffn_b_fc, L0_ffn_w_proj, L0_ffn_b_proj, L0_ffn_alpha_e, L0_ffn_alpha_r)[0]
    return x

_drawn_inputs = setup_inputs


def setup_inputs(seed=0):
    import zlib

    import numpy as np

    out = dict(_drawn_inputs(seed))
    spreads = {'L0_gnn_b1': (0.0, 0.1),
     'L0_gnn_b2': (0.0, 0.1),
     'L0_ffn_b_fc': (0.0, 0.1),
     'L0_ffn_b_proj': (0.0, 0.1)}
    factors = {}
    for name, (base, spread) in spreads.items():
        noise = np.random.default_rng([zlib.crc32(name.encode()), seed]).standard_normal(out[name].shape)
        drawn = base * np.exp(spread * noise) if base else spread * noise
        out[name] = jnp.asarray(drawn.astype(out[name].dtype))
    for name, factor in factors.items():
        out[name] = (out[name] * factor).astype(out[name].dtype)
    return out
```

```python
from contextlib import ExitStack

import numpy as np
import concourse.bass as bass
from concourse import mybir

ALU = mybir.AluOpType
ACT = mybir.ActivationFunctionType
AX = mybir.AxisListType
F32 = mybir.dt.float32
F32R = mybir.dt.float32r
F16 = mybir.dt.float16
I32 = mybir.dt.int32

N = 10000
E = 10000
D = 768
HEADS, HID = 4, 512
DH = HEADS * HID
F = 96
DC = D // 128
KC = DH // 128

EP, EC = 125, 80
SN = 500
NS = N // SN
TN = 125
NT = SN // TN
WN = 50
NW = N // WN
WPS = SN // WN
WE = 128 - WN
XE = 64
REC = 12
MAX_CHUNKS = E // XE + 1
PAD = 128
CHUNKS = NW + 1
TABLE = 2 * (NW + 1)
FAR = 1.0e6
LOW = -1.0e30
SX = 2.0 ** 11
SA = 2.0 ** 14
W2C = D + 4
EPS = 1e-5


class Chain:

    def __init__(self, eng, sem, base=0):
        self.eng, self.sem, self.base, self.n = eng, sem, base, 0

    def put(self, ins):
        self.n += 1
        return ins.then_inc(self.sem, 1)

    def wait(self):
        self.eng.wait_ge(self.sem, self.base + self.n)

    def link(self, ins):
        self.put(ins)
        self.wait()


class Mem:

    def __init__(self, nc, ctx, tag):
        self.nc, self.ctx, self.tag, self.sems = nc, ctx, tag, []
        ctx.callback(self.free_semaphores)

    def free_semaphores(self):
        self.nc.clear_and_free_semaphores(self.sems)
        self.nc.all_engine_barrier()

    def sb(self, name, shape, dt=F32):
        return self.ctx.enter_context(self.nc.sbuf_tensor(f"{self.tag}_{name}", shape, dt))

    def ps(self, name, shape, dt=F32):
        return self.ctx.enter_context(self.nc.psum_tensor(f"{self.tag}_{name}", shape, dt))

    def sem(self, name):
        self.sems.append(self.nc.alloc_semaphore(f"{self.tag}_{name}"))
        return self.sems[-1]


def row_parts(rows):
    cut = rows // 16 * 16
    return [(0, cut), (cut, rows)] if rows % 16 else [(0, rows)]


def persistent(nc, ctx, c):
    c.ident = ctx.enter_context(nc.sbuf_tensor("ident", [128, 128], F32))
    c.ones = ctx.enter_context(nc.sbuf_tensor("ones", [128, 128], F32))
    c.table = ctx.enter_context(nc.sbuf_tensor("table", [1, TABLE], I32))


def layer_weights(nc, ctx, c):
    c.b1 = ctx.enter_context(nc.sbuf_tensor("b1c", [128, KC], F32))
    c.b1s = ctx.enter_context(nc.sbuf_tensor("b1s", [128, KC], F32))
    c.scale = ctx.enter_context(nc.sbuf_tensor("scale", [128, 16], F32))
    c.w1h, c.w1l = (ctx.enter_context(nc.sbuf_tensor(n, [128, DC, DH], F16)) for n in ("w1h", "w1l"))
    c.w2h, c.w2l = (ctx.enter_context(nc.sbuf_tensor(n, [128, KC, W2C], F16)) for n in ("w2h", "w2l"))


def stage_constants(nc, c):
    with ExitStack() as ctx:
        m = Mem(nc, ctx, "cst")
        zeroed, done = m.sem("zeroed"), m.sem("done")
        block = ctx.enter_context(nc.Block())

        @block.gpsimd
        def _(pool):
            nc.gpsimd.memset(c.ident[:], 0.0).then_inc(zeroed, 1)
            nc.gpsimd.memset(c.ones[:], 1.0).then_inc(done, 1)
            pool.wait_ge(zeroed, 1)
            nc.gpsimd.affine_select(out=c.ident[:], in_=c.ident[:], compare_op=ALU.not_equal, fill=1.0, base=0,
                                    pattern=[[-1, 128]], channel_multiplier=1).then_inc(done, 1)
            pool.wait_ge(done, 2)


def stage_normalise(nc, c, io, dr):
    with ExitStack() as ctx:
        m = Mem(nc, ctx, "nrm")
        w1 = m.sb("w1", [128, DC, DH])
        asrc, adst = m.sb("asrc", [128, DH]), m.sb("adst", [128, DH])
        junk = m.sb("junk", [128, 2, HID])
        v1 = m.sb("v1", [128, DC, 2 * HEADS])
        xb = m.sb("xb", [TN, 2, NT, D])
        parts = m.sb("parts", [TN, 2, NT, 2, D], F16)
        stats = m.sb("stats", [TN, NT, 2, 6])
        mv = m.sb("mv", [TN, NT, 2])
        ve = m.sb("ve", [TN, NT])
        std = m.sb("std", [TN, NT])
        rstd = m.sb("rstd", [TN, NT])
        rough, sq, dummy = m.sb("rough", [TN, NT]), m.sb("sq", [TN, NT]), m.sb("dummy", [1, 1])
        xt = m.sb("xt", [128, 2, DC, 128])
        logit = m.sb("logit", [TN, 2, NT, 2 * HEADS])
        pt = [m.ps(f"pt{i}", [128, 2, 512]) for i in range(2)]
        pl = m.ps("pl", [TN, NT, 2 * HEADS])
        weights = m.sem("weights")
        xin = [m.sem(f"xin{b}") for b in range(2)]
        stored = [m.sem(f"stored{b}") for b in range(2)]
        v_ready, chain = m.sem("v_ready"), m.sem("chain")
        var_ready, std_ready = m.sem("var_ready"), m.sem("std_ready")
        xs_ready, hi_ready, lo_ready = m.sem("xs_ready"), m.sem("hi_ready"), m.sem("lo_ready")
        turned, xt_ready, logits_read, logit_ready = (m.sem("turned"), m.sem("xt_ready"),
                                                      m.sem("logits_read"), m.sem("logit_ready"))
        block = ctx.enter_context(nc.Block())
        x_rows = io["x"].rearrange("(s p t) d -> s p t d", p=TN, t=NT)
        t_rows = dr.parts.rearrange("(s p t) d -> s p (t d)", p=TN, t=NT)
        l_rows = dr.logit1.rearrange("(s p t) d -> s p (t d)", p=TN, t=NT)

        @block.sync
        def _(sp):
            def load(s, b):
                for lo, hi in row_parts(TN):
                    sp.dma_start(xb[lo:hi, b], x_rows[s, lo:hi]).then_inc(xin[b], 16)

            def store(s, b):
                sp.wait_ge(hi_ready, NT * s + NT)
                sp.wait_ge(lo_ready, NT * s + NT)
                for lo, hi in row_parts(TN):
                    sp.dma_start(t_rows[s, lo:hi], parts[lo:hi, b].rearrange("p t k d -> p (t k d)")).then_inc(stored[b], 16)
                sp.wait_ge(logit_ready, s + 1)
                for lo, hi in row_parts(TN):
                    sp.dma_start(l_rows[s, lo:hi], logit[lo:hi, b].rearrange("p t k -> p (t k)")).then_inc(stored[b], 16)

            for k in range(DC):
                sp.dma_start(w1[:, k], io["W1"][128 * k:128 * k + 128, :]).then_inc(weights, 16)
            for tile, src in ((asrc, "a1_src"), (adst, "a1_dst")):
                sp.dma_start(tile[:], io[src].rearrange("(a h) d -> a (h d)", a=1).broadcast_to([128, DH])).then_inc(weights, 16)
            load(0, 0)
            load(1, 1)

            def step(j, last):
                for b in range(2):
                    s = 2 * j + b
                    store(s, b)
                    if not last:
                        sp.wait_ge(turned, NT * s + NT)
                        load(s + 2, b)

            step(0, False)
            with sp.Fori(1, NS // 2 - 1) as j:
                step(j, False)
            step(NS // 2 - 1, True)
            for b in range(2):
                sp.wait_ge(stored[b], 64 * (NS // 2))

        @block.vector
        def _(dve):
            ch = Chain(dve, chain)
            nc.vector.memset(xt[:], 0.0).then_inc(v_ready, 1)
            dve.wait_ge(weights, 16 * (DC + 2))
            for k in range(DC):
                for side, a in ((0, asrc), (1, adst)):
                    for h in range(HEADS):
                        cols = slice(h * HID, h * HID + HID)
                        at = side * HEADS + h
                        if ch.n >= 2:
                            dve.wait_ge(chain, ch.n - 1)
                        ch.put(nc.vector.tensor_tensor_reduce(
                            out=junk[:, ch.n % 2], in0=w1[:, k, cols], in1=a[:, cols], scale=1.0, scalar=0.0,
                            op0=ALU.mult, op1=ALU.add, accum_out=v1[:, k, at:at + 1]))
            first_n = ch.n
            per = 2 * NT + NT + 5

            def step(j, first):
                for b in range(2):
                    s = 2 * j + b
                    q = Chain(dve, chain, s * per + first_n)
                    dve.wait_ge(xin[b], 32 * (j + 1))
                    for t in range(NT):
                        for half in range(2):
                            q.put(nc.vector.bn_stats(stats[:, t, half], xb[:, b, t, half * (D // 2):(half + 1) * (D // 2)]))
                    q.wait()
                    nc.vector.memset(dummy[:], 0.0)
                    for t in range(NT):
                        q.put(nc.vector.bn_aggr(mv[:, t], stats[:, t].rearrange("p a b -> p (a b)")))
                    q.wait()
                    nc.vector.tensor_scalar(ve[:], mv[:, :, 1], EPS, None, ALU.add).then_inc(var_ready, 1)
                    dve.wait_ge(std_ready, s + 1)
                    q.link(nc.vector.reciprocal(rough[:], std[:]))
                    q.link(nc.vector.tensor_tensor(sq[:], rough[:], rough[:], ALU.mult))
                    q.link(nc.vector.tensor_tensor(sq[:], sq[:], ve[:], ALU.mult))
                    q.link(nc.vector.tensor_scalar(sq[:], sq[:], -0.5, 1.5, ALU.mult, ALU.add))
                    q.link(nc.vector.tensor_tensor(rstd[:], rough[:], sq[:], ALU.mult))
                    for t in range(NT):
                        nc.vector.tensor_scalar(xb[:, b, t], xb[:, b, t], mv[:, t, 0:1], rstd[:, t:t + 1], ALU.subtract,
                                                ALU.mult).then_inc(xs_ready, 1)
                    for t in range(NT):
                        dve.wait_ge(hi_ready, NT * s + t + 1)
                        nc.vector.scalar_tensor_tensor(out=parts[:, b, t, 1], in0=xb[:, b, t], scalar=SX, in1=parts[:, b, t, 0],
                                                       op0=ALU.mult, op1=ALU.subtract).then_inc(lo_ready, 1)
                    assert q.n == per
                    dve.wait_ge(logits_read, NT * s + NT)
                    if not first:
                        dve.wait_ge(stored[b], 64 * j)
                    nc.vector.tensor_copy(logit[:, b], pl[:]).then_inc(logit_ready, 1)

            step(0, True)
            with dve.Fori(1, NS // 2) as j:
                step(j, False)

        @block.scalar
        def _(act):
            def step(j, first):
                for b in range(2):
                    s = 2 * j + b
                    act.wait_ge(var_ready, s + 1)
                    nc.scalar.activation(std[:], ve[:], ACT.Sqrt).then_inc(std_ready, 1)
                    for t in range(NT):
                        act.wait_ge(xs_ready, NT * s + t + 1)
                        if t == 0 and not first:
                            act.wait_ge(stored[b], 64 * j)
                        nc.scalar.activation(parts[:, b, t, 0], xb[:, b, t], ACT.Copy, scale=SX).then_inc(hi_ready, 1)
                        act.wait_ge(turned, NT * s + t + 1)
                        if not (first and b == 0 and t < 2):
                            act.wait_ge(logits_read, NT * s + t - 1)
                        nc.scalar.activation(xt[:, t % 2, :, 0:TN].rearrange("p (g c) n -> p g c n", g=2),
                                             pt[t % 2][:, :, 0:3 * 128].rearrange("p g (c n) -> p g c n", n=128)[:, :, :, 0:TN],
                                             ACT.Copy).then_inc(xt_ready, 1)

            act.wait_ge(v_ready, 1)
            step(0, True)
            with act.Fori(1, NS // 2) as j:
                step(j, False)

        @block.tensor
        def _(pe):
            pe.wait_ge(chain, 2 * HEADS * DC)

            def turn(s, t):
                pe.wait_ge(xs_ready, NT * s + t + 1)
                for k in range(DC):
                    o = pt[t % 2][:, k // 3, 128 * (k % 3):128 * (k % 3) + TN]
                    ins = pe.transpose(o, xcur[:, t, 128 * k:128 * k + 128], c.ident[0:TN, 0:TN])
                ins.then_inc(turned, 1)

            def logits(s, t, first):
                pe.wait_ge(xt_ready, NT * s + t + 1)
                if t == 0 and not first:
                    pe.wait_ge(logit_ready, s)
                for k in range(DC):
                    ins = pe.matmul(pl[:, t], xt[:, t % 2, k, 0:TN], v1[:, k], start=(k == 0), stop=(k == DC - 1))
                ins.then_inc(logits_read, 1)

            def step(j, first):
                nonlocal xcur
                for b in range(2):
                    s = 2 * j + b
                    xcur = xb[:, b]
                    turn(s, 0)
                    for t in range(NT):
                        if t + 1 < NT:
                            if t + 1 >= 2:
                                pe.wait_ge(xt_ready, NT * s + t)
                            turn(s, t + 1)
                        logits(s, t, first and b == 0)

            xcur = None
            step(0, True)
            with pe.Fori(1, NS // 2) as j:
                step(j, False)


class Weights:

    PIECES = 4

    def __init__(self, nc, c, io, m, dst, loaded):
        self.nc, self.c, self.io, self.dst, self.loaded = nc, c, io, dst, loaded
        self.raw = m.sb("wraw", [128, KC * W2C])
        self.w1 = self.raw[:, 0:DC * DH].rearrange("p (k n) -> p k n", k=DC)
        self.w2 = self.raw[:].rearrange("p (k n) -> p k n", k=KC)
        self.a2 = m.sb("a2", [128, 2, D])
        self.junk = m.sb("junk", [128, 2, D])
        self.top = m.sb("top", [128, 4])
        self.top_t, self.diag = m.sb("top_t", [4, 1]), m.sb("diag", [4, 4])
        self.expo, self.inv = m.sb("expo", [128, 4], I32), m.sb("inv", [128, 4], I32)
        self.edges, self.before = m.sb("edges", [EP, NW // 8, EC]), m.sb("before", [EP, NW])
        self.dstf, self.thr, self.thri = m.sb("dstf", [EP, EC]), m.sb("thr", [EP, NW]), m.sb("thri", [EP, NW], I32)
        self.row, self.count = m.sb("row", [1, NW + 1]), m.sb("count", [1, NW])
        self.counti, self.zero = m.sb("counti", [1, NW], I32), m.sb("zero", [1, NW])
        self.pm, self.pb = m.ps("pm", [4, 128]), m.ps("pb", [128, 4])
        self.pw = m.ps("pw", [1, NW])
        self.b_in, self.w1_in, self.w2_in, self.a_in = (m.sem(n) for n in ("b_in", "w1_in", "w2_in", "a_in"))
        self.steps, self.thr_ready, self.before_ready, self.summed = (m.sem(n) for n in ("steps", "thr_ready",
                                                                                      "before_ready", "summed"))
        self.top_ready, self.top_turned, self.diag_ready, self.spread = (m.sem(n) for n in (
            "top_ready", "top_turned", "diag_ready", "spread"))
        self.scale_ready, self.hi, self.lo = m.sem("scale_ready"), m.sem("hi"), m.sem("lo")

    def sync(self, sp):
        sp.dma_start(self.c.b1[:], self.io["b1"].rearrange("(k p) -> p k", p=128),
                     allow_slow_non_contiguous=True).then_inc(self.b_in, 16)
        for k in range(DC):
            sp.dma_start(self.w1[:, k], self.io["W1"][128 * k:128 * k + 128, :]).then_inc(self.w1_in, 16)
        for n, name in enumerate(("a2_src", "a2_dst")):
            sp.dma_start(self.a2[:, n], self.io[name].broadcast_to([128, D])).then_inc(self.a_in, 16)
        sp.wait_ge(self.lo, self.PIECES)
        for k in range(KC):
            sp.dma_start(self.w2[:, k, 0:D], self.io["W2"][128 * k:128 * k + 128, :]).then_inc(self.w2_in, 16)

    def gpsimd(self, pool):
        self.nc.gpsimd.iota(self.thri[:], pattern=[[WN, NW]], base=0, channel_multiplier=0).then_inc(self.thr_ready, 1)

    def parts(self, which):
        c = self.c
        flat = lambda t: t[:].rearrange("p k n -> p (k n)")
        n = DC * DH if which == 0 else KC * W2C
        step = n // self.PIECES
        hi, lo = (flat(c.w1h), flat(c.w1l)) if which == 0 else (flat(c.w2h), flat(c.w2l))
        for i in range(self.PIECES):
            at = slice(i * step, i * step + step)
            yield i, hi[:, at], lo[:, at], self.raw[:, at]

    def scalar(self, act):
        for which in range(2):
            act.wait_ge(self.scale_ready, which + 1)
            for _, hi, _, raw in self.parts(which):
                self.nc.scalar.activation(hi, raw, ACT.Copy, scale=self.c.scale[:, which:which + 1]).then_inc(self.hi, 1)

    def tensor(self, pe):
        c = self.c
        pe.wait_ge(self.before_ready, 1)
        pe.matmul(self.pw[:], c.ones[0:EP, 0:1], self.before[:], start=True, stop=True).then_inc(self.summed, 1)
        for n in range(2):
            pe.wait_ge(self.top_ready, n + 1)
            pe.transpose(self.pm[:], self.top[:], c.ident[:]).then_inc(self.top_turned, 1)
            pe.wait_ge(self.diag_ready, n + 1)
            pe.matmul(self.pb[:], c.ones[0:4, :], self.diag[:], start=True, stop=True).then_inc(self.spread, 1)

    def vector(self, dve):
        nc, c = self.nc, self.c
        ch = Chain(dve, self.steps)
        dve.wait_ge(self.thr_ready, 1)
        ch.put(nc.vector.tensor_copy(self.thr[:], self.thri[:]))
        ch.link(nc.vector.tensor_copy(self.dstf[:], self.dst[:]))
        part = NW // 8
        for i in range(8):
            ch.link(nc.vector.tensor_tensor(
                self.edges[:], self.dstf[:].rearrange("p (a c) -> p a c", a=1).broadcast_to([EP, part, EC]),
                self.thr[:, i * part:i * part + part].rearrange("p (w a) -> p w a", a=1).broadcast_to([EP, part, EC]),
                ALU.is_lt))
            ch.link(nc.vector.tensor_reduce(self.before[:, i * part:i * part + part], self.edges[:], AX.X, ALU.add))
        nc.vector.memset(self.row[:, NW:NW + 1], float(E)).then_inc(self.before_ready, 1)
        dve.wait_ge(self.summed, 1)
        ch.link(nc.vector.tensor_copy(self.row[:, 0:NW], self.pw[:]))
        ch.put(nc.vector.tensor_copy(c.table[:, 0:NW + 1], self.row[:]))
        ch.link(nc.vector.tensor_tensor(self.count[:], self.row[:, 1:NW + 1], self.row[:, 0:NW], ALU.subtract))
        ch.link(nc.vector.tensor_scalar(self.count[:], self.count[:], float(-WE), 0.0, ALU.add, ALU.max))
        ch.link(nc.vector.tensor_scalar(self.counti[:], self.count[:], float(XE - 1), None, ALU.add))
        ch.link(nc.vector.tensor_scalar(self.counti[:], self.counti[:], 6, None, ALU.arith_shift_right))
        ch.put(nc.vector.tensor_copy(self.count[:], self.counti[:]))
        ch.put(nc.vector.memset(self.zero[:], 0.0))
        ch.link(nc.vector.memset(self.row[:, 0:1], 0.0))
        ch.link(nc.vector.tensor_tensor_scan(out=self.row[:, 1:NW + 1], data0=self.zero[:], data1=self.count[:], initial=0.0,
                                             op0=ALU.add, op1=ALU.add))
        ch.put(nc.vector.tensor_copy(c.table[:, CHUNKS:TABLE], self.row[:]))

        def scales(n):
            nc.vector.memset(self.diag[:], 0.0).then_inc(self.top_ready, 1)
            dve.wait_ge(self.top_turned, n + 1)
            ch.link(nc.vector.tensor_reduce(self.top_t[:], self.pm[:], AX.X, ALU.max))
            nc.vector.tensor_scalar(self.diag[:], c.ident[0:4, 0:4], self.top_t[:], None, ALU.mult)\
                .then_inc(self.diag_ready, 1)
            dve.wait_ge(self.spread, n + 1)
            ch.link(nc.vector.tensor_copy(self.top[:], self.pb[:]))
            ch.link(nc.vector.tensor_scalar(self.top[:, 2:3], self.top[:, 0:1], float(D), self.top[:, 3:4], ALU.mult, ALU.add))
            ch.link(nc.vector.tensor_scalar(self.top[:, 2:3], self.top[:, 2:3], 1.0, 0.5, ALU.max, ALU.mult))
            ch.link(nc.vector.tensor_scalar(self.expo[:], self.top[:].bitcast(I32), 23, None, ALU.logical_shift_right))
            ch.link(nc.vector.tensor_scalar(self.expo[:], self.expo[:], -1.0, 267.0, ALU.mult, ALU.add))
            ch.link(nc.vector.tensor_scalar(self.expo[:], self.expo[:], 253.0, 1.0, ALU.min, ALU.max))
            ch.link(nc.vector.tensor_scalar(self.inv[:], self.expo[:], -1.0, 254.0, ALU.mult, ALU.add))
            ch.put(nc.vector.tensor_scalar(c.scale[:, 0:4].bitcast(I32), self.expo[:], 23, None, ALU.logical_shift_left))
            ch.link(nc.vector.tensor_scalar(c.scale[:, 4:8].bitcast(I32), self.inv[:], 23, None, ALU.logical_shift_left))
            nc.vector.memset(self.diag[:], 0.0).then_inc(self.scale_ready, 1)

        ch.link(nc.vector.memset(self.top[:], 0.0))
        dve.wait_ge(self.b_in, 16)
        ch.put(nc.vector.tensor_reduce(self.top[:, 3:4], c.b1[:], AX.X, ALU.max, apply_absolute_value=True))
        dve.wait_ge(self.w1_in, 16 * DC)
        ch.link(nc.vector.tensor_reduce(self.top[:, 0:1], self.raw[:, 0:DC * DH], AX.X, ALU.max, apply_absolute_value=True))
        scales(0)
        for i, hi, lo, raw in self.parts(0):
            dve.wait_ge(self.hi, i + 1)
            nc.vector.scalar_tensor_tensor(out=lo, in0=raw, scalar=c.scale[:, 0:1], in1=hi, op0=ALU.mult,
                                           op1=ALU.subtract).then_inc(self.lo, 1)
        dve.wait_ge(self.lo, self.PIECES)
        ch.put(nc.vector.memset(self.w2[:, :, D + 2:W2C], 0.0))
        dve.wait_ge(self.a_in, 32)
        dve.wait_ge(self.w2_in, 16 * KC)
        for k in range(KC):
            for n in range(2):
                ch.put(nc.vector.tensor_tensor_reduce(
                    out=self.junk[:, n], in0=self.w2[:, k, 0:D], in1=self.a2[:, n], scale=1.0, scalar=0.0,
                    op0=ALU.mult, op1=ALU.add, accum_out=self.w2[:, k, D + n:D + n + 1]))
            ch.wait()
        ch.link(nc.vector.tensor_reduce(self.top[:, 1:2], self.raw[:], AX.X, ALU.max, apply_absolute_value=True))
        scales(1)
        for i, hi, lo, raw in self.parts(1):
            dve.wait_ge(self.hi, self.PIECES + i + 1)
            nc.vector.scalar_tensor_tensor(out=lo, in0=raw, scalar=c.scale[:, 1:2], in1=hi, op0=ALU.mult,
                                           op1=ALU.subtract).then_inc(self.lo, 1)
        ch.put(nc.vector.tensor_scalar(c.scale[:, 8:9], c.scale[:, 4:5], 1.0 / SX, None, ALU.mult))
        ch.put(nc.vector.tensor_scalar(c.scale[:, 9:10], c.scale[:, 4:5], 1.0 / SX, c.scale[:, 2:3], ALU.mult, ALU.mult))
        ch.put(nc.vector.tensor_scalar(c.scale[:, 10:11], c.scale[:, 2:3], -1.0, None, ALU.mult))
        ch.put(nc.vector.tensor_tensor(c.scale[:, 11:12], c.scale[:, 5:6], c.scale[:, 6:7], ALU.mult))
        ch.link(nc.vector.tensor_scalar(c.b1s[:], c.b1[:], c.scale[:, 2:3], None, ALU.mult))


def stage_softmax(nc, c, io, table, rec, heads, extra=None, tag="sm"):
    H = heads
    with ExitStack() as ctx:
        m = Mem(nc, ctx, tag)
        src, dst = m.sb("src", [EP, EC], I32), m.sb("dst", [EP, EC], I32)
        prev, nxt = m.sb("prev", [EP, EC], I32), m.sb("nxt", [EP, EC], I32)
        gsrc, gdst = m.sb("gsrc", [EP, EC, 2 * H]), m.sb("gdst", [EP, EC, 2 * H])
        record = m.sb("record", [EP, EC, REC])
        pads = m.sb("pads", [PAD, REC])
        first, cont, pen_f, pen_l = (m.sb(n, [EP, EC]) for n in ("first", "cont", "pen_f", "pen_l"))
        raw, l, ls = (m.sb(n, [EP, H, EC]) for n in ("raw", "l", "ls"))
        a, b, ex, exs = (m.sb(n, [EP, H, EC]) for n in ("a", "b", "ex", "exs"))
        edge = m.sb("edge", [EP, 2, H])
        edge_t = m.sb("edge_t", [H, 2, EP])
        carry_t = m.sb("carry_t", [H, EP + 2])
        carry = m.sb("carry", [EP, H])
        zeros_t, low_t = m.sb("zeros_t", [H, EP + 2]), m.sb("low_t", [H, EP + 2])
        pe_t = m.ps("pe_t", [128, 2, 128])
        pe_b = m.ps("pe_b", [128, 128])
        loaded, init = m.sem("loaded"), m.sem("init")
        got_src, got_dst = m.sem("got_src"), m.sem("got_dst")
        chain, edge_ready, turned, carry_ready, back = (m.sem(n) for n in ("chain", "edge_ready", "turned",
                                                                         "carry_ready", "back"))
        shifted, exps, record_ready, stored = (m.sem(n) for n in ("shifted", "exps", "record_ready", "stored"))
        more = extra(nc, c, io, m, dst, loaded) if extra else None
        block = ctx.enter_context(nc.Block())
        d_lin = io["dst"]

        @block.sync
        def _(sp):
            grid = lambda ap: ap.rearrange("(p c) -> p c", c=EC)
            sp.dma_start(src[:], grid(io["src"])).then_inc(loaded, 16)
            sp.dma_start(dst[:], grid(io["dst"])).then_inc(loaded, 16)
            sp.wait_ge(init, 2)
            sp.dma_start(prev[0:1, 1:EC], d_lin[0:EC - 1].rearrange("(a c) -> a c", a=1)).then_inc(loaded, 16)
            sp.dma_start(prev[1:EP, :], grid(d_lin[EC - 1:E - 1])).then_inc(loaded, 16)
            sp.dma_start(nxt[0:EP - 1, :], grid(d_lin[1:E - EC + 1])).then_inc(loaded, 16)
            sp.dma_start(nxt[EP - 1:EP, 0:EC - 1], d_lin[E - EC + 1:E].rearrange("(a c) -> a c", a=1)).then_inc(loaded, 16)
            if more:
                more.sync(sp)
            sp.wait_ge(init, 5)
            sp.dma_start(rec[E:E + PAD, :], pads[:]).then_inc(stored, 16)
            sp.wait_ge(record_ready, 1)
            rows = rec[0:E, :].rearrange("(p c) w -> p (c w)", c=EC)
            for lo, hi in row_parts(EP):
                sp.dma_start(rows[lo:hi], record[lo:hi].rearrange("p c w -> p (c w)")).then_inc(stored, 16)
            sp.wait_ge(stored, 48)

        @block.gpsimd
        def _(pool):
            if more:
                more.gpsimd(pool)
            pool.wait_ge(loaded, 96)
            for idx, out, sem in ((src, gsrc, got_src), (dst, gdst, got_dst)):
                for k in range(EC):
                    nc.gpsimd.indirect_dma_start(out[:, k, :], None, table[:, :], bass.IndirectOffsetOnAxis(
                        ap=idx[:, k:k + 1], axis=0), bounds_check=N - 1, oob_is_err=False).then_inc(sem, 16)

        @block.vector
        def _(dve):
            ch = Chain(dve, chain)
            nc.vector.memset(prev[:], -1).then_inc(init, 1)
            nc.vector.memset(nxt[:], -1).then_inc(init, 1)
            nc.vector.memset(pads[:], 0.0).then_inc(init, 1)
            nc.vector.memset(record[:], 0.0).then_inc(init, 1)
            dve.wait_ge(init, 4)
            nc.vector.memset(pads[:, 9:10], FAR).then_inc(init, 1)
            dve.wait_ge(loaded, 96)
            ch.put(nc.vector.tensor_tensor(first[:], dst[:], prev[:], ALU.not_equal))
            ch.put(nc.vector.tensor_tensor(pen_l[:], dst[:], nxt[:], ALU.not_equal))
            ch.put(nc.vector.tensor_copy(record[:, :, 9], dst[:]))
            ch.put(nc.vector.tensor_copy(record[:, :, 10], src[:]))
            ch.wait()
            ch.put(nc.vector.tensor_copy(record[:, :, 8], first[:]))
            ch.put(nc.vector.tensor_scalar(pen_l[:], pen_l[:], LOW, None, ALU.mult))
            ch.put(nc.vector.tensor_scalar(pen_f[:], first[:], LOW, None, ALU.mult))
            ch.put(nc.vector.tensor_scalar(cont[:], first[:], -1.0, 1.0, ALU.mult, ALU.add))
            if more:
                more.vector(dve)
            dve.wait_ge(got_src, 16 * EC)
            dve.wait_ge(got_dst, 16 * EC)
            sides = gsrc[:].rearrange("p c h -> p h c"), gdst[:].rearrange("p c h -> p h c")
            for out, term in ((l, sides[0]), (ls, sides[1])):
                ch.link(nc.vector.tensor_tensor(raw[:], term[:, 0:H], sides[1][:, H:2 * H], ALU.add))
                ch.link(nc.vector.scalar_tensor_tensor(out=out[:], in0=raw[:], scalar=0.2, in1=raw[:], op0=ALU.mult,
                                                       op1=ALU.max))
            scans = [0]

            def scan(out, gate, x, op0, op1, neutral, backward):
                r = -1 if backward else 1
                n = scans[0]
                scans[0] += 1
                end = 0 if backward else EC - 1
                for h in range(H):
                    ch.put(nc.vector.tensor_tensor_scan(out=out[:, h, ::r], data0=gate[:, ::r], data1=x[:, h, ::r],
                                                        initial=neutral, op0=op0, op1=op1))
                ch.wait()
                ch.put(nc.vector.tensor_copy(edge[:, 0], out[:, :, end]))
                ch.link(nc.vector.tensor_reduce(edge[:, 1, 0:1], gate[:], AX.X, ALU.min))
                for h in range(1, H):
                    ch.put(nc.vector.tensor_copy(edge[:, 1, h:h + 1], edge[:, 1, 0:1]))
                ch.wait()
                nc.vector.tensor_copy(carry_t[:], zeros_t[:] if neutral == 0.0 else low_t[:]).then_inc(edge_ready, 1)
                dve.wait_ge(turned, n + 1)
                ch.link(nc.vector.tensor_copy(edge_t[:], pe_t[0:H, :, 0:EP]))
                dve.wait_ge(edge_ready, n + 1)
                at = slice(1, EP + 1)
                ch.link(nc.vector.tensor_tensor_scan(out=carry_t[:, at][:, ::r], data0=edge_t[:, 1, ::r],
                                                     data1=edge_t[:, 0, ::r], initial=neutral, op0=op0, op1=op1))
                nc.vector.tensor_copy(edge_t[:, 0], carry_t[:, 2:EP + 2] if backward else carry_t[:, 0:EP])\
                    .then_inc(carry_ready, 1)
                dve.wait_ge(back, n + 1)
                ch.link(nc.vector.tensor_copy(carry[:], pe_b[0:EP, 0:H]))
                for h in range(H):
                    ch.put(nc.vector.tensor_tensor_scan(out=out[:, h, ::r], data0=gate[:, ::r], data1=x[:, h, ::r],
                                                        initial=carry[:, h:h + 1], op0=op0, op1=op1))
                ch.wait()

            ch.put(nc.vector.memset(zeros_t[:], 0.0))
            ch.put(nc.vector.memset(low_t[:], LOW))
            ch.wait()
            scan(a, pen_f, l, ALU.add, ALU.max, LOW, False)
            scan(b, pen_l, a, ALU.add, ALU.max, LOW, True)
            ch.link(nc.vector.tensor_tensor(b[:], b[:], ls[:], ALU.max))
            ch.put(nc.vector.tensor_tensor(l[:], l[:], b[:], ALU.subtract))
            ch.link(nc.vector.tensor_tensor(ls[:], ls[:], b[:], ALU.subtract))
            nc.vector.memset(raw[:], 0.0).then_inc(shifted, 1)
            dve.wait_ge(exps, 2)
            scan(a, cont, ex, ALU.mult, ALU.add, 0.0, False)
            scan(b, pen_l, a, ALU.add, ALU.max, LOW, True)
            ch.link(nc.vector.tensor_tensor(b[:], b[:], exs[:], ALU.add))
            ch.link(nc.vector.tensor_scalar(b[:], b[:], 1e-16, None, ALU.add))
            ch.link(nc.vector.reciprocal(a[:], b[:]))
            by_head = lambda lo: record[:, :, lo:lo + H].rearrange("p c h -> p h c")
            ch.put(nc.vector.tensor_tensor(by_head(0), ex[:], a[:], ALU.mult))
            ch.link(nc.vector.tensor_tensor(exs[:], exs[:], a[:], ALU.mult))
            for h in range(H):
                ch.put(nc.vector.tensor_tensor(record[:, :, 4 + h], exs[:, h], first[:], ALU.mult))
            ch.wait()
            nc.vector.memset(raw[:], 0.0).then_inc(record_ready, 1)

        @block.scalar
        def _(act):
            if more:
                more.scalar(act)
            act.wait_ge(shifted, 1)
            nc.scalar.activation(ex[:], l[:], ACT.Exp).then_inc(exps, 1)
            nc.scalar.activation(exs[:], ls[:], ACT.Exp).then_inc(exps, 1)

        @block.tensor
        def _(pe):
            if more:
                more.tensor(pe)
            for n in range(4):
                pe.wait_ge(edge_ready, n + 1)
                pe.transpose(pe_t[0:H, 0, 0:EP], edge[:, 0], c.ident[0:EP, 0:EP])
                pe.transpose(pe_t[0:H, 1, 0:EP], edge[:, 1], c.ident[0:EP, 0:EP]).then_inc(turned, 1)
                pe.wait_ge(carry_ready, n + 1)
                pe.transpose(pe_b[0:EP, 0:H], edge_t[:, 0], c.ident[0:H, 0:H]).then_inc(back, 1)


STEPS = NT * KC
XPER = 19
AT_STEP = {2 + 6 * i: i for i in range(WPS)}


def second_phase():
    for g in range(STEPS):
        if g in AT_STEP:
            yield "window", AT_STEP[g]
        if g % KC == KC - 1:
            yield "tile", g // KC


def table_value(eng, c, at, top):
    return eng.value_load(c.table[0:1, bass.ds(at, 1)], min_val=0, max_val=top)


def windows_with_extras(eng, c, first, count, chunk):
    before = lambda w: table_value(eng, c, CHUNKS + w, MAX_CHUNKS)
    with eng.If(before(first + count) > before(first)):
        with eng.Fori(0, count) as i:
            lo, hi = before(first + i), before(first + i + 1)
            with eng.If(hi > lo):
                with eng.Fori(lo, hi) as k:
                    chunk(i, first + i, k)


def load_extra_slots(nc, sp, c, rec, slots, sem, w, k):
    start = table_value(sp, c, w, E) + (k - table_value(sp, c, CHUNKS + w, MAX_CHUNKS)) * XE + WE
    start = nc.s_assert_within(start, 0, E, skip_runtime_bounds_check_because="a chunk starts at an edge of its window")
    for half in range(2):
        sp.dma_start(slots[XE * half:XE * half + XE, :], rec[bass.ds(start, XE), :]).then_inc(sem, 16)


def extra_slot_math(nc, ch, slots, rel, far, off, idx, idx_ready, w, heads):
    edges, nodes = slice(0, XE), slice(XE, 2 * XE)
    ch.link(nc.vector.tensor_tensor(rel[:], slots[:, 9:10], off, ALU.add))
    ch.link(nc.vector.tensor_scalar(far[:], rel[:], float(WN), FAR, ALU.is_ge, ALU.mult))
    nc.vector.tensor_tensor(idx[edges, :], slots[edges, 10:11], far[edges, :], ALU.add).then_inc(idx_ready, 1)
    nc.vector.tensor_tensor(idx[nodes, :], slots[nodes, 9:10], far[nodes, :], ALU.add).then_inc(idx_ready, 1)
    ch.put(nc.vector.tensor_copy(w[edges, :], slots[edges, 0:heads]))
    ch.link(nc.vector.tensor_scalar(w[nodes, :], slots[nodes, 4:4 + heads], slots[nodes, 8:9], None, ALU.subtract))


def stage_layers(nc, c, io, dr):
    with ExitStack() as ctx:
        m = Mem(nc, ctx, "lay")
        zh, zl = (m.sb(n, [128, DC, HEADS, SN], F16) for n in ("zh", "zl"))
        gh, gl = (m.sb(n, [128, KC, SN + 4], F16) for n in ("gh", "gl"))
        rows = m.sb("rows", [128, 2, 2 * D], F16)
        slots = m.sb("slots", [128, WPS, REC])
        rel, far, own = m.sb("rel", [128, WPS]), m.sb("far", [128, WPS]), m.sb("own", [128, WPS])
        woff, wself = m.sb("woff", [128, WPS]), m.sb("wself", [128, WPS])
        is_edge, is_self = m.sb("is_edge", [128, 1]), m.sb("is_self", [128, 1])
        step_off, step_self = m.sb("step_off", [128, 1]), m.sb("step_self", [128, 1])
        place, posi = m.sb("place", [128, 1]), m.sb("posi", [128, 128], I32)
        pos = m.sb("pos", [128, 128])
        idx = m.sb("idx", [128, WPS], I32)
        mask = m.sb("mask", [128, 2, 128])
        near = m.sb("near", [128, 2, WN], F16)
        w, wh, wl = m.sb("w", [128, WPS, HEADS]), m.sb("wh", [128, WPS, HEADS], F16), m.sb("wl", [128, WPS, HEADS], F16)
        ah, al = (m.sb(n, [128, 2, HEADS, WN], F16) for n in ("ah", "al"))
        ex, y = m.sb("ex", [128, 2, SN]), m.sb("y", [128, 2, SN])
        h2 = m.sb("h2", [128, 2, W2C])
        xslots, xoff = m.sb("xslots", [128, REC]), m.sb("xoff", [128, WPS])
        xrel, xfar, xidx = m.sb("xrel", [128, 1]), m.sb("xfar", [128, 1]), m.sb("xidx", [128, 1], I32)
        xw, xwh, xwl = m.sb("xw", [128, HEADS]), m.sb("xwh", [128, HEADS], F16), m.sb("xwl", [128, HEADS], F16)
        pz = [m.ps(f"pz{i}", [128, 512]) for i in range(3)]
        pm = [m.ps(f"pm{i}", [128, 512]) for i in range(4)]
        look = m.ps("look", [128, WPS, 5])
        (init, posed, slots_in, idx_ready, mask_ready, looked, a_ready, z_done, zh_ready, zl_ready, p1_done, ex_ready,
         y_ready, g_ready, gh_ready, gl_ready, tile_done, h2a, h2b, chain, setup, held, paused,
         xslots_free, xslots_in, xidx_ready, xgathered, xa_ready, xz_done, xz_added, xchain) = (m.sem(n) for n in (
             "init", "posed", "slots_in", "idx_ready", "mask_ready", "looked", "a_ready", "z_done", "zh_ready", "zl_ready",
             "p1_done", "ex_ready", "y_ready", "g_ready", "gh_ready", "gl_ready", "tile_done", "h2a", "h2b", "chain",
             "setup", "held", "paused",
             "xslots_free", "xslots_in", "xidx_ready", "xgathered", "xa_ready", "xz_done", "xz_added", "xchain"))
        gathered = [m.sem(f"gathered{b}") for b in range(2)]
        h2_out = [m.sem(f"h2_out{b}") for b in range(2)]
        block = ctx.enter_context(nc.Block())

        def window_shape(tile, k, i):
            return tile[:, 2 * k:2 * k + 2, :, WN * i:WN * i + WN].rearrange("p k h n -> p (k h) n")

        @block.sync
        def _(sp):
            def load_slots(q, first):
                if not first:
                    sp.wait_ge(a_ready, WPS * q)
                for i in range(WPS):
                    start = sp.value_load(c.table[0:1, bass.ds(WPS * q + i, 1)], min_val=0, max_val=E)
                    sp.dma_start(slots[0:WE, i, :], dr.rec1[bass.ds(start, WE), :]).then_inc(slots_in, 16)

            def extra_chunk(i, w, k):
                sp.wait_ge(xslots_free, k + 1)
                sp.sem_inc(paused, 1)
                load_extra_slots(nc, sp, c, dr.rec1, xslots, xslots_in, w, k)

            def body(s, first, last):
                windows_with_extras(sp, c, WPS * s, WPS, extra_chunk)
                if not last:
                    load_slots(s + 1, False)
                for t in range(NT):
                    sp.wait_ge(h2a, NT * s + t + 1)
                    sp.wait_ge(h2b, NT * s + t + 1)
                    for lo, hi in row_parts(TN):
                        node = SN * s + TN * t + lo
                        sp.dma_start(dr.h2[bass.ds(node, hi - lo), :], h2[lo:hi, t % 2, 0:D]).then_inc(h2_out[t % 2], 16)
                        sp.dma_start(dr.logit2[bass.ds(node, hi - lo), :], h2[lo:hi, t % 2, D:D + 2])\
                            .then_inc(h2_out[t % 2], 16)

            sp.wait_ge(init, 3)
            load_slots(0, True)
            body(0, True, False)
            with sp.Fori(1, NS - 1) as s:
                body(s, False, False)
            body(NS - 1, False, True)
            for b in range(2):
                sp.wait_ge(h2_out[b], 64 * (NT // 2) * NS)

        @block.gpsimd
        def _(pool):
            nc.gpsimd.iota(posi[:], pattern=[[1, 128]], base=-WE, channel_multiplier=0).then_inc(posed, 1)
            nc.gpsimd.iota(idx[:, 0:1], pattern=[[0, 1]], base=-WE, channel_multiplier=1).then_inc(posed, 1)

            def hold(sem, value):
                pool.wait_ge(sem, value)
                pool.sem_inc(held, 1)

            pool.wait_ge(posed, 2)

            def gather(q, first):
                hold(idx_ready, q + 1)
                for i in range(WPS):
                    if not (first and i < 2):
                        hold(z_done, 3 * (WPS * q + i - 1))
                    nc.gpsimd.indirect_dma_start(rows[:, i % 2, :], None, dr.parts[:, :], bass.IndirectOffsetOnAxis(
                        ap=idx[:, i:i + 1], axis=0), bounds_check=N - 1, oob_is_err=False).then_inc(gathered[i % 2], 16)

            def extra_chunk(i, w, k):
                hold(xidx_ready, 2 * k + 2)
                nc.gpsimd.indirect_dma_start(rows[:, 0, :], None, dr.parts[:, :], bass.IndirectOffsetOnAxis(
                    ap=xidx[:, 0:1], axis=0), bounds_check=N - 1, oob_is_err=False).then_inc(xgathered, 16)

            gather(0, True)
            with pool.Fori(1, NS) as q:
                windows_with_extras(pool, c, WPS * (q - 1), WPS, extra_chunk)
                gather(q, False)
            windows_with_extras(pool, c, WPS * (NS - 1), WPS, extra_chunk)

        @block.vector
        def _(dve):
            ch = Chain(dve, setup)
            nc.vector.memset(rows[:], 0.0).then_inc(init, 1)
            nc.vector.memset(gh[:, :, SN:], 0.0).then_inc(init, 1)
            nc.vector.memset(gl[:, :, SN:], 0.0)
            dve.wait_ge(posed, 2)
            ch.put(nc.vector.tensor_copy(pos[:], posi[:]))
            ch.put(nc.vector.memset(slots[:], 0.0))
            ch.link(nc.vector.tensor_copy(place[:], idx[:, 0:1]))
            ch.put(nc.vector.tensor_scalar(is_self[:], place[:], 0.0, None, ALU.is_ge))
            ch.link(nc.vector.tensor_scalar(is_edge[:], place[:], 0.0, None, ALU.is_lt))
            ch.put(nc.vector.tensor_scalar(step_off[:], is_edge[:], float(-SN), None, ALU.mult))
            ch.put(nc.vector.tensor_scalar(step_self[:], is_self[:], float(SN), None, ALU.mult))
            nc.vector.memset(xslots[:], 0.0).then_inc(xslots_free, 1)
            for i in range(WPS):
                ch.put(nc.vector.memset(xoff[:, i:i + 1], float(SN - WN * i)))
                ch.put(nc.vector.tensor_scalar(woff[:, i:i + 1], is_edge[:], float(-WN * i), None, ALU.mult))
                ch.put(nc.vector.tensor_scalar(wself[:, i:i + 1], place[:], float(WN * i), is_self[:, 0:1], ALU.add, ALU.mult))
                for h in range(HEADS):
                    ch.put(nc.vector.tensor_copy(slots[:, i, h:h + 1], is_self[:]))
                ch.put(nc.vector.tensor_scalar(slots[:, i, 9:10], place[:], 0.0, None, ALU.max))
            ch.wait()
            nc.vector.memset(near[:], 0.0).then_inc(init, 1)
            per = 10 + WPS

            def slot_math(qc, q, first):
                dve.wait_ge(slots_in, 16 * WPS * (q + 1))
                if not first:
                    for b in range(2):
                        dve.wait_ge(gathered[b], 16 * (WPS // 2) * q)
                qc.put(nc.vector.tensor_tensor(rel[:], slots[:, :, 9], woff[:], ALU.add))
                qc.link(nc.vector.tensor_tensor(own[:], slots[:, :, 10], wself[:], ALU.add))
                qc.put(nc.vector.tensor_scalar(woff[:], woff[:], step_off[:, 0:1], None, ALU.add))
                qc.put(nc.vector.tensor_scalar(wself[:], wself[:], step_self[:, 0:1], None, ALU.add))
                qc.put(nc.vector.tensor_scalar(xoff[:], xoff[:], float(-SN), None, ALU.add))
                qc.link(nc.vector.tensor_scalar(far[:], rel[:], float(WN), FAR, ALU.is_ge, ALU.mult))
                nc.vector.tensor_tensor(idx[:], own[:], far[:], ALU.add).then_inc(idx_ready, 1)

            def window_mask(q, i, first):
                if not (first and i < 2):
                    dve.wait_ge(looked, WPS * q + i - 1)
                nc.vector.tensor_scalar(mask[:, i % 2], pos[:], rel[:, i:i + 1], None, ALU.is_equal).then_inc(mask_ready, 1)

            def weights(qc, q):
                dve.wait_ge(looked, WPS * (q + 1))
                qc.link(nc.vector.tensor_tensor(w[:], slots[:, :, 0:HEADS], look[:, :, 4:5].broadcast_to([128, WPS, HEADS]),
                                                ALU.subtract))
                qc.link(nc.vector.tensor_tensor(w[:], w[:], look[:, :, 0:HEADS], ALU.add))
                qc.link(nc.vector.tensor_scalar(wh[:], w[:], SA, None, ALU.mult))
                qc.link(nc.vector.scalar_tensor_tensor(out=wl[:], in0=w[:], scalar=SA, in1=wh[:], op0=ALU.mult,
                                                       op1=ALU.subtract))

            def spread(qc, q, i, first):
                if not (first and i < 2):
                    dve.wait_ge(z_done, 3 * (WPS * q + i - 1))
                qc.link(nc.vector.tensor_scalar(near[:, i % 2], pos[:, WE:], rel[:, i:i + 1], None, ALU.is_equal))
                m_ = near[:, i % 2:i % 2 + 1, :].broadcast_to([128, HEADS, WN])
                of = lambda t: t[:, i, :].rearrange("p (h a) -> p h a", a=1).broadcast_to([128, HEADS, WN])
                nc.vector.tensor_tensor(ah[:, i % 2], m_, of(wh), ALU.mult)
                nc.vector.tensor_tensor(al[:, i % 2], m_, of(wl), ALU.mult).then_inc(a_ready, 1)

            def low_parts(q, i):
                for k in range(3):
                    dve.wait_ge(zh_ready, 3 * (WPS * q + i) + k + 1)
                    nc.vector.scalar_tensor_tensor(
                        out=window_shape(zl, k, i), in0=pz[k][:, 0:2 * HEADS * WN].rearrange("p (k n) -> p k n", n=WN),
                        scalar=1.0 / SA, in1=window_shape(zh, k, i), op0=ALU.mult, op1=ALU.subtract).then_inc(zl_ready, 1)

            def extra_chunk(i, w, k):
                xc = Chain(dve, xchain, XPER * k)
                dve.wait_ge(xslots_in, 32 * k + 32)
                extra_slot_math(nc, xc, xslots, xrel, xfar, xoff[:, bass.ds(i, 1)], xidx, xidx_ready, xw, HEADS)
                xc.put(nc.vector.tensor_scalar(near[:, 0], pos[:, WE:], xrel[:, 0:1], None, ALU.is_equal))
                xc.link(nc.vector.tensor_scalar(xwh[:], xw[:], SA, None, ALU.mult))
                xc.link(nc.vector.scalar_tensor_tensor(out=xwl[:], in0=xw[:], scalar=SA, in1=xwh[:], op0=ALU.mult,
                                                       op1=ALU.subtract))
                nc.vector.memset(xfar[:], 0.0).then_inc(xslots_free, 1)
                of = lambda t: t[:].rearrange("p (h a) -> p h a", a=1).broadcast_to([128, HEADS, WN])
                m_ = near[:, 0:1, :].broadcast_to([128, HEADS, WN])
                nc.vector.tensor_tensor(ah[:, 0], m_, of(xwh), ALU.mult)
                nc.vector.tensor_tensor(al[:, 0], m_, of(xwl), ALU.mult).then_inc(xa_ready, 1)
                dve.wait_ge(xz_done, k + 1)
                for j in range(3):
                    z_hi, z_lo = (t[:, 2 * j:2 * j + 2, :, bass.ds(WN * i, WN)].rearrange("p k h n -> p (k h) n")
                                  for t in (zh, zl))
                    as_window = lambda t: t[:, 0:2 * HEADS * WN].rearrange("p (k n) -> p k n", n=WN)
                    part, total = as_window(ex[:, 0]), as_window(y[:, 0])
                    xc.link(nc.vector.scalar_tensor_tensor(out=part, in0=as_window(pz[j]), scalar=1.0 / SA, in1=z_hi,
                                                           op0=ALU.mult, op1=ALU.add))
                    xc.link(nc.vector.tensor_tensor(total, part, z_lo, ALU.add))
                    xc.link(nc.vector.tensor_scalar(z_hi, total, 1.0, None, ALU.mult))
                    xc.link(nc.vector.tensor_tensor(z_lo, total, z_hi, ALU.subtract))
                nc.vector.memset(xfar[:], 0.0).then_inc(xz_added, 1)
                assert xc.n == XPER, xc.n

            def elu(gc, s, k, first):
                dve.wait_ge(ex_ready, KC * s + k + 1)
                gc.link(nc.vector.tensor_scalar(ex[:, k % 2], ex[:, k % 2], 1.0, c.scale[:, 2:3], ALU.min, ALU.mult))
                dve.wait_ge(y_ready, KC * s + k + 1)
                nc.vector.scalar_tensor_tensor(out=y[:, k % 2], in0=ex[:, k % 2], scalar=c.scale[:, 10:11], in1=y[:, k % 2],
                                               op0=ALU.add, op1=ALU.max).then_inc(g_ready, 1)

            def elu_low(s, k):
                dve.wait_ge(gh_ready, KC * s + k + 1)
                nc.vector.tensor_tensor(gl[:, k, 0:SN], y[:, k % 2], gh[:, k, 0:SN], ALU.subtract).then_inc(gl_ready, 1)

            def body(s, first, last):
                q = s + 1
                windows_with_extras(dve, c, WPS * s, WPS, extra_chunk)
                gc = Chain(dve, chain, KC * s)
                qc = Chain(dve, setup, q * per + ch.n)
                for k in range(KC):
                    elu(gc, s, k, first)
                    if k:
                        elu_low(s, k - 1)
                    if last:
                        continue
                    if k == 2:
                        slot_math(qc, q, False)
                    if 3 <= k < 3 + WPS:
                        if k == 3:
                            qc.wait()
                        window_mask(q, k - 3, False)
                    if k == 15:
                        weights(qc, q)
                elu_low(s, KC - 1)
                if not last:
                    spread(qc, q, 0, False)
                    spread(qc, q, 1, False)
                for what, n in second_phase():
                    if what == "window" and not last:
                        low_parts(q, n)
                        if n + 2 < WPS:
                            spread(qc, q, n + 2, False)
                    if what == "tile":
                        dve.wait_ge(tile_done, NT * s + n + 1)
                        if not (first and n < 2):
                            dve.wait_ge(h2_out[n % 2], 64 * ((NT * s + n) // 2) if isinstance(s, int) else
                                        64 * (NT // 2) * s + 64 * (n // 2))
                        nc.vector.tensor_scalar(h2[:, n % 2, 512:D + 2], pm[2 * (n % 2) + 1][:, 0:D + 2 - 512],
                                                c.scale[:, 11:12], None, ALU.mult).then_inc(h2b, 1)
                assert last or qc.n == per, qc.n

            qc = Chain(dve, setup, ch.n)
            slot_math(qc, 0, True)
            qc.wait()
            for i in range(WPS):
                window_mask(0, i, True)
            weights(qc, 0)
            spread(qc, 0, 0, True)
            spread(qc, 0, 1, True)
            for i in range(WPS):
                low_parts(0, i)
                if i + 2 < WPS:
                    spread(qc, 0, i + 2, True)
            assert qc.n == per, qc.n
            body(0, True, False)
            with dve.Fori(1, NS - 1) as s:
                body(s, False, False)
            body(NS - 1, False, True)

        @block.scalar
        def _(act):
            def high_parts(q, i):
                for k in range(3):
                    act.wait_ge(z_done, 3 * (WPS * q + i) + k + 1)
                    nc.scalar.activation(window_shape(zh, k, i), pz[k][:, 0:2 * HEADS * WN].rearrange("p (k n) -> p k n", n=WN),
                                         ACT.Copy, scale=1.0 / SA).then_inc(zh_ready, 1)

            def body(s, first, last):
                for k in range(KC):
                    act.wait_ge(p1_done, KC * s + k + 1)
                    if not (first and k < 2):
                        act.wait_ge(gl_ready, KC * s + k - 1)
                    p = pm[k % 4][:, 0:SN]
                    nc.scalar.activation(ex[:, k % 2], p, ACT.Exp, bias=c.b1[:, k:k + 1], scale=c.scale[:, 8:9])\
                        .then_inc(ex_ready, 1)
                    nc.scalar.activation(y[:, k % 2], p, ACT.Identity, bias=c.b1s[:, k:k + 1], scale=c.scale[:, 9:10])\
                        .then_inc(y_ready, 1)
                    if k:
                        high(s, k - 1)
                high(s, KC - 1)
                for what, n in second_phase():
                    if what == "window" and not last:
                        high_parts(s + 1, n)
                    if what == "tile":
                        act.wait_ge(tile_done, NT * s + n + 1)
                        if not (first and n < 2):
                            act.wait_ge(h2_out[n % 2], 64 * (NT // 2) * s + 64 * (n // 2))
                        nc.scalar.activation(h2[:, n % 2, 0:512], pm[2 * (n % 2)][:], ACT.Copy, scale=c.scale[:, 11:12])\
                            .then_inc(h2a, 1)

            def high(s, k):
                act.wait_ge(g_ready, KC * s + k + 1)
                nc.scalar.activation(gh[:, k, 0:SN], y[:, k % 2], ACT.Copy).then_inc(gh_ready, 1)

            for i in range(WPS):
                high_parts(0, i)
            body(0, True, False)
            with act.Fori(1, NS - 1) as s:
                body(s, False, False)
            body(NS - 1, False, True)

        @block.tensor
        def _(pe):
            pe.wait_ge(init, 2)

            def look_up(q, i):
                pe.wait_ge(mask_ready, WPS * q + i + 1)
                pe.matmul(look[:, i], mask[:, i % 2], slots[:, i, 4:9], start=True, stop=True).then_inc(looked, 1)

            def window_products(d, b):
                o = pz[d // 2][:, d % 2 * HEADS * WN:(d % 2 + 1) * HEADS * WN]
                high, low = (rows[:, b, part * D + 128 * d:part * D + 128 * d + 128] for part in range(2))
                flat = lambda t: t[:, b].rearrange("p h n -> p (h n)")
                pe.matmul(o, high, flat(ah), start=True, stop=False)
                pe.matmul(o, high, flat(al), start=False, stop=False)
                return pe.matmul(o, low, flat(ah), start=False, stop=True)

            def window(q, i, first):
                pe.wait_ge(gathered[i % 2], 16 * (WPS // 2) * q + 16 * (i // 2 + 1))
                pe.wait_ge(a_ready, WPS * q + i + 1)
                for k in range(3):
                    if not (first and i == 0):
                        pe.wait_ge(zl_ready, 3 * (WPS * q + i - 1) + k + 1)
                    for d in (2 * k, 2 * k + 1):
                        ins = window_products(d, i % 2)
                    ins.then_inc(z_done, 1)

            def extra_chunk(i, w, k):
                pe.wait_ge(xgathered, 16 * k + 16)
                pe.wait_ge(xa_ready, k + 1)
                for d in range(DC):
                    ins = window_products(d, 0)
                ins.then_inc(xz_done, 1)
                pe.wait_ge(xz_added, k + 1)

            def body(s, first, last):
                q = s + 1
                pe.wait_ge(zl_ready, 3 * WPS * (s + 1))
                windows_with_extras(pe, c, WPS * s, WPS, extra_chunk)
                for k in range(KC):
                    h = k // (KC // HEADS)
                    if k >= 4:
                        pe.wait_ge(y_ready, KC * s + k - 3)
                    elif not first:
                        pe.wait_ge(h2a, NT * s - 1 + k // 2)
                        pe.wait_ge(h2b, NT * s - 1 + k // 2)
                    for d in range(DC):
                        cols = slice(128 * k, 128 * k + 128)
                        o = pm[k % 4][:, 0:SN]
                        pe.matmul(o, c.w1h[:, d, cols], zh[:, d, h], start=(d == 0), stop=False)
                        pe.matmul(o, c.w1h[:, d, cols], zl[:, d, h], start=False, stop=False)
                        ins = pe.matmul(o, c.w1l[:, d, cols], zh[:, d, h], start=False, stop=(d == DC - 1))
                    ins.then_inc(p1_done, 1)
                    if 4 <= k < 4 + WPS and not last:
                        look_up(q, k - 4)
                for g in range(STEPS):
                    t, k = g // KC, g % KC
                    if g in AT_STEP and not last:
                        window(q, AT_STEP[g], False)
                    oa, ob = pm[2 * (t % 2)], pm[2 * (t % 2) + 1]
                    if k == 0:
                        if t < 2:
                            pe.wait_ge(y_ready, KC * s + 14 + 2 * t)
                        else:
                            pe.wait_ge(h2a, NT * s + t - 1)
                            pe.wait_ge(h2b, NT * s + t - 1)
                    if t == 0:
                        pe.wait_ge(gl_ready, KC * s + k + 1)
                    nodes = slice(TN * t, TN * t + 128)
                    for n, (x, wt) in enumerate(((gh, c.w2h), (gh, c.w2l), (gl, c.w2h))):
                        go = dict(start=(k == 0 and n == 0), stop=(k == KC - 1 and n == 2))
                        pe.matmul(oa[:], x[:, k, nodes], wt[:, k, 0:512], **go)
                        ins = pe.matmul(ob[:, 0:D + 2 - 512], x[:, k, nodes], wt[:, k, 512:D + 2], **go)
                    if k == KC - 1:
                        ins.then_inc(tile_done, 1)

            for i in range(WPS):
                look_up(0, i)
            for i in range(WPS):
                window(0, i, True)
            body(0, True, False)
            with pe.Fori(1, NS - 1) as s:
                body(s, False, False)
            body(NS - 1, False, True)


def stage_extra_rows(nc, c, io, dr):
    with ExitStack() as ctx:
        m = Mem(nc, ctx, "more")
        slots, rows, acc = m.sb("slots", [128, REC]), m.sb("rows", [128, D]), m.sb("acc", [WN, D])
        rel, far, idx, w_ = m.sb("rel", [128, 1]), m.sb("far", [128, 1]), m.sb("idx", [128, 1], I32), m.sb("w", [128, 1])
        offi, off = m.sb("offi", [128, NW], I32), m.sb("off", [128, NW])
        posi, pos, att = m.sb("posi", [128, 128], I32), m.sb("pos", [128, 128]), m.sb("att", [128, 128])
        pa, pb = m.ps("pa", [128, 512]), m.ps("pb", [128, D - 512])
        (posed, copied, slots_free, slots_in, acc_in, idx_ready, gathered, att_ready, summed, added, stored, chain,
         held) = (m.sem(n) for n in ("posed", "copied", "slots_free", "slots_in", "acc_in", "idx_ready", "gathered",
                                     "att_ready", "summed", "added", "stored", "chain", "held"))
        block = ctx.enter_context(nc.Block())
        COPIES = 4
        any_chunk = lambda eng: eng.If(table_value(eng, c, CHUNKS + NW, MAX_CHUNKS) > 0)

        @block.sync
        def _(sp):
            def chunk(i, w, k):
                sp.wait_ge(slots_free, k + 1)
                sp.sem_inc(held, 1)
                load_extra_slots(nc, sp, c, dr.rec2, slots, slots_in, w, k)
                part = bass.ds(WN * w, WN)
                sp.dma_start(acc[:], dr.x_more[part, :]).then_inc(acc_in, 16)
                sp.wait_ge(added, k + 1)
                sp.sem_inc(held, 1)
                sp.dma_start(dr.x_more[part, :], acc[:]).then_inc(stored, 16)
                sp.wait_ge(stored, 16 * k + 16)
                sp.sem_inc(held, 1)

            with any_chunk(sp):
                for n in range(COPIES):
                    part = slice(n * (N // COPIES), (n + 1) * (N // COPIES))
                    sp.dma_start(dr.x_more[part, :], io["x"][part, :]).then_inc(copied, 16)
                sp.wait_ge(copied, 16 * COPIES)
                windows_with_extras(sp, c, 0, NW, chunk)

        @block.gpsimd
        def _(pool):
            def chunk(i, w, k):
                pool.wait_ge(idx_ready, 2 * k + 2)
                pool.sem_inc(held, 1)
                nc.gpsimd.indirect_dma_start(rows[:, :], None, dr.h2[:, :], bass.IndirectOffsetOnAxis(ap=idx[:, 0:1], axis=0),
                                             bounds_check=N - 1, oob_is_err=False).then_inc(gathered, 16)

            with any_chunk(pool):
                nc.gpsimd.iota(posi[:], pattern=[[1, 128]], base=0, channel_multiplier=0).then_inc(posed, 1)
                nc.gpsimd.iota(offi[:], pattern=[[-WN, NW]], base=0, channel_multiplier=0).then_inc(posed, 1)
                windows_with_extras(pool, c, 0, NW, chunk)

        @block.vector
        def _(dve):
            def chunk(i, w, k):
                ch = Chain(dve, chain, 4 * k + 4)
                dve.wait_ge(slots_in, 32 * k + 32)
                extra_slot_math(nc, ch, slots, rel, far, off[:, bass.ds(w, 1)], idx, idx_ready, w_, 1)
                nc.vector.memset(far[:], 0.0).then_inc(slots_free, 1)
                nc.vector.tensor_scalar(att[:], pos[:], rel[:, 0:1], w_[:, 0:1], ALU.is_equal, ALU.mult).then_inc(att_ready, 1)
                dve.wait_ge(summed, k + 1)
                dve.wait_ge(acc_in, 16 * k + 16)
                nc.vector.tensor_tensor(acc[:, 0:512], acc[:, 0:512], pa[0:WN, :], ALU.add)
                nc.vector.tensor_tensor(acc[:, 512:D], acc[:, 512:D], pb[0:WN, :], ALU.add).then_inc(added, 1)
                assert ch.n == 4, ch.n

            with any_chunk(dve):
                ch = Chain(dve, chain)
                ch.put(nc.vector.memset(rows[:], 0.0))
                dve.wait_ge(posed, 2)
                ch.put(nc.vector.tensor_copy(pos[:], posi[:]))
                ch.put(nc.vector.tensor_copy(off[:], offi[:]))
                ch.link(nc.vector.memset(far[:], 0.0))
                nc.vector.memset(rel[:], 0.0).then_inc(slots_free, 1)
                windows_with_extras(dve, c, 0, NW, chunk)

        @block.tensor
        def _(pe):
            def chunk(i, w, k):
                pe.wait_ge(att_ready, k + 1)
                pe.wait_ge(gathered, 16 * k + 16)
                pe.matmul(pa[:], att[:], rows[:, 0:512], start=True, stop=True)
                pe.matmul(pb[:], att[:], rows[:, 512:D], start=True, stop=True).then_inc(summed, 1)
                pe.wait_ge(added, k + 1)

            with any_chunk(pe):
                windows_with_extras(pe, c, 0, NW, chunk)


OT = 2 * WN
GT = 10
GW = 2 * GT
NG = N // (OT * GT)
RB = 4
LOOKS = 3
MB = 2 * LOOKS
PREP = 8
GELU_C = float(np.sqrt(2.0 / np.pi))
EMBEDS = (384, 576, D)
PARTS = (slice(0, EMBEDS[0]), slice(EMBEDS[0], EMBEDS[1]), slice(EMBEDS[1], EMBEDS[2]))
assert F <= 2 * EMBEDS[0]


def stage_output(nc, c, io, dr):
    with ExitStack() as ctx:
        m = Mem(nc, ctx, "out")
        wfc, wpr = m.sb("wfc", [F, D]), m.sb("wpr", [128, DC, F])
        w0, w1 = m.sb("w0", [128, DC, F]), m.sb("w1", [F + 1, D])
        b0, b2 = m.sb("b0", [F, 1]), m.sb("b2", [OT, D])
        bp = m.sb("bp", [1, D])
        ae, ar, pairs, coef = m.sb("ae", [128, 3]), m.sb("ar", [128, 3]), m.sb("pairs", [128, 3]), m.sb("coef", [128, 3])
        x = m.sb("x", [OT, GT, D])
        xn = m.sb("xn", [OT, 2, D])
        xt = m.sb("xt", [128, 2, DC, OT])
        rows = m.sb("rows", [128, RB, D])
        slots = m.sb("slots", [128, GW, REC])
        names = ("rel", "far", "own", "woff", "wself", "w", "rel_now", "w_now")
        rel, far, own, woff, wself, w, rel_now, w_now = (m.sb(n, [128, GW]) for n in names)
        idx, idx_now = m.sb("idx", [128, GW], I32), m.sb("idx_now", [128, GW], I32)
        is_edge, is_self, step_off, step_self, place = (m.sb(n, [128, 1]) for n in ("is_edge", "is_self", "step_off",
                                                                                   "step_self", "place"))
        posi = m.sb("posi", [128, 128], I32)
        pos, pos_own = m.sb("pos", [128, 128]), m.sb("pos_own", [128, 128])
        mask = m.sb("mask", [128, MB, 128])
        att = m.sb("att", [128, RB, 128])
        stats, mv = m.sb("stats", [OT, 2, 2, 6]), m.sb("mv", [OT, 2, 2])
        ve, rough, sq, rstd = (m.sb(n, [OT, 2]) for n in ("ve", "rough", "sq", "rstd"))
        power, spare = m.sb("power", [OT, 1]), m.sb("spare", [1, 1])
        u, u2, th = (m.sb(n, [F, 2, OT]) for n in ("u", "u2", "th"))
        g = m.sb("g", [F + 1, 2, OT])
        pa = [m.ps(f"pa{i}", [128, 512]) for i in range(2)]
        pa_tail = m.ps("pa_tail", [128, D - 512])
        pt = [m.ps(f"pt{i}", [128, 4, 128]) for i in range(2)]
        po = [m.ps(f"po{i}", [128, 512]) for i in range(2)]
        ph = m.ps("ph", [128, 512])
        look = ph[:, 0:2 * GW].rearrange("p (i k) -> p i k", k=2)
        hid = ph[0:F, 128:128 + OT]
        sems = ("par_in", "coef_ready", "turned_w", "w_ready", "init", "posed", "slots_in", "idx_ready", "mask_ready",
                "looked", "weights_ready", "att_ready", "agg_done", "x2_ready", "ve_ready", "pow_ready", "xn_ready",
                "turned", "xt_ready", "h_done", "u_ready", "t_ready", "th_ready", "g_ready", "o_done", "o_ready",
                "xb_ready", "tail_read", "chain", "setup", "gelu", "prep", "bias_in",
                "held", "paused")
        (par_in, coef_ready, turned_w, w_ready, init, posed, slots_in, idx_ready, mask_ready, looked, weights_ready,
         att_ready, agg_done, x2_ready, ve_ready, pow_ready, xn_ready, turned, xt_ready, h_done, u_ready, t_ready,
         th_ready, g_ready, o_done, o_ready, xb_ready, tail_read, chain, setup, gelu, prep, bias_in, held, paused) = (m.sem(n) for n in sems)
        gathered = [m.sem(f"gathered{b}") for b in range(RB)]
        x_in = [m.sem(f"x_in{j}") for j in range(GT)]
        x_out = [m.sem(f"x_out{j}") for j in range(GT)]
        block = ctx.enter_context(nc.Block())
        TILES = NG * GT
        FIRST, LAST = -2, TILES + 2

        def schedule(eng, iteration):
            for t in range(FIRST, GT):
                iteration(t // GT, t % GT)
            with eng.Fori(1, NG - 1) as grp:
                for j in range(GT):
                    iteration(grp, j)
            for t in range((NG - 1) * GT, LAST + 1):
                iteration(t // GT, t % GT)

        def tile_at(grp, j, ahead):
            at = j + ahead
            there, t = grp + at // GT, GT * grp + at
            return t, at % GT, there, (0 <= t < TILES if isinstance(t, int) else True)

        def beyond(t, n):
            return t >= n if isinstance(t, int) else True

        def next_group(grp):
            return 0 <= grp < NG - 1 if isinstance(grp, int) else True

        @block.sync
        def _(sp):
            row = lambda name: io[name].rearrange("(a d) -> a d", a=1)
            sp.dma_start(ae[:], row("alpha_e").broadcast_to([128, 3])).then_inc(par_in, 16)
            sp.dma_start(ar[:], row("alpha_r").broadcast_to([128, 3])).then_inc(par_in, 16)
            sp.dma_start(wfc[:], io["w_fc"]).then_inc(par_in, 16)
            sp.dma_start(wpr[:], io["w_proj"].rearrange("(k p) f -> p k f", p=128)).then_inc(par_in, 16)
            sp.dma_start(b0[:], io["b_fc"].rearrange("(p a) -> p a", a=1)).then_inc(par_in, 16)
            sp.dma_start(bp[:], row("b_proj")).then_inc(par_in, 16)
            sp.dma_start(b2[:], row("b2").broadcast_to([OT, D])).then_inc(par_in, 16)

            def load_slots(grp):
                for i in range(GW):
                    start = sp.value_load(c.table[0:1, bass.ds(GW * grp + i, 1)], min_val=0, max_val=E)
                    sp.dma_start(slots[0:WE, i, :], dr.rec2[bass.ds(start, WE), :]).then_inc(slots_in, 16)

            chunks = table_value(sp, c, CHUNKS + NW, MAX_CHUNKS)

            def load_rows(t, at, source, wait):
                if wait is not None:
                    sp.wait_ge(x_out[at], wait)
                    sp.sem_inc(paused, 1)
                for lo, hi in row_parts(OT):
                    sp.dma_start(x[lo:hi, at], source[bass.ds(OT * t + lo, hi - lo), :]).then_inc(x_in[at], 16)

            def load_x(t, at, wait=None):
                with sp.If(chunks > 0):
                    load_rows(t, at, dr.x_more, wait)
                with sp.Else():
                    load_rows(t, at, io["x"], wait)

            def iteration(grp, j):
                t, at, there, ok = tile_at(grp, j, 4)
                if ok:
                    load_x(t, at, 32 * there if beyond(t, GT) else None)
                if j == 0 and next_group(grp):
                    sp.wait_ge(weights_ready, grp + 1)
                    load_slots(grp + 1)
                t, at, there, ok = tile_at(grp, j, -3)
                if ok:
                    sp.wait_ge(o_ready, t + 1)
                    for lo, hi in row_parts(OT):
                        sp.dma_start(dr.out[bass.ds(OT * t + lo, hi - lo), :], x[lo:hi, at]).then_inc(x_out[at], 16)

            sp.wait_ge(init, 3)
            load_slots(0)
            for at in range(2):
                load_x(at, at)
            sp.wait_ge(w_ready, 2)
            sp.dma_start(w1[F:F + 1, :], bp[:]).then_inc(bias_in, 16)
            schedule(sp, iteration)
            for j in range(GT):
                sp.wait_ge(x_out[j], 32 * NG)

        @block.gpsimd
        def _(pool):
            def hold(sem, value):
                pool.wait_ge(sem, value)
                pool.sem_inc(held, 1)

            nc.gpsimd.iota(posi[:], pattern=[[1, 128]], base=0, channel_multiplier=0).then_inc(posed, 1)
            nc.gpsimd.iota(idx[:, 0:1], pattern=[[0, 1]], base=-WE, channel_multiplier=1).then_inc(posed, 1)
            nc.gpsimd.memset(power[:], -0.5).then_inc(posed, 1)
            pool.wait_ge(posed, 3)
            pool.wait_ge(par_in, 16 * 7)
            pool.wait_ge(init, 3)

            def iteration(grp, j):
                t, at, there, ok = tile_at(grp, j, 1)
                if ok:
                    pool.wait_ge(x_in[at], 32 * (there + 1))
                    nc.gpsimd.tensor_tensor(x[:, at], x[:, at], b2[:], ALU.add).then_inc(xb_ready, 1)
                t, at, there, ok = tile_at(grp, j, 2)
                if ok:
                    if at == 0:
                        hold(idx_ready, there + 1)
                    if beyond(t, 2):
                        hold(agg_done, t - 1)
                    for i in (2 * at, 2 * at + 1):
                        nc.gpsimd.indirect_dma_start(
                            rows[:, i % RB, :], None, dr.h2[:, :], bass.IndirectOffsetOnAxis(ap=idx_now[:, i:i + 1], axis=0),
                            bounds_check=N - 1, oob_is_err=False).then_inc(gathered[i % RB], 16)
                t, at, there, ok = tile_at(grp, j, 0)
                if ok:
                    pool.wait_ge(ve_ready, t + 1)
                    nc.gpsimd.tensor_tensor(rough[:, at % 2:at % 2 + 1], ve[:, at % 2:at % 2 + 1], power[:], ALU.pow)\
                        .then_inc(pow_ready, 1)

            schedule(pool, iteration)

        @block.vector
        def _(dve):
            ch = Chain(dve, setup)
            nc.vector.memset(rows[:], 0.0).then_inc(init, 1)
            ch.put(nc.vector.memset(att[:], 0.0))
            ch.put(nc.vector.memset(w1[:], 0.0))
            ch.put(nc.vector.memset(g[:], 1.0))
            dve.wait_ge(init, 1)
            dve.wait_ge(posed, 2)
            ch.put(nc.vector.tensor_copy(pos[:], posi[:]))
            ch.put(nc.vector.tensor_scalar(pos_own[:], posi[:], float(-WE), None, ALU.add))
            ch.put(nc.vector.memset(slots[:], 0.0))
            ch.link(nc.vector.tensor_copy(place[:], idx[:, 0:1]))
            ch.put(nc.vector.tensor_scalar(is_self[:], place[:], 0.0, None, ALU.is_ge))
            ch.link(nc.vector.tensor_scalar(is_edge[:], place[:], 0.0, None, ALU.is_lt))
            ch.put(nc.vector.tensor_scalar(step_off[:], is_edge[:], float(-WN * GW), None, ALU.mult))
            ch.put(nc.vector.tensor_scalar(step_self[:], is_self[:], float(WN * GW), None, ALU.mult))
            for i in range(GW):
                ch.put(nc.vector.tensor_scalar(woff[:, i:i + 1], is_edge[:], float(-WN * i), None, ALU.mult))
                ch.put(nc.vector.tensor_scalar(wself[:, i:i + 1], place[:], float(WN * i), is_self[:, 0:1], ALU.add, ALU.mult))
                ch.put(nc.vector.tensor_copy(slots[:, i, 0:1], is_self[:]))
                ch.put(nc.vector.tensor_scalar(slots[:, i, 9:10], place[:], 0.0, None, ALU.max))
            ch.wait()
            nc.vector.memset(mask[:], 0.0).then_inc(init, 1)
            nc.vector.memset(far[:], 0.0).then_inc(init, 1)

            dve.wait_ge(par_in, 16 * 7)
            ch.link(nc.vector.tensor_scalar(pairs[:], ae[:], ar[:, 0:1], None, ALU.mult))
            for n in (1, 2):
                ch.link(nc.vector.scalar_tensor_tensor(out=pairs[:], in0=ae[:], scalar=ar[:, n:n + 1], in1=pairs[:],
                                                       op0=ALU.mult, op1=ALU.add))
            ch.link(nc.vector.tensor_copy(coef[:, 2:3], pairs[:, 2:3]))
            for n in (1, 0):
                ch.link(nc.vector.tensor_tensor(coef[:, n:n + 1], pairs[:, n:n + 1], coef[:, n + 1:n + 2], ALU.add))
            for n, part in enumerate(PARTS):
                ch.put(nc.vector.tensor_scalar(wfc[:, part], wfc[:, part], coef[0:F, n:n + 1], None, ALU.mult))
                ch.put(nc.vector.tensor_scalar(bp[:, part], bp[:, part], coef[0:1, n:n + 1], None, ALU.mult))
            ch.put(nc.vector.tensor_scalar(b0[:], b0[:], coef[0:F, 0:1], None, ALU.mult))
            ch.wait()
            nc.vector.memset(th[:], 0.0).then_inc(w_ready, 1)
            nc.vector.memset(u2[:], 0.0).then_inc(w_ready, 1)
            dve.wait_ge(turned_w, 1)
            for k in range(2):
                ch.put(nc.vector.tensor_copy(w0[:, 3 * k:3 * k + 3], pt[k][:, 0:3, 0:F]))
            ch.put(nc.vector.tensor_copy(w1[0:F, 0:512], po[0][0:F, :]))
            ch.link(nc.vector.tensor_copy(w1[0:F, 512:D], po[1][0:F, 0:D - 512]))
            for n, part in enumerate(PARTS):
                ch.put(nc.vector.tensor_scalar(w1[0:F, part], w1[0:F, part], coef[0:F, n:n + 1], 0.5, ALU.mult, ALU.mult))
            ch.wait()
            nc.vector.memset(stats[:], 0.0).then_inc(w_ready, 1)

            def slot_math(grp):
                qc = Chain(dve, prep, PREP * grp)
                dve.wait_ge(slots_in, 16 * GW * (grp + 1))
                qc.put(nc.vector.tensor_tensor(rel[:], slots[:, :, 9], woff[:], ALU.add))
                qc.link(nc.vector.tensor_tensor(own[:], slots[:, :, 10], wself[:], ALU.add))
                qc.put(nc.vector.tensor_scalar(woff[:], woff[:], step_off[:, 0:1], None, ALU.add))
                qc.put(nc.vector.tensor_scalar(wself[:], wself[:], step_self[:, 0:1], None, ALU.add))
                qc.link(nc.vector.tensor_scalar(far[:], rel[:], float(WN), FAR, ALU.is_ge, ALU.mult))
                qc.link(nc.vector.tensor_tensor(idx[:], own[:], far[:], ALU.add))

            def window_mask(grp, i):
                if i >= MB:
                    dve.wait_ge(looked, GW * grp + i - MB + 1)
                elif not isinstance(grp, int) or grp:
                    dve.wait_ge(looked, GW * grp)
                nc.vector.tensor_scalar(mask[:, i % MB], pos_own[:], rel[:, i:i + 1], None, ALU.is_equal).then_inc(mask_ready, 1)

            def weights(grp):
                qc = Chain(dve, prep, PREP * grp + 6)
                dve.wait_ge(looked, GW * (grp + 1))
                qc.link(nc.vector.tensor_tensor(w[:], slots[:, :, 0], look[:, :, 1], ALU.subtract))
                if not isinstance(grp, int) or grp:
                    for b in range(RB):
                        dve.wait_ge(gathered[b], 16 * (GW // RB) * grp)
                nc.vector.tensor_tensor(w_now[:], w[:], look[:, :, 0], ALU.add).then_inc(weights_ready, 1)
                qc.link(nc.vector.tensor_copy(rel_now[:], rel[:]))
                dve.wait_ge(weights_ready, grp + 1)
                nc.vector.tensor_copy(idx_now[:], idx[:]).then_inc(idx_ready, 1)

            def spread(t, at):
                if beyond(t, 2):
                    dve.wait_ge(agg_done, t - 1)
                for i in (2 * at, 2 * at + 1):
                    half = slice(WN * (i % 2), WN * (i % 2) + WN)
                    nc.vector.tensor_scalar(att[:, i % RB, half], pos[:, 0:WN], rel_now[:, i:i + 1], w_now[:, i:i + 1],
                                            ALU.is_equal, ALU.mult).then_inc(att_ready, 1)

            def iteration(grp, j):
                t, at, _, ok = tile_at(grp, j, 0)
                b = at % 2
                col = slice(b, b + 1)
                lc = Chain(dve, chain, 7 * t)
                if ok:
                    dve.wait_ge(agg_done, t + 1)
                    dve.wait_ge(xb_ready, t + 1)
                    nc.vector.tensor_tensor(x[:, at, 512:D], x[:, at, 512:D], pa_tail[0:OT, :], ALU.add)\
                        .then_inc(tail_read, 1)
                    nc.vector.tensor_tensor(x[:, at, 0:512], x[:, at, 0:512], pa[b][0:OT, :], ALU.add)\
                        .then_inc(x2_ready, 1)
                    dve.wait_ge(x2_ready, t + 1)
                    for half in range(2):
                        lc.put(nc.vector.bn_stats(stats[:, b, half], x[:, at, half * (D // 2):(half + 1) * (D // 2)]))
                    lc.wait()
                    nc.vector.memset(spare[:], 0.0)
                    lc.link(nc.vector.bn_aggr(mv[:, b], stats[:, b].rearrange("p a b -> p (a b)")))
                    nc.vector.tensor_scalar(ve[:, col], mv[:, b, 1:2], EPS, None, ALU.add).then_inc(ve_ready, 1)
                if next_group(grp):
                    if j == 0:
                        slot_math(grp + 1)
                    if 1 <= j <= 7:
                        for i in range(LOOKS * (j - 1), min(LOOKS * j, GW)):
                            window_mask(grp + 1, i)
                    if j == 8:
                        weights(grp + 1)
                t2, at2, _, ok2 = tile_at(grp, j, 2)
                if ok2:
                    spread(t2, at2)
                tg, ag, _, okg = tile_at(grp, j, -2)
                gb = ag % 2
                if okg:
                    dve.wait_ge(u_ready, 2 * (tg + 1))
                    gc = Chain(dve, gelu, tg)
                    gc.link(nc.vector.tensor_scalar(u2[:, gb], u2[:, gb], 0.044715, 1.0, ALU.mult, ALU.add))
                    nc.vector.tensor_tensor(u2[:, gb], u2[:, gb], u[:, gb], ALU.mult).then_inc(t_ready, 1)
                tf, af, _, okf = tile_at(grp, j, -3)
                if okf:
                    dve.wait_ge(o_done, tf + 1)
                    nc.vector.tensor_tensor(x[:, af, 0:512], x[:, af, 0:512], po[0][0:OT, :], ALU.add)
                    nc.vector.tensor_tensor(x[:, af, 512:D], x[:, af, 512:D], po[1][0:OT, 0:D - 512], ALU.add)\
                        .then_inc(o_ready, 1)
                if okg:
                    dve.wait_ge(th_ready, tg + 1)
                    nc.vector.scalar_tensor_tensor(out=g[0:F, gb], in0=th[:, gb], scalar=1.0, in1=u[:, gb], op0=ALU.add,
                                                   op1=ALU.mult).then_inc(g_ready, 1)
                if ok:
                    dve.wait_ge(pow_ready, t + 1)
                    lc.link(nc.vector.tensor_tensor(sq[:, col], rough[:, col], rough[:, col], ALU.mult))
                    lc.link(nc.vector.tensor_tensor(sq[:, col], sq[:, col], ve[:, col], ALU.mult))
                    lc.link(nc.vector.tensor_scalar(sq[:, col], sq[:, col], -0.5, 1.5, ALU.mult, ALU.add))
                    lc.link(nc.vector.tensor_tensor(rstd[:, col], rough[:, col], sq[:, col], ALU.mult))
                    if beyond(t, 2):
                        dve.wait_ge(turned, t - 1)
                    nc.vector.tensor_scalar(xn[:, b], x[:, at], mv[:, b, 0:1], rstd[:, col], ALU.subtract, ALU.mult)\
                        .then_inc(xn_ready, 1)
                    assert lc.n == 7, lc.n

            slot_math(0)
            for i in range(GW):
                window_mask(0, i)
            weights(0)
            schedule(dve, iteration)

        @block.scalar
        def _(act):
            act.wait_ge(w_ready, 2)

            def iteration(grp, j):
                tg, ag, _, okg = tile_at(grp, j, -2)
                if okg:
                    act.wait_ge(t_ready, tg + 1)
                    nc.scalar.activation(th[:, ag % 2], u2[:, ag % 2], ACT.Tanh, scale=GELU_C).then_inc(th_ready, 1)
                t, at, _, ok = tile_at(grp, j, 0)
                if ok:
                    act.wait_ge(turned, t + 1)
                    if beyond(t, 2):
                        act.wait_ge(h_done, t - 1)
                    for k in range(2):
                        nc.scalar.activation(xt[:, at % 2, 3 * k:3 * k + 3], pt[k][:, 0:3, 0:OT], ACT.Copy)\
                            .then_inc(xt_ready, 1)
                th_, ah_, _, okh = tile_at(grp, j, -1)
                if okh:
                    act.wait_ge(h_done, th_ + 1)
                    if beyond(th_, 2):
                        act.wait_ge(g_ready, th_ - 1)
                    hb = ah_ % 2
                    nc.scalar.activation(u[:, hb], hid, ACT.Identity, bias=b0[:]).then_inc(u_ready, 1)
                    nc.scalar.activation(u2[:, hb], hid, ACT.Square, bias=b0[:]).then_inc(u_ready, 1)

            schedule(act, iteration)

        @block.tensor
        def _(pe):
            pe.wait_ge(w_ready, 2)
            for k in range(DC):
                pe.transpose(pt[k // 3][:, k % 3, 0:F], wfc[:, 128 * k:128 * k + 128], c.ident[0:F, 0:F])
            for k in range(DC):
                ins = pe.transpose(po[k // 4][0:F, 128 * (k % 4):128 * (k % 4) + 128], wpr[:, k], c.ident[:])
            ins.then_inc(turned_w, 1)

            def look_up(grp, i):
                pe.wait_ge(mask_ready, GW * grp + i + 1)
                pe.matmul(look[:, i], mask[:, i % MB], slots[:, i, 4:9:4], start=True, stop=True).then_inc(looked, 1)

            for i in range(GW):
                look_up(0, i)
            pe.wait_ge(w_ready, 3)
            pe.wait_ge(bias_in, 16)

            def iteration(grp, j):
                t, at, there, ok = tile_at(grp, j, 1)
                if ok:
                    pe.wait_ge(att_ready, 2 * (t + 1))
                    if beyond(t, 2):
                        pe.wait_ge(x2_ready, t - 1)
                    for i in (2 * at, 2 * at + 1):
                        pe.wait_ge(gathered[i % RB], 16 * (GW // RB) * there + 16 * (i // RB + 1))
                        go = dict(start=(i % 2 == 0), stop=(i % 2 == 1))
                        pe.matmul(pa[at % 2][:], att[:, i % RB], rows[:, i % RB, 0:512], **go)
                    if beyond(t, 1):
                        pe.wait_ge(tail_read, t)
                    for i in (2 * at, 2 * at + 1):
                        ins = pe.matmul(pa_tail[:], att[:, i % RB], rows[:, i % RB, 512:D], start=(i % 2 == 0),
                                        stop=(i % 2 == 1))
                    ins.then_inc(agg_done, 1)
                t, at, _, ok = tile_at(grp, j, 0)
                if ok:
                    pe.wait_ge(xn_ready, t + 1)
                    if beyond(t, 1):
                        pe.wait_ge(xt_ready, 2 * t)
                    for k in range(DC):
                        ins = pe.transpose(pt[k // 3][:, k % 3, 0:OT], xn[:, at % 2, 128 * k:128 * k + 128],
                                           c.ident[0:OT, 0:OT])
                    ins.then_inc(turned, 1)
                t, at, _, ok = tile_at(grp, j, -1)
                if ok:
                    pe.wait_ge(xt_ready, 2 * (t + 1))
                    if beyond(t, 1):
                        pe.wait_ge(u_ready, 2 * t)
                    for k in range(DC):
                        ins = pe.matmul(hid, w0[:, k], xt[:, at % 2, k], start=(k == 0), stop=(k == DC - 1))
                    ins.then_inc(h_done, 1)
                t, at, _, ok = tile_at(grp, j, -2)
                if ok:
                    pe.wait_ge(g_ready, t + 1)
                    if beyond(t, 1):
                        pe.wait_ge(o_ready, t)
                    pe.matmul(po[0][0:OT, :], g[:, at % 2], w1[:, 0:512], start=True, stop=True)
                    pe.matmul(po[1][0:OT, 0:D - 512], g[:, at % 2], w1[:, 512:D], start=True, stop=True).then_inc(o_done, 1)
                if next_group(grp) and 1 <= j <= 7:
                    pe.wait_ge(u_ready, 2 * (GT * grp + j))
                    for i in range(LOOKS * (j - 1), min(LOOKS * j, GW)):
                        look_up(grp + 1, i)

            schedule(pe, iteration)


class Names:
    pass


def build(nc, ins, out):
    io = {name.removeprefix("L0_gnn_").removeprefix("L0_ffn_"): ap for name, ap in ins.items()}
    dr, c = Names(), Names()
    dr.out = out
    dr.parts = nc.dram_tensor("parts", [N, 2 * D], F16).ap()
    dr.logit1, dr.logit2 = nc.dram_tensor("logit1", [N, 2 * HEADS], F32).ap(), nc.dram_tensor("logit2", [N, 2], F32).ap()
    dr.rec1, dr.rec2 = (nc.dram_tensor(f"rec{n}", [E + PAD, REC], F32).ap() for n in (1, 2))
    dr.h2, dr.x_more = nc.dram_tensor("h2", [N, D], F32).ap(), nc.dram_tensor("x_more", [N, D], F32).ap()
    with ExitStack() as ctx:
        persistent(nc, ctx, c)
        stage_constants(nc, c)
        stage_normalise(nc, c, io, dr)
        with ExitStack() as big:
            layer_weights(nc, big, c)
            stage_softmax(nc, c, io, dr.logit1, dr.rec1, HEADS, extra=Weights, tag="sm1")
            stage_layers(nc, c, io, dr)
        stage_softmax(nc, c, io, dr.logit2, dr.rec2, 1, tag="sm2")
        stage_extra_rows(nc, c, io, dr)
        stage_output(nc, c, io, dr)


def kernel(**inputs):
    import concourse.bacc as bacc
    from concourse.bass_utils import run_bass_kernel_spmd

    nc = bacc.Bacc("TRN2", target_bir_lowering=False, num_devices=1)
    arrays, ins = {}, {}
    for name, value in inputs.items():
        a = np.ascontiguousarray(value)
        arrays[f"in_{name}_dram"] = a
        ins[name] = nc.dram_tensor(f"in_{name}_dram", a.shape, mybir.dt.from_np(a.dtype), kind="ExternalInput").ap()
    out = nc.dram_tensor("out_0_dram", [N, D], F32, kind="ExternalOutput").ap()
    build(nc, ins, out)
    r = run_bass_kernel_spmd(nc, [arrays], core_ids=[0])
    return r.results[0]["out_0_dram"]
```

```python
from contextlib import ExitStack

import numpy as np
import concourse.bass as bass
from concourse import mybir

ALU = mybir.AluOpType
ACT = mybir.ActivationFunctionType
AX = mybir.AxisListType
F32 = mybir.dt.float32
F16 = mybir.dt.float16
I32 = mybir.dt.int32

N = 10000
E = 10000
D = 768
HEADS, HID = 4, 512
DH = HEADS * HID
F = 96
DC = D // 128
KC = DH // 128

EP, EC = 125, 80
SN = 500
NS = N // SN
TN = 125
NT = SN // TN
WN = 50
NW = N // WN
WPS = SN // WN
WE = 128 - WN
XE = 64
REC = 12
MAX_CHUNKS = E // XE + 1
PAD = 128
CHUNKS = NW + 1
TABLE = 2 * (NW + 1)
FAR = 1.0e6
LOW = -1.0e30
SX = 2.0 ** 11
SA = 2.0 ** 14
W2C = D + 4
EPS = 1e-5


class Chain:

    def __init__(self, eng, sem, base=0):
        self.eng, self.sem, self.base, self.n = eng, sem, base, 0

    def put(self, ins):
        self.n += 1
        return ins.then_inc(self.sem, 1)

    def wait(self):
        self.eng.wait_ge(self.sem, self.base + self.n)

    def link(self, ins):
        self.put(ins)
        self.wait()


class Mem:

    def __init__(self, nc, ctx, tag):
        self.nc, self.ctx, self.tag, self.sems = nc, ctx, tag, []
        ctx.callback(self.free_semaphores)

    def free_semaphores(self):
        self.nc.clear_and_free_semaphores(self.sems)
        self.nc.all_engine_barrier()

    def sb(self, name, shape, dt=F32):
        return self.ctx.enter_context(self.nc.sbuf_tensor(f"{self.tag}_{name}", shape, dt))

    def ps(self, name, shape, dt=F32):
        return self.ctx.enter_context(self.nc.psum_tensor(f"{self.tag}_{name}", shape, dt))

    def sem(self, name):
        self.sems.append(self.nc.alloc_semaphore(f"{self.tag}_{name}"))
        return self.sems[-1]


def row_parts(rows):
    cut = rows // 16 * 16
    return [(0, cut), (cut, rows)] if rows % 16 else [(0, rows)]


def persistent(nc, ctx, c):
    c.ident = ctx.enter_context(nc.sbuf_tensor("ident", [128, 128], F32))
    c.ones = ctx.enter_context(nc.sbuf_tensor("ones", [128, 128], F32))
    c.table = ctx.enter_context(nc.sbuf_tensor("table", [1, TABLE], I32))


def layer_weights(nc, ctx, c):
    c.b1 = ctx.enter_context(nc.sbuf_tensor("b1c", [128, KC], F32))
    c.b1s = ctx.enter_context(nc.sbuf_tensor("b1s", [128, KC], F32))
    c.scale = ctx.enter_context(nc.sbuf_tensor("scale", [128, 16], F32))
    c.w1h, c.w1l = (ctx.enter_context(nc.sbuf_tensor(n, [128, DC, DH], F16)) for n in ("w1h", "w1l"))
    c.w2h, c.w2l = (ctx.enter_context(nc.sbuf_tensor(n, [128, KC, W2C], F16)) for n in ("w2h", "w2l"))


def stage_constants(nc, c):
    with ExitStack() as ctx:
        m = Mem(nc, ctx, "cst")
        zeroed, done = m.sem("zeroed"), m.sem("done")
        block = ctx.enter_context(nc.Block())

        @block.gpsimd
        def _(pool):
            nc.gpsimd.memset(c.ident[:], 0.0).then_inc(zeroed, 1)
            nc.gpsimd.memset(c.ones[:], 1.0).then_inc(done, 1)
            pool.wait_ge(zeroed, 1)
            nc.gpsimd.affine_select(out=c.ident[:], in_=c.ident[:], compare_op=ALU.not_equal, fill=1.0, base=0,
                                    pattern=[[-1, 128]], channel_multiplier=1).then_inc(done, 1)
            pool.wait_ge(done, 2)


NB = 4
NJ = NS // NB
POOL_LOWS = (1, 3)


def stage_normalise(nc, c, io, dr):
    with ExitStack() as ctx:
        m = Mem(nc, ctx, "nrm")
        w1 = m.sb("w1", [128, DC, DH])
        asrc, adst = m.sb("asrc", [128, DH]), m.sb("adst", [128, DH])
        junk = m.sb("junk", [128, 2, HID])
        v1 = m.sb("v1", [128, DC, 2 * HEADS])
        xb = m.sb("xb", [TN, NB, NT, D])
        parts = m.sb("parts", [TN, NB, NT, 2, D], F16)
        stats = m.sb("stats", [TN, NT, 2, 6])
        mv = m.sb("mv", [TN, NB, NT, 2])
        ve, rough, rstd = (m.sb(n, [TN, NB, NT]) for n in ("ve", "rough", "rstd"))
        sq, spare, power = m.sb("sq", [TN, NT]), m.sb("spare", [1, 1]), m.sb("power", [TN, NT])
        xt = m.sb("xt", [128, 2, DC, 128])
        logit = m.sb("logit", [TN, NB, NT, 2 * HEADS])
        pt = [m.ps(f"pt{i}", [128, 2, 512]) for i in range(2)]
        pl = [m.ps(f"pl{i}", [2 * HEADS, NT, 128]) for i in range(2)]
        pb = [m.ps(f"pb{i}", [TN, NT, 2 * HEADS]) for i in range(2)]
        turned_logits = m.sb("turned_logits", [2 * HEADS, 2, NT, 128])
        weights, v_chain, init, held = m.sem("weights"), m.sem("v_chain"), m.sem("init"), m.sem("held")
        xin, stored, logits_out = ([m.sem(f"{n}{b}") for b in range(NB)] for n in ("xin", "stored", "logits_out"))
        held_pe, w1_in = m.sem("held_pe"), [m.sem(f"w1_in{k}") for k in range(DC)]
        chain, var_ready, pow_ready = m.sem("chain"), m.sem("var_ready"), m.sem("pow_ready")
        xs_ready, hi_ready, lo_ready, pool_lo_ready = (m.sem(n) for n in ("xs_ready", "hi_ready", "lo_ready", "pool_lo_ready"))
        turned, xt_ready, logits_done, row_ready, turned_back, logit_ready = (m.sem(n) for n in (
            "turned", "xt_ready", "logits_done", "row_ready", "turned_back", "logit_ready"))
        block = ctx.enter_context(nc.Block())
        x_rows = io["x"].rearrange("(s p t) d -> s p t d", p=TN, t=NT)
        t_rows = dr.parts.rearrange("(s p t) d -> s p (t d)", p=TN, t=NT)
        l_rows = dr.logit1.rearrange("(s p t) d -> s p (t d)", p=TN, t=NT)
        VECTOR_LOWS = [t for t in range(NT) if t not in POOL_LOWS]

        def rounds(eng, step):
            for b in range(NB):
                step(b, b, 0)
            with eng.Fori(1, NJ - 1) as j:
                for b in range(NB):
                    step(NB * j + b, b, j)
            for b in range(NB):
                step(NB * (NJ - 1) + b, b, NJ - 1)

        def within(s, lo=0, hi=NS):
            return lo <= s < hi if isinstance(s, int) else True

        @block.sync
        def _(sp):
            def hold(sem, value):
                sp.wait_ge(sem, value)
                sp.sem_inc(held, 1)

            def load(s, b):
                for lo, hi in row_parts(TN):
                    sp.dma_start(xb[lo:hi, b], x_rows[s, lo:hi]).then_inc(xin[b], 16)

            def store_logits(s, b):
                hold(logit_ready, s + 1)
                for lo, hi in row_parts(TN):
                    sp.dma_start(l_rows[s, lo:hi], logit[lo:hi, b].rearrange("p t k -> p (t k)")).then_inc(logits_out[b], 16)

            def step(s, b, j):
                hold(hi_ready, NT * s + NT)
                hold(lo_ready, len(VECTOR_LOWS) * (s + 1))
                hold(pool_lo_ready, len(POOL_LOWS) * (s + 1))
                for lo, hi in row_parts(TN):
                    sp.dma_start(t_rows[s, lo:hi], parts[lo:hi, b].rearrange("p t k d -> p (t k d)")).then_inc(stored[b], 16)
                if within(s + NB):
                    hold(turned, NT * s + NT)
                    load(s + NB, b)
                if within(s - 2):
                    store_logits(s - 2, (b - 2) % NB)

            load(0, 0)
            for tile, src in ((asrc, "a1_src"), (adst, "a1_dst")):
                sp.dma_start(tile[:], io[src].rearrange("(a h) d -> a (h d)", a=1).broadcast_to([128, DH])).then_inc(weights, 16)
            for k in range(DC):
                sp.dma_start(w1[:, k], io["W1"][128 * k:128 * k + 128, :]).then_inc(w1_in[k], 16)
            for b in range(1, NB):
                load(b, b)
            rounds(sp, step)
            store_logits(NS - 2, NB - 2)
            store_logits(NS - 1, NB - 1)
            for b in range(NB):
                sp.wait_ge(stored[b], 32 * NJ)
                sp.wait_ge(logits_out[b], 32 * NJ)

        @block.gpsimd
        def _(pool):
            nc.gpsimd.memset(power[:], -0.5).then_inc(init, 1)
            pool.wait_ge(init, 2)

            def rough_rstd(u, b):
                pool.wait_ge(var_ready, u + 1)
                nc.gpsimd.tensor_tensor(rough[:, b], ve[:, b], power[:], ALU.pow).then_inc(pow_ready, 1)

            def step(s, b, j):
                for t in POOL_LOWS:
                    pool.wait_ge(hi_ready, NT * s + t + 1)
                    nc.gpsimd.tensor_tensor(parts[:, b, t, 1], xb[:, b, t], parts[:, b, t, 0], ALU.subtract)\
                        .then_inc(pool_lo_ready, 1)
                if within(s + 1):
                    rough_rstd(s + 1, (b + 1) % NB)

            rough_rstd(0, 0)
            rounds(pool, step)

        @block.vector
        def _(dve):
            PER = 2 * NT + NT + 4

            def statistics(u, b, j):
                q = Chain(dve, chain, PER * u)
                dve.wait_ge(xin[b], 32 * (j + 1))
                for t in range(NT):
                    for half in range(2):
                        q.put(nc.vector.bn_stats(stats[:, t, half], xb[:, b, t, half * (D // 2):(half + 1) * (D // 2)]))
                q.wait()
                nc.vector.memset(spare[:], 0.0)
                for t in range(NT):
                    q.put(nc.vector.bn_aggr(mv[:, b, t], stats[:, t].rearrange("p a b -> p (a b)")))
                q.wait()
                nc.vector.tensor_scalar(ve[:, b], mv[:, b, :, 1], EPS, None, ALU.add).then_inc(var_ready, 1)

            def refine(u, b):
                q = Chain(dve, chain, PER * u + 3 * NT)
                dve.wait_ge(pow_ready, u + 1)
                q.link(nc.vector.tensor_tensor(sq[:], rough[:, b], rough[:, b], ALU.mult))
                q.link(nc.vector.tensor_tensor(sq[:], sq[:], ve[:, b], ALU.mult))
                q.link(nc.vector.tensor_scalar(sq[:], sq[:], -0.5 * SX, 1.5 * SX, ALU.mult, ALU.add))
                q.link(nc.vector.tensor_tensor(rstd[:, b], rough[:, b], sq[:], ALU.mult))

            def copy_logits(s, b, j):
                dve.wait_ge(turned_back, s + 1)
                if within(s, NB):
                    dve.wait_ge(logits_out[b], 32 * j)
                nc.vector.tensor_copy(logit[:, b], pb[b % 2][:]).then_inc(logit_ready, 1)

            def copy_rows(s, b):
                dve.wait_ge(logits_done, NT * s + NT)
                if within(s, 2):
                    dve.wait_ge(turned_back, s - 1)
                nc.vector.tensor_scalar(turned_logits[:, b % 2, :, 0:TN], pl[b % 2][:, :, 0:TN], 1.0 / SX, None, ALU.mult)\
                    .then_inc(row_ready, 1)

            def step(s, b, j):
                for t in range(NT):
                    nc.vector.tensor_scalar(xb[:, b, t], xb[:, b, t], mv[:, b, t, 0:1], rstd[:, b, t:t + 1], ALU.subtract,
                                            ALU.mult).then_inc(xs_ready, 1)
                if within(s + 1):
                    statistics(s + 1, (b + 1) % NB, j + (b + 1) // NB)
                for t in VECTOR_LOWS:
                    dve.wait_ge(hi_ready, NT * s + t + 1)
                    nc.vector.tensor_tensor(parts[:, b, t, 1], xb[:, b, t], parts[:, b, t, 0], ALU.subtract).then_inc(lo_ready, 1)
                if within(s - 1):
                    copy_rows(s - 1, (b - 1) % NB)
                if within(s + 1):
                    refine(s + 1, (b + 1) % NB)
                if within(s - 2):
                    copy_logits(s - 2, (b - 2) % NB, j - (b < 2))

            nc.vector.memset(xt[:], 0.0).then_inc(init, 1)
            statistics(0, 0, 0)
            refine(0, 0)
            ch = Chain(dve, v_chain)
            dve.wait_ge(weights, 32)
            for k in range(DC):
                dve.wait_ge(w1_in[k], 16)
                for side, a in ((0, asrc), (1, adst)):
                    for h in range(HEADS):
                        cols = slice(h * HID, h * HID + HID)
                        at = side * HEADS + h
                        if ch.n >= 2:
                            dve.wait_ge(v_chain, ch.n - 1)
                        ch.put(nc.vector.tensor_tensor_reduce(
                            out=junk[:, ch.n % 2], in0=w1[:, k, cols], in1=a[:, cols], scale=1.0, scalar=0.0,
                            op0=ALU.mult, op1=ALU.add, accum_out=v1[:, k, at:at + 1]))
            rounds(dve, step)
            copy_rows(NS - 1, NB - 1)
            copy_logits(NS - 2, NB - 2, NJ - 1)
            copy_logits(NS - 1, NB - 1, NJ - 1)

        @block.scalar
        def _(act):
            def step(s, b, j):
                for t in range(NT):
                    act.wait_ge(xs_ready, NT * s + t + 1)
                    if t == 0 and within(s, NB):
                        act.wait_ge(stored[b], 32 * j)
                    nc.scalar.activation(parts[:, b, t, 0], xb[:, b, t], ACT.Copy).then_inc(hi_ready, 1)
                    if t:
                        copy_turned(s, t - 1)
                    elif within(s, 1):
                        copy_turned(s - 1, NT - 1)

            def copy_turned(s, t):
                act.wait_ge(turned, NT * s + t + 1)
                if within(s, 1) or t >= 2:
                    act.wait_ge(logits_done, NT * s + t - 1)
                nc.scalar.activation(xt[:, t % 2, :, 0:TN].rearrange("p (g c) n -> p g c n", g=2),
                                     pt[t % 2][:, :, 0:3 * 128].rearrange("p g (c n) -> p g c n", n=128)[:, :, :, 0:TN],
                                     ACT.Copy).then_inc(xt_ready, 1)

            act.wait_ge(init, 2)
            rounds(act, step)
            copy_turned(NS - 1, NT - 1)

        @block.tensor
        def _(pe):
            def turn(s, b, t):
                pe.wait_ge(xs_ready, NT * s + t + 1)
                if within(s, 1) or t >= 2:
                    pe.wait_ge(xt_ready, NT * s + t - 1)
                for k in range(DC):
                    o = pt[t % 2][:, k // 3, 128 * (k % 3):128 * (k % 3) + TN]
                    ins = pe.transpose(o, xb[:, b, t, 128 * k:128 * k + 128], c.ident[0:TN, 0:TN])
                ins.then_inc(turned, 1)

            def logits(s, b, t):
                pe.wait_ge(xt_ready, NT * s + t + 1)
                if t == 0 and within(s, 2):
                    pe.wait_ge(row_ready, s - 1)
                for k in range(DC):
                    ins = pe.matmul(pl[b % 2][:, t, 0:TN], v1[:, k], xt[:, t % 2, k, 0:TN], start=(k == 0), stop=(k == DC - 1))
                ins.then_inc(logits_done, 1)

            def turn_back(s, b):
                pe.wait_ge(row_ready, s + 1)
                if within(s, 2):
                    pe.wait_ge(logit_ready, s - 1)
                pe.sem_inc(held_pe, 1)
                for t in range(NT):
                    ins = pe.transpose(pb[b % 2][:, t], turned_logits[:, b % 2, t, 0:TN], c.ident[0:2 * HEADS, 0:2 * HEADS])
                ins.then_inc(turned_back, 1)

            def step(s, b, j):
                for t in range(NT):
                    turn(s, b, t)
                    if t >= 2:
                        logits(s, b, t - 2)
                    elif within(s, 1):
                        logits(s - 1, (b - 1) % NB, NT - 2 + t)
                    if t == 2 and within(s, 2):
                        turn_back(s - 2, (b - 2) % NB)

            pe.wait_ge(v_chain, 2 * HEADS * DC)
            rounds(pe, step)
            logits(NS - 1, NB - 1, NT - 2)
            logits(NS - 1, NB - 1, NT - 1)
            turn_back(NS - 2, NB - 2)
            turn_back(NS - 1, NB - 1)


class Weights:

    PIECES = 4

    def __init__(self, nc, c, io, m, dst, loaded):
        self.nc, self.c, self.io, self.dst, self.loaded = nc, c, io, dst, loaded
        self.raw = m.sb("wraw", [128, KC * W2C])
        self.w1 = self.raw[:, 0:DC * DH].rearrange("p (k n) -> p k n", k=DC)
        self.w2 = self.raw[:].rearrange("p (k n) -> p k n", k=KC)
        self.a2 = m.sb("a2", [128, 2, D])
        self.junk = m.sb("junk", [128, 2, D])
        self.top = m.sb("top", [128, 4])
        self.top_t, self.diag = m.sb("top_t", [4, 1]), m.sb("diag", [4, 4])
        self.expo, self.inv = m.sb("expo", [128, 4], I32), m.sb("inv", [128, 4], I32)
        self.edges, self.before = m.sb("edges", [EP, NW // 8, EC]), m.sb("before", [EP, NW])
        self.dstf, self.thr, self.thri = m.sb("dstf", [EP, EC]), m.sb("thr", [EP, NW]), m.sb("thri", [EP, NW], I32)
        self.row, self.count = m.sb("row", [1, NW + 1]), m.sb("count", [1, NW])
        self.counti, self.zero = m.sb("counti", [1, NW], I32), m.sb("zero", [1, NW])
        self.pm, self.pb = m.ps("pm", [4, 128]), m.ps("pb", [128, 4])
        self.pw = m.ps("pw", [1, NW])
        self.b_in, self.w1_in, self.w2_in, self.a_in = (m.sem(n) for n in ("b_in", "w1_in", "w2_in", "a_in"))
        self.steps, self.thr_ready, self.before_ready, self.summed = (m.sem(n) for n in ("steps", "thr_ready",
                                                                                      "before_ready", "summed"))
        self.top_ready, self.top_turned, self.diag_ready, self.spread = (m.sem(n) for n in (
            "top_ready", "top_turned", "diag_ready", "spread"))
        self.scale_ready, self.hi, self.lo = m.sem("scale_ready"), m.sem("hi"), m.sem("lo")

    def sync(self, sp):
        sp.dma_start(self.c.b1[:], self.io["b1"].rearrange("(k p) -> p k", p=128),
                     allow_slow_non_contiguous=True).then_inc(self.b_in, 16)
        for k in range(DC):
            sp.dma_start(self.w1[:, k], self.io["W1"][128 * k:128 * k + 128, :]).then_inc(self.w1_in, 16)
        for n, name in enumerate(("a2_src", "a2_dst")):
            sp.dma_start(self.a2[:, n], self.io[name].broadcast_to([128, D])).then_inc(self.a_in, 16)
        sp.wait_ge(self.lo, self.PIECES)
        for k in range(KC):
            sp.dma_start(self.w2[:, k, 0:D], self.io["W2"][128 * k:128 * k + 128, :]).then_inc(self.w2_in, 16)

    def gpsimd(self, pool):
        self.nc.gpsimd.iota(self.thri[:], pattern=[[WN, NW]], base=0, channel_multiplier=0).then_inc(self.thr_ready, 1)

    def parts(self, which):
        c = self.c
        flat = lambda t: t[:].rearrange("p k n -> p (k n)")
        n = DC * DH if which == 0 else KC * W2C
        step = n // self.PIECES
        hi, lo = (flat(c.w1h), flat(c.w1l)) if which == 0 else (flat(c.w2h), flat(c.w2l))
        for i in range(self.PIECES):
            at = slice(i * step, i * step + step)
            yield i, hi[:, at], lo[:, at], self.raw[:, at]

    def scalar(self, act):
        for which in range(2):
            act.wait_ge(self.scale_ready, which + 1)
            for _, hi, _, raw in self.parts(which):
                self.nc.scalar.activation(hi, raw, ACT.Copy, scale=self.c.scale[:, which:which + 1]).then_inc(self.hi, 1)

    def tensor(self, pe):
        c = self.c
        pe.wait_ge(self.before_ready, 1)
        pe.matmul(self.pw[:], c.ones[0:EP, 0:1], self.before[:], start=True, stop=True).then_inc(self.summed, 1)
        for n in range(2):
            pe.wait_ge(self.top_ready, n + 1)
            pe.transpose(self.pm[:], self.top[:], c.ident[:]).then_inc(self.top_turned, 1)
            pe.wait_ge(self.diag_ready, n + 1)
            pe.matmul(self.pb[:], c.ones[0:4, :], self.diag[:], start=True, stop=True).then_inc(self.spread, 1)

    def vector(self, dve):
        nc, c = self.nc, self.c
        ch = Chain(dve, self.steps)
        dve.wait_ge(self.thr_ready, 1)
        ch.put(nc.vector.tensor_copy(self.thr[:], self.thri[:]))
        ch.link(nc.vector.tensor_copy(self.dstf[:], self.dst[:]))
        part = NW // 8
        for i in range(8):
            ch.link(nc.vector.tensor_tensor(
                self.edges[:], self.dstf[:].rearrange("p (a c) -> p a c", a=1).broadcast_to([EP, part, EC]),
                self.thr[:, i * part:i * part + part].rearrange("p (w a) -> p w a", a=1).broadcast_to([EP, part, EC]),
                ALU.is_lt))
            ch.link(nc.vector.tensor_reduce(self.before[:, i * part:i * part + part], self.edges[:], AX.X, ALU.add))
        nc.vector.memset(self.row[:, NW:NW + 1], float(E)).then_inc(self.before_ready, 1)
        dve.wait_ge(self.summed, 1)
        ch.link(nc.vector.tensor_copy(self.row[:, 0:NW], self.pw[:]))
        ch.put(nc.vector.tensor_copy(c.table[:, 0:NW + 1], self.row[:]))
        ch.link(nc.vector.tensor_tensor(self.count[:], self.row[:, 1:NW + 1], self.row[:, 0:NW], ALU.subtract))
        ch.link(nc.vector.tensor_scalar(self.count[:], self.count[:], float(-WE), 0.0, ALU.add, ALU.max))
        ch.link(nc.vector.tensor_scalar(self.counti[:], self.count[:], float(XE - 1), None, ALU.add))
        ch.link(nc.vector.tensor_scalar(self.counti[:], self.counti[:], 6, None, ALU.arith_shift_right))
        ch.put(nc.vector.tensor_copy(self.count[:], self.counti[:]))
        ch.put(nc.vector.memset(self.zero[:], 0.0))
        ch.link(nc.vector.memset(self.row[:, 0:1], 0.0))
        ch.link(nc.vector.tensor_tensor_scan(out=self.row[:, 1:NW + 1], data0=self.zero[:], data1=self.count[:], initial=0.0,
                                             op0=ALU.add, op1=ALU.add))
        ch.put(nc.vector.tensor_copy(c.table[:, CHUNKS:TABLE], self.row[:]))

        def scales(n):
            nc.vector.memset(self.diag[:], 0.0).then_inc(self.top_ready, 1)
            dve.wait_ge(self.top_turned, n + 1)
            ch.link(nc.vector.tensor_reduce(self.top_t[:], self.pm[:], AX.X, ALU.max))
            nc.vector.tensor_scalar(self.diag[:], c.ident[0:4, 0:4], self.top_t[:], None, ALU.mult)\
                .then_inc(self.diag_ready, 1)
            dve.wait_ge(self.spread, n + 1)
            ch.link(nc.vector.tensor_copy(self.top[:], self.pb[:]))
            ch.link(nc.vector.tensor_scalar(self.top[:, 2:3], self.top[:, 0:1], float(D), self.top[:, 3:4], ALU.mult, ALU.add))
            ch.link(nc.vector.tensor_scalar(self.top[:, 2:3], self.top[:, 2:3], 1.0, 0.5, ALU.max, ALU.mult))
            ch.link(nc.vector.tensor_scalar(self.expo[:], self.top[:].bitcast(I32), 23, None, ALU.logical_shift_right))
            ch.link(nc.vector.tensor_scalar(self.expo[:], self.expo[:], -1.0, 267.0, ALU.mult, ALU.add))
            ch.link(nc.vector.tensor_scalar(self.expo[:], self.expo[:], 253.0, 1.0, ALU.min, ALU.max))
            ch.link(nc.vector.tensor_scalar(self.inv[:], self.expo[:], -1.0, 254.0, ALU.mult, ALU.add))
            ch.put(nc.vector.tensor_scalar(c.scale[:, 0:4].bitcast(I32), self.expo[:], 23, None, ALU.logical_shift_left))
            ch.link(nc.vector.tensor_scalar(c.scale[:, 4:8].bitcast(I32), self.inv[:], 23, None, ALU.logical_shift_left))
            nc.vector.memset(self.diag[:], 0.0).then_inc(self.scale_ready, 1)

        ch.link(nc.vector.memset(self.top[:], 0.0))
        dve.wait_ge(self.b_in, 16)
        ch.put(nc.vector.tensor_reduce(self.top[:, 3:4], c.b1[:], AX.X, ALU.max, apply_absolute_value=True))
        dve.wait_ge(self.w1_in, 16 * DC)
        ch.link(nc.vector.tensor_reduce(self.top[:, 0:1], self.raw[:, 0:DC * DH], AX.X, ALU.max, apply_absolute_value=True))
        scales(0)
        for i, hi, lo, raw in self.parts(0):
            dve.wait_ge(self.hi, i + 1)
            nc.vector.scalar_tensor_tensor(out=lo, in0=raw, scalar=c.scale[:, 0:1], in1=hi, op0=ALU.mult,
                                           op1=ALU.subtract).then_inc(self.lo, 1)
        dve.wait_ge(self.lo, self.PIECES)
        ch.put(nc.vector.memset(self.w2[:, :, D + 2:W2C], 0.0))
        dve.wait_ge(self.a_in, 32)
        dve.wait_ge(self.w2_in, 16 * KC)
        for k in range(KC):
            for n in range(2):
                ch.put(nc.vector.tensor_tensor_reduce(
                    out=self.junk[:, n], in0=self.w2[:, k, 0:D], in1=self.a2[:, n], scale=1.0, scalar=0.0,
                    op0=ALU.mult, op1=ALU.add, accum_out=self.w2[:, k, D + n:D + n + 1]))
            ch.wait()
        ch.link(nc.vector.tensor_reduce(self.top[:, 1:2], self.raw[:], AX.X, ALU.max, apply_absolute_value=True))
        scales(1)
        for i, hi, lo, raw in self.parts(1):
            dve.wait_ge(self.hi, self.PIECES + i + 1)
            nc.vector.scalar_tensor_tensor(out=lo, in0=raw, scalar=c.scale[:, 1:2], in1=hi, op0=ALU.mult,
                                           op1=ALU.subtract).then_inc(self.lo, 1)
        ch.put(nc.vector.tensor_scalar(c.scale[:, 8:9], c.scale[:, 4:5], 1.0 / SX, None, ALU.mult))
        ch.put(nc.vector.tensor_scalar(c.scale[:, 9:10], c.scale[:, 4:5], 1.0 / SX, c.scale[:, 2:3], ALU.mult, ALU.mult))
        ch.put(nc.vector.tensor_scalar(c.scale[:, 10:11], c.scale[:, 2:3], -1.0, None, ALU.mult))
        ch.put(nc.vector.tensor_tensor(c.scale[:, 11:12], c.scale[:, 5:6], c.scale[:, 6:7], ALU.mult))
        ch.link(nc.vector.tensor_scalar(c.b1s[:], c.b1[:], c.scale[:, 2:3], None, ALU.mult))


def stage_softmax(nc, c, io, table, rec, heads, extra=None, tag="sm"):
    H = heads
    with ExitStack() as ctx:
        m = Mem(nc, ctx, tag)
        src, dst = m.sb("src", [EP, EC], I32), m.sb("dst", [EP, EC], I32)
        prev, nxt = m.sb("prev", [EP, EC], I32), m.sb("nxt", [EP, EC], I32)
        gsrc, gdst = m.sb("gsrc", [EP, EC, 2 * H]), m.sb("gdst", [EP, EC, 2 * H])
        record = m.sb("record", [EP, EC, REC])
        pads = m.sb("pads", [PAD, REC])
        first, cont, pen_f, pen_l = (m.sb(n, [EP, EC]) for n in ("first", "cont", "pen_f", "pen_l"))
        raw, l, ls = (m.sb(n, [EP, H, EC]) for n in ("raw", "l", "ls"))
        a, b, ex, exs = (m.sb(n, [EP, H, EC]) for n in ("a", "b", "ex", "exs"))
        edge = m.sb("edge", [EP, 2, H])
        edge_t = m.sb("edge_t", [H, 2, EP])
        carry_t = m.sb("carry_t", [H, EP + 2])
        carry = m.sb("carry", [EP, H])
        zeros_t, low_t = m.sb("zeros_t", [H, EP + 2]), m.sb("low_t", [H, EP + 2])
        pe_t = m.ps("pe_t", [128, 2, 128])
        pe_b = m.ps("pe_b", [128, 128])
        loaded, init = m.sem("loaded"), m.sem("init")
        got_src, got_dst = m.sem("got_src"), m.sem("got_dst")
        chain, edge_ready, turned, carry_ready, back = (m.sem(n) for n in ("chain", "edge_ready", "turned",
                                                                         "carry_ready", "back"))
        shifted, exps, record_ready, stored = (m.sem(n) for n in ("shifted", "exps", "record_ready", "stored"))
        more = extra(nc, c, io, m, dst, loaded) if extra else None
        block = ctx.enter_context(nc.Block())
        dst_line = io["dst"]

        @block.sync
        def _(sp):
            grid = lambda ap: ap.rearrange("(p c) -> p c", c=EC)
            sp.dma_start(src[:], grid(io["src"])).then_inc(loaded, 16)
            sp.dma_start(dst[:], grid(io["dst"])).then_inc(loaded, 16)
            sp.wait_ge(init, 2)
            sp.dma_start(prev[0:1, 1:EC], dst_line[0:EC - 1].rearrange("(a c) -> a c", a=1)).then_inc(loaded, 16)
            sp.dma_start(prev[1:EP, :], grid(dst_line[EC - 1:E - 1])).then_inc(loaded, 16)
            sp.dma_start(nxt[0:EP - 1, :], grid(dst_line[1:E - EC + 1])).then_inc(loaded, 16)
            sp.dma_start(nxt[EP - 1:EP, 0:EC - 1], dst_line[E - EC + 1:E].rearrange("(a c) -> a c", a=1)).then_inc(loaded, 16)
            if more:
                more.sync(sp)
            sp.wait_ge(init, 5)
            sp.dma_start(rec[E:E + PAD, :], pads[:]).then_inc(stored, 16)
            sp.wait_ge(record_ready, 1)
            rows = rec[0:E, :].rearrange("(p c) w -> p (c w)", c=EC)
            for lo, hi in row_parts(EP):
                sp.dma_start(rows[lo:hi], record[lo:hi].rearrange("p c w -> p (c w)")).then_inc(stored, 16)
            sp.wait_ge(stored, 48)

        @block.gpsimd
        def _(pool):
            if more:
                more.gpsimd(pool)
            pool.wait_ge(loaded, 96)
            for idx, out, sem in ((src, gsrc, got_src), (dst, gdst, got_dst)):
                for k in range(EC):
                    nc.gpsimd.indirect_dma_start(out[:, k, :], None, table[:, :], bass.IndirectOffsetOnAxis(
                        ap=idx[:, k:k + 1], axis=0), bounds_check=N - 1, oob_is_err=False).then_inc(sem, 16)

        @block.vector
        def _(dve):
            ch = Chain(dve, chain)
            nc.vector.memset(prev[:], -1).then_inc(init, 1)
            nc.vector.memset(nxt[:], -1).then_inc(init, 1)
            nc.vector.memset(pads[:], 0.0).then_inc(init, 1)
            nc.vector.memset(record[:], 0.0).then_inc(init, 1)
            dve.wait_ge(init, 4)
            nc.vector.memset(pads[:, 9:10], FAR).then_inc(init, 1)
            dve.wait_ge(loaded, 96)
            ch.put(nc.vector.tensor_tensor(first[:], dst[:], prev[:], ALU.not_equal))
            ch.put(nc.vector.tensor_tensor(pen_l[:], dst[:], nxt[:], ALU.not_equal))
            ch.put(nc.vector.tensor_copy(record[:, :, 9], dst[:]))
            ch.put(nc.vector.tensor_copy(record[:, :, 10], src[:]))
            ch.wait()
            ch.put(nc.vector.tensor_copy(record[:, :, 8], first[:]))
            ch.put(nc.vector.tensor_scalar(pen_l[:], pen_l[:], LOW, None, ALU.mult))
            ch.put(nc.vector.tensor_scalar(pen_f[:], first[:], LOW, None, ALU.mult))
            ch.put(nc.vector.tensor_scalar(cont[:], first[:], -1.0, 1.0, ALU.mult, ALU.add))
            if more:
                more.vector(dve)
            dve.wait_ge(got_src, 16 * EC)
            dve.wait_ge(got_dst, 16 * EC)
            sides = gsrc[:].rearrange("p c h -> p h c"), gdst[:].rearrange("p c h -> p h c")
            for out, term in ((l, sides[0]), (ls, sides[1])):
                ch.link(nc.vector.tensor_tensor(raw[:], term[:, 0:H], sides[1][:, H:2 * H], ALU.add))
                ch.link(nc.vector.scalar_tensor_tensor(out=out[:], in0=raw[:], scalar=0.2, in1=raw[:], op0=ALU.mult,
                                                       op1=ALU.max))
            scans = [0]

            def scan(out, gate, x, op0, op1, neutral, backward):
                r = -1 if backward else 1
                n = scans[0]
                scans[0] += 1
                end = 0 if backward else EC - 1
                for h in range(H):
                    ch.put(nc.vector.tensor_tensor_scan(out=out[:, h, ::r], data0=gate[:, ::r], data1=x[:, h, ::r],
                                                        initial=neutral, op0=op0, op1=op1))
                ch.wait()
                ch.put(nc.vector.tensor_copy(edge[:, 0], out[:, :, end]))
                ch.link(nc.vector.tensor_reduce(edge[:, 1, 0:1], gate[:], AX.X, ALU.min))
                for h in range(1, H):
                    ch.put(nc.vector.tensor_copy(edge[:, 1, h:h + 1], edge[:, 1, 0:1]))
                ch.wait()
                nc.vector.tensor_copy(carry_t[:], zeros_t[:] if neutral == 0.0 else low_t[:]).then_inc(edge_ready, 1)
                dve.wait_ge(turned, n + 1)
                ch.link(nc.vector.tensor_copy(edge_t[:], pe_t[0:H, :, 0:EP]))
                dve.wait_ge(edge_ready, n + 1)
                at = slice(1, EP + 1)
                ch.link(nc.vector.tensor_tensor_scan(out=carry_t[:, at][:, ::r], data0=edge_t[:, 1, ::r],
                                                     data1=edge_t[:, 0, ::r], initial=neutral, op0=op0, op1=op1))
                nc.vector.tensor_copy(edge_t[:, 0], carry_t[:, 2:EP + 2] if backward else carry_t[:, 0:EP])\
                    .then_inc(carry_ready, 1)
                dve.wait_ge(back, n + 1)
                ch.link(nc.vector.tensor_copy(carry[:], pe_b[0:EP, 0:H]))
                for h in range(H):
                    ch.put(nc.vector.tensor_tensor_scan(out=out[:, h, ::r], data0=gate[:, ::r], data1=x[:, h, ::r],
                                                        initial=carry[:, h:h + 1], op0=op0, op1=op1))
                ch.wait()

            ch.put(nc.vector.memset(zeros_t[:], 0.0))
            ch.put(nc.vector.memset(low_t[:], LOW))
            ch.wait()
            scan(a, pen_f, l, ALU.add, ALU.max, LOW, False)
            scan(b, pen_l, a, ALU.add, ALU.max, LOW, True)
            ch.link(nc.vector.tensor_tensor(b[:], b[:], ls[:], ALU.max))
            ch.put(nc.vector.tensor_tensor(l[:], l[:], b[:], ALU.subtract))
            ch.link(nc.vector.tensor_tensor(ls[:], ls[:], b[:], ALU.subtract))
            nc.vector.memset(raw[:], 0.0).then_inc(shifted, 1)
            dve.wait_ge(exps, 2)
            scan(a, cont, ex, ALU.mult, ALU.add, 0.0, False)
            scan(b, pen_l, a, ALU.add, ALU.max, LOW, True)
            ch.link(nc.vector.tensor_tensor(b[:], b[:], exs[:], ALU.add))
            ch.link(nc.vector.tensor_scalar(b[:], b[:], 1e-16, None, ALU.add))
            ch.link(nc.vector.reciprocal(a[:], b[:]))
            by_head = lambda lo: record[:, :, lo:lo + H].rearrange("p c h -> p h c")
            ch.put(nc.vector.tensor_tensor(by_head(0), ex[:], a[:], ALU.mult))
            ch.link(nc.vector.tensor_tensor(exs[:], exs[:], a[:], ALU.mult))
            for h in range(H):
                ch.put(nc.vector.tensor_tensor(record[:, :, 4 + h], exs[:, h], first[:], ALU.mult))
            ch.wait()
            nc.vector.memset(raw[:], 0.0).then_inc(record_ready, 1)

        @block.scalar
        def _(act):
            if more:
                more.scalar(act)
            act.wait_ge(shifted, 1)
            nc.scalar.activation(ex[:], l[:], ACT.Exp).then_inc(exps, 1)
            nc.scalar.activation(exs[:], ls[:], ACT.Exp).then_inc(exps, 1)

        @block.tensor
        def _(pe):
            if more:
                more.tensor(pe)
            for n in range(4):
                pe.wait_ge(edge_ready, n + 1)
                pe.transpose(pe_t[0:H, 0, 0:EP], edge[:, 0], c.ident[0:EP, 0:EP])
                pe.transpose(pe_t[0:H, 1, 0:EP], edge[:, 1], c.ident[0:EP, 0:EP]).then_inc(turned, 1)
                pe.wait_ge(carry_ready, n + 1)
                pe.transpose(pe_b[0:EP, 0:H], edge_t[:, 0], c.ident[0:H, 0:H]).then_inc(back, 1)


ROWS_CHUNK, MASKS_CHUNK, WEIGHTS_CHUNK = 4, 5, 12
STEPS = NT * KC
XPER = 19
AT_STEP = {1 + 6 * i: i for i in range(WPS)}


def masks_beside(k):
    at = 2 * (k - MASKS_CHUNK)
    return range(at, at + 2) if 0 <= at < WPS else range(0)


def second_phase():
    for g in range(STEPS):
        if g in AT_STEP:
            yield "window", AT_STEP[g]
        if g % KC == KC - 1:
            yield "tile", g // KC


def table_value(eng, c, at, top):
    return eng.value_load(c.table[0:1, bass.ds(at, 1)], min_val=0, max_val=top)


def has_extras(eng, c, first, count):
    before = lambda w: table_value(eng, c, CHUNKS + w, MAX_CHUNKS)
    return before(first + count) > before(first)


def windows_with_extras(eng, c, first, count, chunk, any_of_them=None):
    before = lambda w: table_value(eng, c, CHUNKS + w, MAX_CHUNKS)
    with eng.If(has_extras(eng, c, first, count) if any_of_them is None else any_of_them):
        with eng.Fori(0, count) as i:
            lo, hi = before(first + i), before(first + i + 1)
            with eng.If(hi > lo):
                with eng.Fori(lo, hi) as k:
                    chunk(i, first + i, k)


def load_records(eng, c, rec, slots, sem, w, i):
    start = table_value(eng, c, w, E)
    eng.dma_start(slots[0:WE, i, :], rec[bass.ds(start, WE), :]).then_inc(sem, 16)


def load_extra_slots(nc, sp, c, rec, slots, sem, w, k):
    start = table_value(sp, c, w, E) + (k - table_value(sp, c, CHUNKS + w, MAX_CHUNKS)) * XE + WE
    start = nc.s_assert_within(start, 0, E, skip_runtime_bounds_check_because="a chunk starts at an edge of its window")
    for half in range(2):
        sp.dma_start(slots[XE * half:XE * half + XE, :], rec[bass.ds(start, XE), :]).then_inc(sem, 16)


def extra_slot_math(nc, ch, slots, rel, far, off, idx, idx_ready, w, heads):
    edges, nodes = slice(0, XE), slice(XE, 2 * XE)
    ch.link(nc.vector.tensor_tensor(rel[:], slots[:, 9:10], off, ALU.add))
    ch.link(nc.vector.tensor_scalar(far[:], rel[:], float(WN), FAR, ALU.is_ge, ALU.mult))
    nc.vector.tensor_tensor(idx[edges, :], slots[edges, 10:11], far[edges, :], ALU.add).then_inc(idx_ready, 1)
    nc.vector.tensor_tensor(idx[nodes, :], slots[nodes, 9:10], far[nodes, :], ALU.add).then_inc(idx_ready, 1)
    ch.put(nc.vector.tensor_copy(w[edges, :], slots[edges, 0:heads]))
    ch.link(nc.vector.tensor_scalar(w[nodes, :], slots[nodes, 4:4 + heads], slots[nodes, 8:9], None, ALU.subtract))


def stage_layers(nc, c, io, dr):
    with ExitStack() as ctx:
        m = Mem(nc, ctx, "lay")
        zh, zl = (m.sb(n, [128, DC, HEADS, SN], F16) for n in ("zh", "zl"))
        gh, gl = (m.sb(n, [128, KC, SN + 4], F16) for n in ("gh", "gl"))
        rows = m.sb("rows", [128, 2, 2 * D], F16)
        slots = m.sb("slots", [128, WPS, REC])
        rel, far, own = m.sb("rel", [128, WPS]), m.sb("far", [128, WPS]), m.sb("own", [128, WPS])
        woff, wself = m.sb("woff", [128, WPS]), m.sb("wself", [128, WPS])
        is_edge, is_self = m.sb("is_edge", [128, 1]), m.sb("is_self", [128, 1])
        step_off, step_self = m.sb("step_off", [128, 1]), m.sb("step_self", [128, 1])
        place, posi = m.sb("place", [128, 1]), m.sb("posi", [128, 128], I32)
        pos = m.sb("pos", [128, 128])
        idx = m.sb("idx", [128, WPS], I32)
        mask = m.sb("mask", [128, 2, 128])
        near = m.sb("near", [128, 2, WN], F16)
        w, wh, wl = m.sb("w", [128, WPS, HEADS]), m.sb("wh", [128, WPS, HEADS], F16), m.sb("wl", [128, WPS, HEADS], F16)
        ah, al = (m.sb(n, [128, 2, HEADS, WN], F16) for n in ("ah", "al"))
        ex, y = m.sb("ex", [128, 2, SN]), m.sb("y", [128, 2, SN])
        h2 = m.sb("h2", [128, 2, W2C])
        xslots, xoff = m.sb("xslots", [128, REC]), m.sb("xoff", [128, WPS])
        xrel, xfar, xidx = m.sb("xrel", [128, 1]), m.sb("xfar", [128, 1]), m.sb("xidx", [128, 1], I32)
        xw, xwh, xwl = m.sb("xw", [128, HEADS]), m.sb("xwh", [128, HEADS], F16), m.sb("xwl", [128, HEADS], F16)
        pz = [m.ps(f"pz{i}", [128, 512]) for i in range(3)]
        pm = [m.ps(f"pm{i}", [128, 512]) for i in range(4)]
        look = m.ps("look", [128, WPS, 5])
        (init, posed, slots_in, idx_ready, mask_ready, looked, a_ready, z_done, zh_ready, zl_ready, p1_done, ex_ready,
         y_ready, g_ready, gh_ready, gl_ready, tile_done, h2a, h2b, chain, setup, held, paused,
         xslots_free, xslots_in, xidx_ready, xgathered, xa_ready, xz_done, xz_added, xchain) = (m.sem(n) for n in (
             "init", "posed", "slots_in", "idx_ready", "mask_ready", "looked", "a_ready", "z_done", "zh_ready", "zl_ready",
             "p1_done", "ex_ready", "y_ready", "g_ready", "gh_ready", "gl_ready", "tile_done", "h2a", "h2b", "chain",
             "setup", "held", "paused",
             "xslots_free", "xslots_in", "xidx_ready", "xgathered", "xa_ready", "xz_done", "xz_added", "xchain"))
        gathered = [m.sem(f"gathered{b}") for b in range(2)]
        h2_out = [m.sem(f"h2_out{b}") for b in range(2)]
        block = ctx.enter_context(nc.Block())

        def window_shape(tile, k, i):
            return tile[:, 2 * k:2 * k + 2, :, WN * i:WN * i + WN].rearrange("p k h n -> p (k h) n")

        @block.sync
        def _(sp):
            def load_slots(q, first):
                if not first:
                    sp.wait_ge(a_ready, WPS * q)
                for i in range(WPS // 2 if first else WPS):
                    load_records(sp, c, dr.rec1, slots, slots_in, WPS * q + i, i)

            def extra_chunk(i, w, k):
                sp.wait_ge(xslots_free, k + 1)
                sp.sem_inc(paused, 1)
                load_extra_slots(nc, sp, c, dr.rec1, xslots, xslots_in, w, k)

            def body(s, first, last):
                if not last:
                    load_slots(s + 1, False)
                for t in range(NT):
                    sp.wait_ge(h2a, NT * s + t + 1)
                    sp.wait_ge(h2b, NT * s + t + 1)
                    for lo, hi in row_parts(TN):
                        node = SN * s + TN * t + lo
                        sp.dma_start(dr.h2[bass.ds(node, hi - lo), :], h2[lo:hi, t % 2, 0:D]).then_inc(h2_out[t % 2], 16)
                        sp.dma_start(dr.logit2[bass.ds(node, hi - lo), :], h2[lo:hi, t % 2, D:D + 2])\
                            .then_inc(h2_out[t % 2], 16)
                if not last:
                    windows_with_extras(sp, c, WPS * (s + 1), WPS, extra_chunk)

            sp.wait_ge(init, 3)
            load_slots(0, True)
            windows_with_extras(sp, c, 0, WPS, extra_chunk)
            body(0, True, False)
            with sp.Fori(1, NS - 1) as s:
                body(s, False, False)
            body(NS - 1, False, True)
            for b in range(2):
                sp.wait_ge(h2_out[b], 64 * (NT // 2) * NS)

        @block.gpsimd
        def _(pool):
            nc.gpsimd.iota(posi[:], pattern=[[1, 128]], base=-WE, channel_multiplier=0).then_inc(posed, 1)
            nc.gpsimd.iota(idx[:, 0:1], pattern=[[0, 1]], base=-WE, channel_multiplier=1).then_inc(posed, 1)

            def hold(sem, value):
                pool.wait_ge(sem, value)
                pool.sem_inc(held, 1)

            pool.wait_ge(posed, 2)

            def gather(q, first):
                hold(idx_ready, q + 1)
                for i in range(WPS):
                    if not (first and i < 2):
                        hold(z_done, 3 * (WPS * q + i - 1))
                    nc.gpsimd.indirect_dma_start(rows[:, i % 2, :], None, dr.parts[:, :], bass.IndirectOffsetOnAxis(
                        ap=idx[:, i:i + 1], axis=0), bounds_check=N - 1, oob_is_err=False).then_inc(gathered[i % 2], 16)

            def extra_chunk(i, w, k):
                hold(xidx_ready, 2 * k + 2)
                nc.gpsimd.indirect_dma_start(rows[:, 0, :], None, dr.parts[:, :], bass.IndirectOffsetOnAxis(
                    ap=xidx[:, 0:1], axis=0), bounds_check=N - 1, oob_is_err=False).then_inc(xgathered, 16)

            gather(0, True)
            windows_with_extras(pool, c, 0, WPS, extra_chunk)
            with pool.Fori(1, NS) as q:
                gather(q, False)
                windows_with_extras(pool, c, WPS * q, WPS, extra_chunk)

        @block.vector
        def _(dve):
            ch = Chain(dve, setup)
            nc.vector.memset(rows[:], 0.0).then_inc(init, 1)
            nc.vector.memset(gh[:, :, SN:], 0.0).then_inc(init, 1)
            nc.vector.memset(gl[:, :, SN:], 0.0)
            dve.wait_ge(posed, 2)
            ch.put(nc.vector.tensor_copy(pos[:], posi[:]))
            ch.put(nc.vector.memset(slots[:], 0.0))
            ch.link(nc.vector.tensor_copy(place[:], idx[:, 0:1]))
            ch.put(nc.vector.tensor_scalar(is_self[:], place[:], 0.0, None, ALU.is_ge))
            ch.link(nc.vector.tensor_scalar(is_edge[:], place[:], 0.0, None, ALU.is_lt))
            ch.put(nc.vector.tensor_scalar(step_off[:], is_edge[:], float(-SN), None, ALU.mult))
            ch.put(nc.vector.tensor_scalar(step_self[:], is_self[:], float(SN), None, ALU.mult))
            nc.vector.memset(xslots[:], 0.0).then_inc(xslots_free, 1)
            for i in range(WPS):
                ch.put(nc.vector.memset(xoff[:, i:i + 1], float(SN - WN * i)))
                ch.put(nc.vector.tensor_scalar(woff[:, i:i + 1], is_edge[:], float(-WN * i), None, ALU.mult))
                ch.put(nc.vector.tensor_scalar(wself[:, i:i + 1], place[:], float(WN * i), is_self[:, 0:1], ALU.add, ALU.mult))
                for h in range(HEADS):
                    ch.put(nc.vector.tensor_copy(slots[:, i, h:h + 1], is_self[:]))
                ch.put(nc.vector.tensor_scalar(slots[:, i, 9:10], place[:], 0.0, None, ALU.max))
            ch.wait()
            nc.vector.memset(near[:], 0.0).then_inc(init, 1)
            per = 10 + WPS

            def slot_math(qc, q, first):
                dve.wait_ge(slots_in, 16 * WPS * (q + 1))
                if not first:
                    for b in range(2):
                        dve.wait_ge(gathered[b], 16 * (WPS // 2) * q)
                qc.put(nc.vector.tensor_tensor(rel[:], slots[:, :, 9], woff[:], ALU.add))
                qc.link(nc.vector.tensor_tensor(own[:], slots[:, :, 10], wself[:], ALU.add))
                qc.put(nc.vector.tensor_scalar(woff[:], woff[:], step_off[:, 0:1], None, ALU.add))
                qc.put(nc.vector.tensor_scalar(wself[:], wself[:], step_self[:, 0:1], None, ALU.add))
                qc.put(nc.vector.tensor_scalar(xoff[:], xoff[:], float(-SN), None, ALU.add))
                qc.link(nc.vector.tensor_scalar(far[:], rel[:], float(WN), FAR, ALU.is_ge, ALU.mult))
                nc.vector.tensor_tensor(idx[:], own[:], far[:], ALU.add).then_inc(idx_ready, 1)

            def window_mask(q, i, first):
                if not (first and i < 2):
                    dve.wait_ge(looked, WPS * q + i - 1)
                nc.vector.tensor_scalar(mask[:, i % 2], pos[:], rel[:, i:i + 1], None, ALU.is_equal).then_inc(mask_ready, 1)

            def weights(qc, q):
                dve.wait_ge(looked, WPS * (q + 1))
                qc.link(nc.vector.tensor_tensor(w[:], slots[:, :, 0:HEADS], look[:, :, 4:5].broadcast_to([128, WPS, HEADS]),
                                                ALU.subtract))
                qc.link(nc.vector.tensor_tensor(w[:], w[:], look[:, :, 0:HEADS], ALU.add))
                qc.link(nc.vector.tensor_scalar(wh[:], w[:], SA, None, ALU.mult))
                qc.link(nc.vector.scalar_tensor_tensor(out=wl[:], in0=w[:], scalar=SA, in1=wh[:], op0=ALU.mult,
                                                       op1=ALU.subtract))

            def spread(qc, q, i, first):
                if not (first and i < 2):
                    dve.wait_ge(z_done, 3 * (WPS * q + i - 1))
                qc.link(nc.vector.tensor_scalar(near[:, i % 2], pos[:, WE:], rel[:, i:i + 1], None, ALU.is_equal))
                m_ = near[:, i % 2:i % 2 + 1, :].broadcast_to([128, HEADS, WN])
                of = lambda t: t[:, i, :].rearrange("p (h a) -> p h a", a=1).broadcast_to([128, HEADS, WN])
                nc.vector.tensor_tensor(ah[:, i % 2], m_, of(wh), ALU.mult)
                nc.vector.tensor_tensor(al[:, i % 2], m_, of(wl), ALU.mult).then_inc(a_ready, 1)

            def low_parts(q, i):
                for k in range(3):
                    dve.wait_ge(zh_ready, 3 * (WPS * q + i) + k + 1)
                    nc.vector.scalar_tensor_tensor(
                        out=window_shape(zl, k, i), in0=pz[k][:, 0:2 * HEADS * WN].rearrange("p (k n) -> p k n", n=WN),
                        scalar=1.0 / SA, in1=window_shape(zh, k, i), op0=ALU.mult, op1=ALU.subtract).then_inc(zl_ready, 1)

            def extra_chunk(i, w, k):
                xc = Chain(dve, xchain, XPER * k)
                dve.wait_ge(xslots_in, 32 * k + 32)
                extra_slot_math(nc, xc, xslots, xrel, xfar, xoff[:, bass.ds(i, 1)], xidx, xidx_ready, xw, HEADS)
                xc.put(nc.vector.tensor_scalar(near[:, 0], pos[:, WE:], xrel[:, 0:1], None, ALU.is_equal))
                xc.link(nc.vector.tensor_scalar(xwh[:], xw[:], SA, None, ALU.mult))
                xc.link(nc.vector.scalar_tensor_tensor(out=xwl[:], in0=xw[:], scalar=SA, in1=xwh[:], op0=ALU.mult,
                                                       op1=ALU.subtract))
                nc.vector.memset(xfar[:], 0.0).then_inc(xslots_free, 1)
                of = lambda t: t[:].rearrange("p (h a) -> p h a", a=1).broadcast_to([128, HEADS, WN])
                m_ = near[:, 0:1, :].broadcast_to([128, HEADS, WN])
                nc.vector.tensor_tensor(ah[:, 0], m_, of(xwh), ALU.mult)
                nc.vector.tensor_tensor(al[:, 0], m_, of(xwl), ALU.mult).then_inc(xa_ready, 1)
                dve.wait_ge(xz_done, k + 1)
                for j in range(3):
                    z_hi, z_lo = (t[:, 2 * j:2 * j + 2, :, bass.ds(WN * i, WN)].rearrange("p k h n -> p (k h) n")
                                  for t in (zh, zl))
                    as_window = lambda t: t[:, 0:2 * HEADS * WN].rearrange("p (k n) -> p k n", n=WN)
                    part, total = as_window(ex[:, 0]), as_window(y[:, 0])
                    xc.link(nc.vector.scalar_tensor_tensor(out=part, in0=as_window(pz[j]), scalar=1.0 / SA, in1=z_hi,
                                                           op0=ALU.mult, op1=ALU.add))
                    xc.link(nc.vector.tensor_tensor(total, part, z_lo, ALU.add))
                    xc.link(nc.vector.tensor_scalar(z_hi, total, 1.0, None, ALU.mult))
                    xc.link(nc.vector.tensor_tensor(z_lo, total, z_hi, ALU.subtract))
                nc.vector.memset(xfar[:], 0.0).then_inc(xz_added, 1)
                assert xc.n == XPER, xc.n

            def elu(gc, s, k, first):
                dve.wait_ge(ex_ready, KC * s + k + 1)
                gc.link(nc.vector.tensor_scalar(ex[:, k % 2], ex[:, k % 2], 1.0, c.scale[:, 2:3], ALU.min, ALU.mult))
                dve.wait_ge(y_ready, KC * s + k + 1)
                nc.vector.scalar_tensor_tensor(out=y[:, k % 2], in0=ex[:, k % 2], scalar=c.scale[:, 10:11], in1=y[:, k % 2],
                                               op0=ALU.add, op1=ALU.max).then_inc(g_ready, 1)

            def elu_low(s, k):
                dve.wait_ge(gh_ready, KC * s + k + 1)
                nc.vector.tensor_tensor(gl[:, k, 0:SN], y[:, k % 2], gh[:, k, 0:SN], ALU.subtract).then_inc(gl_ready, 1)

            def body(s, first, last):
                q = s + 1
                gc = Chain(dve, chain, KC * s)
                qc = Chain(dve, setup, q * per + ch.n)
                for k in range(KC):
                    elu(gc, s, k, first)
                    if k:
                        elu_low(s, k - 1)
                    if last:
                        continue
                    if k == ROWS_CHUNK:
                        slot_math(qc, q, False)
                    if k == ROWS_CHUNK + 1:
                        qc.wait()
                    for i in masks_beside(k):
                        window_mask(q, i, False)
                    if k == WEIGHTS_CHUNK:
                        weights(qc, q)
                    if k in (WEIGHTS_CHUNK + 1, WEIGHTS_CHUNK + 2):
                        spread(qc, q, k - WEIGHTS_CHUNK - 1, False)
                elu_low(s, KC - 1)
                extras = None if last else has_extras(dve, c, WPS * q, WPS)
                for what, n in second_phase():
                    if what == "window" and not last:
                        low_parts(q, n)
                        if n + 2 < WPS:
                            spread(qc, q, n + 2, False)
                    if what == "tile":
                        dve.wait_ge(tile_done, NT * s + n + 1)
                        if not (first and n < 2):
                            dve.wait_ge(h2_out[n % 2], 64 * ((NT * s + n) // 2) if isinstance(s, int) else
                                        64 * (NT // 2) * s + 64 * (n // 2))
                        nc.vector.tensor_scalar(h2[:, n % 2, 512:D + 2], pm[2 * (n % 2) + 1][:, 0:D + 2 - 512],
                                                c.scale[:, 11:12], None, ALU.mult).then_inc(h2b, 1)
                if not last:
                    windows_with_extras(dve, c, WPS * q, WPS, extra_chunk, extras)
                assert last or qc.n == per, qc.n

            qc = Chain(dve, setup, ch.n)
            slot_math(qc, 0, True)
            qc.wait()
            for i in range(WPS):
                window_mask(0, i, True)
            weights(qc, 0)
            spread(qc, 0, 0, True)
            spread(qc, 0, 1, True)
            for i in range(WPS):
                low_parts(0, i)
                if i + 2 < WPS:
                    spread(qc, 0, i + 2, True)
            assert qc.n == per, qc.n
            windows_with_extras(dve, c, 0, WPS, extra_chunk)
            body(0, True, False)
            with dve.Fori(1, NS - 1) as s:
                body(s, False, False)
            body(NS - 1, False, True)

        @block.scalar
        def _(act):
            def high_parts(q, i):
                for k in range(3):
                    act.wait_ge(z_done, 3 * (WPS * q + i) + k + 1)
                    nc.scalar.activation(window_shape(zh, k, i), pz[k][:, 0:2 * HEADS * WN].rearrange("p (k n) -> p k n", n=WN),
                                         ACT.Copy, scale=1.0 / SA).then_inc(zh_ready, 1)

            def body(s, first, last):
                for k in range(KC):
                    act.wait_ge(p1_done, KC * s + k + 1)
                    if not (first and k < 2):
                        act.wait_ge(gl_ready, KC * s + k - 1)
                    p = pm[k % 4][:, 0:SN]
                    nc.scalar.activation(ex[:, k % 2], p, ACT.Exp, bias=c.b1[:, k:k + 1], scale=c.scale[:, 8:9])\
                        .then_inc(ex_ready, 1)
                    nc.scalar.activation(y[:, k % 2], p, ACT.Identity, bias=c.b1s[:, k:k + 1], scale=c.scale[:, 9:10])\
                        .then_inc(y_ready, 1)
                    if k:
                        high(s, k - 1)
                high(s, KC - 1)
                for what, n in second_phase():
                    if what == "window" and not last:
                        high_parts(s + 1, n)
                    if what == "tile":
                        act.wait_ge(tile_done, NT * s + n + 1)
                        if not (first and n < 2):
                            act.wait_ge(h2_out[n % 2], 64 * (NT // 2) * s + 64 * (n // 2))
                        nc.scalar.activation(h2[:, n % 2, 0:512], pm[2 * (n % 2)][:], ACT.Copy, scale=c.scale[:, 11:12])\
                            .then_inc(h2a, 1)

            def high(s, k):
                act.wait_ge(g_ready, KC * s + k + 1)
                nc.scalar.activation(gh[:, k, 0:SN], y[:, k % 2], ACT.Copy).then_inc(gh_ready, 1)

            act.wait_ge(init, 3)
            for i in range(WPS // 2, WPS):
                load_records(act, c, dr.rec1, slots, slots_in, i, i)
            for i in range(WPS):
                high_parts(0, i)
            body(0, True, False)
            with act.Fori(1, NS - 1) as s:
                body(s, False, False)
            body(NS - 1, False, True)

        @block.tensor
        def _(pe):
            pe.wait_ge(init, 2)

            def look_up(q, i):
                pe.wait_ge(mask_ready, WPS * q + i + 1)
                pe.matmul(look[:, i], mask[:, i % 2], slots[:, i, 4:9], start=True, stop=True).then_inc(looked, 1)

            def window_products(d, b):
                o = pz[d // 2][:, d % 2 * HEADS * WN:(d % 2 + 1) * HEADS * WN]
                high, low = (rows[:, b, part * D + 128 * d:part * D + 128 * d + 128] for part in range(2))
                flat = lambda t: t[:, b].rearrange("p h n -> p (h n)")
                pe.matmul(o, high, flat(ah), start=True, stop=False)
                pe.matmul(o, high, flat(al), start=False, stop=False)
                return pe.matmul(o, low, flat(ah), start=False, stop=True)

            def window(q, i, first):
                pe.wait_ge(gathered[i % 2], 16 * (WPS // 2) * q + 16 * (i // 2 + 1))
                pe.wait_ge(a_ready, WPS * q + i + 1)
                for k in range(3):
                    if not (first and i == 0):
                        pe.wait_ge(zl_ready, 3 * (WPS * q + i - 1) + k + 1)
                    for d in (2 * k, 2 * k + 1):
                        ins = window_products(d, i % 2)
                    ins.then_inc(z_done, 1)

            def extra_chunk(i, w, k):
                pe.wait_ge(xgathered, 16 * k + 16)
                pe.wait_ge(xa_ready, k + 1)
                for d in range(DC):
                    ins = window_products(d, 0)
                ins.then_inc(xz_done, 1)
                pe.wait_ge(xz_added, k + 1)

            def body(s, first, last):
                q = s + 1
                pe.wait_ge(zl_ready, 3 * WPS * (s + 1))
                for k in range(KC):
                    h = k // (KC // HEADS)
                    if k >= 4:
                        pe.wait_ge(y_ready, KC * s + k - 3)
                    elif not first:
                        pe.wait_ge(h2a, NT * s - 1 + k // 2)
                        pe.wait_ge(h2b, NT * s - 1 + k // 2)
                    for d in range(DC):
                        cols = slice(128 * k, 128 * k + 128)
                        o = pm[k % 4][:, 0:SN]
                        pe.matmul(o, c.w1h[:, d, cols], zh[:, d, h], start=(d == 0), stop=False)
                        pe.matmul(o, c.w1h[:, d, cols], zl[:, d, h], start=False, stop=False)
                        ins = pe.matmul(o, c.w1l[:, d, cols], zh[:, d, h], start=False, stop=(d == DC - 1))
                    ins.then_inc(p1_done, 1)
                    if not last:
                        for i in masks_beside(k - 1):
                            look_up(q, i)
                extras = None if last else has_extras(pe, c, WPS * q, WPS)
                for g in range(STEPS):
                    t, k = g // KC, g % KC
                    if g in AT_STEP and not last:
                        window(q, AT_STEP[g], False)
                    oa, ob = pm[2 * (t % 2)], pm[2 * (t % 2) + 1]
                    if k == 0:
                        if t < 2:
                            pe.wait_ge(y_ready, KC * s + 14 + 2 * t)
                        else:
                            pe.wait_ge(h2a, NT * s + t - 1)
                            pe.wait_ge(h2b, NT * s + t - 1)
                    if t == 0:
                        pe.wait_ge(gl_ready, KC * s + k + 1)
                    nodes = slice(TN * t, TN * t + 128)
                    for n, (x, wt) in enumerate(((gh, c.w2h), (gh, c.w2l), (gl, c.w2h))):
                        go = dict(start=(k == 0 and n == 0), stop=(k == KC - 1 and n == 2))
                        pe.matmul(oa[:], x[:, k, nodes], wt[:, k, 0:512], **go)
                        ins = pe.matmul(ob[:, 0:D + 2 - 512], x[:, k, nodes], wt[:, k, 512:D + 2], **go)
                    if k == KC - 1:
                        ins.then_inc(tile_done, 1)
                if not last:
                    pe.wait_ge(zl_ready, 3 * WPS * (q + 1))
                    z_extras(q, extras)

            def z_extras(q, extras):
                windows_with_extras(pe, c, WPS * q, WPS, extra_chunk, extras)

            for i in range(WPS):
                look_up(0, i)
            for i in range(WPS):
                window(0, i, True)
            pe.wait_ge(zl_ready, 3 * WPS)
            z_extras(0, None)
            body(0, True, False)
            with pe.Fori(1, NS - 1) as s:
                body(s, False, False)
            body(NS - 1, False, True)


def stage_extra_rows(nc, c, io, dr):
    with ExitStack() as ctx:
        m = Mem(nc, ctx, "more")
        slots, rows, acc = m.sb("slots", [128, REC]), m.sb("rows", [128, D]), m.sb("acc", [WN, D])
        rel, far, idx, w_ = m.sb("rel", [128, 1]), m.sb("far", [128, 1]), m.sb("idx", [128, 1], I32), m.sb("w", [128, 1])
        offi, off = m.sb("offi", [128, NW], I32), m.sb("off", [128, NW])
        posi, pos, att = m.sb("posi", [128, 128], I32), m.sb("pos", [128, 128]), m.sb("att", [128, 128])
        pa, pb = m.ps("pa", [128, 512]), m.ps("pb", [128, D - 512])
        (posed, copied, slots_free, slots_in, acc_in, idx_ready, gathered, att_ready, summed, added, stored, chain,
         held) = (m.sem(n) for n in ("posed", "copied", "slots_free", "slots_in", "acc_in", "idx_ready", "gathered",
                                     "att_ready", "summed", "added", "stored", "chain", "held"))
        block = ctx.enter_context(nc.Block())
        COPIES = 4
        any_chunk = lambda eng: eng.If(table_value(eng, c, CHUNKS + NW, MAX_CHUNKS) > 0)

        @block.sync
        def _(sp):
            def chunk(i, w, k):
                sp.wait_ge(slots_free, k + 1)
                sp.sem_inc(held, 1)
                load_extra_slots(nc, sp, c, dr.rec2, slots, slots_in, w, k)
                part = bass.ds(WN * w, WN)
                sp.dma_start(acc[:], dr.x_more[part, :]).then_inc(acc_in, 16)
                sp.wait_ge(added, k + 1)
                sp.sem_inc(held, 1)
                sp.dma_start(dr.x_more[part, :], acc[:]).then_inc(stored, 16)
                sp.wait_ge(stored, 16 * k + 16)
                sp.sem_inc(held, 1)

            with any_chunk(sp):
                for n in range(COPIES):
                    part = slice(n * (N // COPIES), (n + 1) * (N // COPIES))
                    sp.dma_start(dr.x_more[part, :], io["x"][part, :]).then_inc(copied, 16)
                sp.wait_ge(copied, 16 * COPIES)
                windows_with_extras(sp, c, 0, NW, chunk)

        @block.gpsimd
        def _(pool):
            def chunk(i, w, k):
                pool.wait_ge(idx_ready, 2 * k + 2)
                pool.sem_inc(held, 1)
                nc.gpsimd.indirect_dma_start(rows[:, :], None, dr.h2[:, :], bass.IndirectOffsetOnAxis(ap=idx[:, 0:1], axis=0),
                                             bounds_check=N - 1, oob_is_err=False).then_inc(gathered, 16)

            with any_chunk(pool):
                nc.gpsimd.iota(posi[:], pattern=[[1, 128]], base=0, channel_multiplier=0).then_inc(posed, 1)
                nc.gpsimd.iota(offi[:], pattern=[[-WN, NW]], base=0, channel_multiplier=0).then_inc(posed, 1)
                windows_with_extras(pool, c, 0, NW, chunk)

        @block.vector
        def _(dve):
            def chunk(i, w, k):
                ch = Chain(dve, chain, 4 * k + 4)
                dve.wait_ge(slots_in, 32 * k + 32)
                extra_slot_math(nc, ch, slots, rel, far, off[:, bass.ds(w, 1)], idx, idx_ready, w_, 1)
                nc.vector.memset(far[:], 0.0).then_inc(slots_free, 1)
                nc.vector.tensor_scalar(att[:], pos[:], rel[:, 0:1], w_[:, 0:1], ALU.is_equal, ALU.mult).then_inc(att_ready, 1)
                dve.wait_ge(summed, k + 1)
                dve.wait_ge(acc_in, 16 * k + 16)
                nc.vector.tensor_tensor(acc[:, 0:512], acc[:, 0:512], pa[0:WN, :], ALU.add)
                nc.vector.tensor_tensor(acc[:, 512:D], acc[:, 512:D], pb[0:WN, :], ALU.add).then_inc(added, 1)
                assert ch.n == 4, ch.n

            with any_chunk(dve):
                ch = Chain(dve, chain)
                ch.put(nc.vector.memset(rows[:], 0.0))
                dve.wait_ge(posed, 2)
                ch.put(nc.vector.tensor_copy(pos[:], posi[:]))
                ch.put(nc.vector.tensor_copy(off[:], offi[:]))
                ch.link(nc.vector.memset(far[:], 0.0))
                nc.vector.memset(rel[:], 0.0).then_inc(slots_free, 1)
                windows_with_extras(dve, c, 0, NW, chunk)

        @block.tensor
        def _(pe):
            def chunk(i, w, k):
                pe.wait_ge(att_ready, k + 1)
                pe.wait_ge(gathered, 16 * k + 16)
                pe.matmul(pa[:], att[:], rows[:, 0:512], start=True, stop=True)
                pe.matmul(pb[:], att[:], rows[:, 512:D], start=True, stop=True).then_inc(summed, 1)
                pe.wait_ge(added, k + 1)

            with any_chunk(pe):
                windows_with_extras(pe, c, 0, NW, chunk)


OT = 2 * WN
GT = 10
GW = 2 * GT
NG = N // (OT * GT)
RB = 10
AHEAD = 2
X_AHEAD = 4
LOOKS = 7
ROWS_AT, LOOKS_AT, WEIGHTS_AT, REST_AT = 3, 4, 7, 9
LOADS = 3
MB = 2 * LOOKS
PREP = 8
GELU_C = float(np.sqrt(2.0 / np.pi))
EMBEDS = (384, 576, D)
PARTS = (slice(0, EMBEDS[0]), slice(EMBEDS[0], EMBEDS[1]), slice(EMBEDS[1], EMBEDS[2]))
assert F <= 2 * EMBEDS[0]


def stage_output(nc, c, io, dr):
    with ExitStack() as ctx:
        m = Mem(nc, ctx, "out")
        wfc, wpr = m.sb("wfc", [F, D]), m.sb("wpr", [128, DC, F])
        w0, w1 = m.sb("w0", [128, DC, F]), m.sb("w1", [F + 1, D])
        b0, b2 = m.sb("b0", [F, 1]), m.sb("b2", [OT, D])
        bp = m.sb("bp", [1, D])
        ae, ar, pairs, coef = m.sb("ae", [128, 3]), m.sb("ar", [128, 3]), m.sb("pairs", [128, 3]), m.sb("coef", [128, 3])
        x = m.sb("x", [OT, GT, D])
        xn = m.sb("xn", [OT, 2, D])
        xt = m.sb("xt", [128, 2, DC, OT])
        rows = m.sb("rows", [128, RB, D])
        slots = m.sb("slots", [128, GW, REC])
        names = ("rel", "far", "own", "woff", "wself", "w", "rel_now", "w_now")
        rel, far, own, woff, wself, w, rel_now, w_now = (m.sb(n, [128, GW]) for n in names)
        idx, idx_now = m.sb("idx", [128, GW], I32), m.sb("idx_now", [128, GW], I32)
        is_edge, is_self, step_off, step_self, place = (m.sb(n, [128, 1]) for n in ("is_edge", "is_self", "step_off",
                                                                                   "step_self", "place"))
        posi = m.sb("posi", [128, 128], I32)
        pos, pos_own = m.sb("pos", [128, 128]), m.sb("pos_own", [128, 128])
        mask = m.sb("mask", [128, MB, 128])
        att = m.sb("att", [128, RB, 128])
        stats, mv = m.sb("stats", [OT, 2, 2, 6]), m.sb("mv", [OT, 2, 2])
        ve, nm, rough, sq, rstd, shift = (m.sb(n, [OT, 2]) for n in ("ve", "nm", "rough", "sq", "rstd", "shift"))
        onehalf = m.sb("onehalf", [OT, 1])
        power, spare = m.sb("power", [OT, 1]), m.sb("spare", [1, 1])
        u, u2, th = (m.sb(n, [F, 2, OT]) for n in ("u", "u2", "th"))
        g = m.sb("g", [F + 1, 2, OT])
        pa = [m.ps(f"pa{i}", [128, 512]) for i in range(2)]
        pa_tail = m.ps("pa_tail", [128, D - 512])
        pt = [m.ps(f"pt{i}", [128, 4, 128]) for i in range(2)]
        po = [m.ps(f"po{i}", [128, 512]) for i in range(2)]
        ph = m.ps("ph", [128, 512])
        look = ph[:, 0:2 * GW].rearrange("p (i k) -> p i k", k=2)
        hid = ph[0:F, 128:128 + OT]
        sems = ("par_in", "turned_w", "w_ready", "init", "posed", "slots_in", "idx_ready", "mask_ready",
                "looked", "weights_ready", "att_ready", "agg_done", "x2_ready", "ve_ready", "norm_ready", "newton", "xn_ready",
                "turned", "xt_ready", "h_done", "u_ready", "t_ready", "th_ready", "g_ready", "o_done", "o_ready",
                "xb_ready", "tail_read", "chain", "setup", "gelu", "prep", "bias_in",
                "held", "paused")
        (par_in, turned_w, w_ready, init, posed, slots_in, idx_ready, mask_ready, looked, weights_ready,
         att_ready, agg_done, x2_ready, ve_ready, norm_ready, newton, xn_ready, turned, xt_ready, h_done, u_ready, t_ready,
         th_ready, g_ready, o_done, o_ready, xb_ready, tail_read, chain, setup, gelu, prep, bias_in, held, paused) = (m.sem(n) for n in sems)
        gathered = [m.sem(f"gathered{b}") for b in range(RB)]
        x_in = [m.sem(f"x_in{j}") for j in range(GT)]
        x_out = [m.sem(f"x_out{j}") for j in range(GT)]
        block = ctx.enter_context(nc.Block())
        TILES = NG * GT
        FIRST, LAST = -AHEAD, TILES + 3

        def schedule(eng, iteration):
            for t in range(FIRST, GT):
                iteration(t // GT, t % GT)
            with eng.Fori(1, NG - 2) as grp:
                for j in range(GT):
                    iteration(grp, j)
            for t in range((NG - 2) * GT, LAST + 1):
                iteration(t // GT, t % GT)

        def tile_at(grp, j, ahead):
            at = j + ahead
            there, t = grp + at // GT, GT * grp + at
            return t, at % GT, there, (0 <= t < TILES if isinstance(t, int) else True)

        def beyond(t, n):
            return t >= n if isinstance(t, int) else True

        def looks(j):
            at = LOOKS * (j - LOOKS_AT)
            return range(at, min(at + LOOKS, GW)) if 0 <= at < GW else range(0)

        def next_group(grp):
            return 0 <= grp < NG - 1 if isinstance(grp, int) else True

        @block.sync
        def _(sp):
            row = lambda name: io[name].rearrange("(a d) -> a d", a=1)
            sp.dma_start(ae[:], row("alpha_e").broadcast_to([128, 3])).then_inc(par_in, 16)
            sp.dma_start(ar[:], row("alpha_r").broadcast_to([128, 3])).then_inc(par_in, 16)
            sp.dma_start(wfc[:], io["w_fc"]).then_inc(par_in, 16)
            sp.dma_start(wpr[:], io["w_proj"].rearrange("(k p) f -> p k f", p=128)).then_inc(par_in, 16)
            sp.dma_start(b0[:], io["b_fc"].rearrange("(p a) -> p a", a=1)).then_inc(par_in, 16)
            sp.dma_start(bp[:], row("b_proj")).then_inc(par_in, 16)
            sp.dma_start(b2[:], row("b2").broadcast_to([OT, D])).then_inc(par_in, 16)

            def load_slots(grp, windows):
                for i in windows:
                    load_records(sp, c, dr.rec2, slots, slots_in, GW * grp + i, i)

            chunks = table_value(sp, c, CHUNKS + NW, MAX_CHUNKS)

            def load_rows(t, at, source, wait):
                if wait is not None:
                    sp.wait_ge(x_out[at], wait)
                    sp.sem_inc(paused, 1)
                for lo, hi in row_parts(OT):
                    sp.dma_start(x[lo:hi, at], source[bass.ds(OT * t + lo, hi - lo), :]).then_inc(x_in[at], 16)

            def load_x(t, at, wait=None):
                with sp.If(chunks > 0):
                    load_rows(t, at, dr.x_more, wait)
                with sp.Else():
                    load_rows(t, at, io["x"], wait)

            def iteration(grp, j):
                t, at, there, ok = tile_at(grp, j, X_AHEAD)
                if ok:
                    load_x(t, at, 32 * there if beyond(t, GT) else None)
                part = (j - WEIGHTS_AT - 1) % GT
                of = grp + 2 if j > WEIGHTS_AT else grp + 1
                if part < LOADS and (not isinstance(of, int) or 1 <= of < NG):
                    sp.wait_ge(weights_ready, of)
                    load_slots(of, range(GW * part // LOADS, GW * (part + 1) // LOADS))
                t, at, there, ok = tile_at(grp, j, -4)
                if ok:
                    sp.wait_ge(o_ready, t + 1)
                    for lo, hi in row_parts(OT):
                        sp.dma_start(dr.out[bass.ds(OT * t + lo, hi - lo), :], x[lo:hi, at]).then_inc(x_out[at], 16)

            sp.wait_ge(init, 2)
            load_slots(0, range(GW // 2))
            for at in range(X_AHEAD - AHEAD):
                load_x(at, at)
            sp.wait_ge(w_ready, 2)
            sp.dma_start(w1[F:F + 1, :], bp[:]).then_inc(bias_in, 16)
            schedule(sp, iteration)
            for j in range(GT):
                sp.wait_ge(x_out[j], 32 * NG)

        @block.gpsimd
        def _(pool):
            def hold(sem, value):
                pool.wait_ge(sem, value)
                pool.sem_inc(held, 1)

            nc.gpsimd.iota(posi[:], pattern=[[1, 128]], base=0, channel_multiplier=0).then_inc(posed, 1)
            nc.gpsimd.iota(idx[:, 0:1], pattern=[[0, 1]], base=-WE, channel_multiplier=1).then_inc(posed, 1)
            nc.gpsimd.memset(power[:], -0.5).then_inc(posed, 1)
            nc.gpsimd.memset(onehalf[:], 1.5).then_inc(posed, 1)
            nc.gpsimd.memset(rows[:], 0.0).then_inc(posed, 1)
            pool.wait_ge(posed, 5)
            pool.wait_ge(par_in, 16 * 7)
            pool.wait_ge(init, 2)

            def iteration(grp, j):
                t, at, there, ok = tile_at(grp, j, 1)
                if ok:
                    pool.wait_ge(x_in[at], 32 * (there + 1))
                    nc.gpsimd.tensor_tensor(x[:, at], x[:, at], b2[:], ALU.add).then_inc(xb_ready, 1)
                t, at, there, ok = tile_at(grp, j, AHEAD)
                if ok:
                    if at % (RB // 2) == 0:
                        hold(idx_ready, 2 * there + 1 + at // (RB // 2))
                    if beyond(t, RB // 2):
                        hold(agg_done, t + 1 - RB // 2)
                    for i in (2 * at, 2 * at + 1):
                        nc.gpsimd.indirect_dma_start(
                            rows[:, i % RB, :], None, dr.h2[:, :], bass.IndirectOffsetOnAxis(ap=idx_now[:, i:i + 1], axis=0),
                            bounds_check=N - 1, oob_is_err=False).then_inc(gathered[i % RB], 16)
                t, at, there, ok = tile_at(grp, j, 0)
                if ok:
                    rough_, sq_, ve_, rstd_ = (a[:, at % 2:at % 2 + 1] for a in (rough, sq, ve, rstd))
                    nw = Chain(pool, newton, 6 * t)
                    pool.wait_ge(ve_ready, t + 1)
                    nw.link(nc.gpsimd.tensor_tensor(rough_, ve_, power[:], ALU.pow))
                    nw.link(nc.gpsimd.tensor_tensor(sq_, rough_, rough_, ALU.mult))
                    nw.link(nc.gpsimd.tensor_tensor(sq_, sq_, ve_, ALU.mult))
                    nw.link(nc.gpsimd.tensor_tensor(sq_, sq_, power[:], ALU.mult))
                    nw.link(nc.gpsimd.tensor_tensor(sq_, sq_, onehalf[:], ALU.add))
                    if beyond(t, 2):
                        pool.wait_ge(xn_ready, t - 1)
                    nw.link(nc.gpsimd.tensor_tensor(rstd_, rough_, sq_, ALU.mult))
                    nc.gpsimd.tensor_tensor(shift[:, at % 2:at % 2 + 1], nm[:, at % 2:at % 2 + 1], rstd_, ALU.mult)\
                        .then_inc(norm_ready, 1)

            schedule(pool, iteration)

        @block.vector
        def _(dve):
            ch = Chain(dve, setup)
            ch.put(nc.vector.memset(att[:], 0.0))
            ch.put(nc.vector.memset(w1[:], 0.0))
            ch.put(nc.vector.memset(g[:], 1.0))
            dve.wait_ge(posed, 2)
            ch.put(nc.vector.tensor_copy(pos[:], posi[:]))
            ch.put(nc.vector.tensor_scalar(pos_own[:], posi[:], float(-WE), None, ALU.add))
            ch.put(nc.vector.memset(slots[:], 0.0))
            ch.link(nc.vector.tensor_copy(place[:], idx[:, 0:1]))
            ch.put(nc.vector.tensor_scalar(is_self[:], place[:], 0.0, None, ALU.is_ge))
            ch.link(nc.vector.tensor_scalar(is_edge[:], place[:], 0.0, None, ALU.is_lt))
            ch.put(nc.vector.tensor_scalar(step_off[:], is_edge[:], float(-WN * GW), None, ALU.mult))
            ch.put(nc.vector.tensor_scalar(step_self[:], is_self[:], float(WN * GW), None, ALU.mult))
            for i in range(GW):
                ch.put(nc.vector.tensor_scalar(woff[:, i:i + 1], is_edge[:], float(-WN * i), None, ALU.mult))
                ch.put(nc.vector.tensor_scalar(wself[:, i:i + 1], place[:], float(WN * i), is_self[:, 0:1], ALU.add, ALU.mult))
                ch.put(nc.vector.tensor_copy(slots[:, i, 0:1], is_self[:]))
                ch.put(nc.vector.tensor_scalar(slots[:, i, 9:10], place[:], 0.0, None, ALU.max))
            ch.wait()
            nc.vector.memset(mask[:], 0.0).then_inc(init, 1)
            nc.vector.memset(far[:], 0.0).then_inc(init, 1)

            dve.wait_ge(par_in, 16 * 7)
            ch.link(nc.vector.tensor_scalar(pairs[:], ae[:], ar[:, 0:1], None, ALU.mult))
            for n in (1, 2):
                ch.link(nc.vector.scalar_tensor_tensor(out=pairs[:], in0=ae[:], scalar=ar[:, n:n + 1], in1=pairs[:],
                                                       op0=ALU.mult, op1=ALU.add))
            ch.link(nc.vector.tensor_copy(coef[:, 2:3], pairs[:, 2:3]))
            for n in (1, 0):
                ch.link(nc.vector.tensor_tensor(coef[:, n:n + 1], pairs[:, n:n + 1], coef[:, n + 1:n + 2], ALU.add))
            for n, part in enumerate(PARTS):
                ch.put(nc.vector.tensor_scalar(wfc[:, part], wfc[:, part], coef[0:F, n:n + 1], None, ALU.mult))
                ch.put(nc.vector.tensor_scalar(bp[:, part], bp[:, part], coef[0:1, n:n + 1], None, ALU.mult))
            ch.put(nc.vector.tensor_scalar(b0[:], b0[:], coef[0:F, 0:1], None, ALU.mult))
            ch.wait()
            nc.vector.memset(th[:], 0.0).then_inc(w_ready, 1)
            nc.vector.memset(u2[:], 0.0).then_inc(w_ready, 1)
            dve.wait_ge(turned_w, 1)
            for k in range(2):
                ch.put(nc.vector.tensor_copy(w0[:, 3 * k:3 * k + 3], pt[k][:, 0:3, 0:F]))
            ch.put(nc.vector.tensor_copy(w1[0:F, 0:512], po[0][0:F, :]))
            ch.link(nc.vector.tensor_copy(w1[0:F, 512:D], po[1][0:F, 0:D - 512]))
            for n, part in enumerate(PARTS):
                ch.put(nc.vector.tensor_scalar(w1[0:F, part], w1[0:F, part], coef[0:F, n:n + 1], 0.5, ALU.mult, ALU.mult))
            ch.wait()
            nc.vector.memset(stats[:], 0.0).then_inc(w_ready, 1)

            def slot_math(grp):
                qc = Chain(dve, prep, PREP * grp)
                dve.wait_ge(slots_in, 16 * GW * (grp + 1))
                qc.put(nc.vector.tensor_tensor(rel[:], slots[:, :, 9], woff[:], ALU.add))
                qc.link(nc.vector.tensor_tensor(own[:], slots[:, :, 10], wself[:], ALU.add))
                qc.put(nc.vector.tensor_scalar(woff[:], woff[:], step_off[:, 0:1], None, ALU.add))
                qc.put(nc.vector.tensor_scalar(wself[:], wself[:], step_self[:, 0:1], None, ALU.add))
                qc.link(nc.vector.tensor_scalar(far[:], rel[:], float(WN), FAR, ALU.is_ge, ALU.mult))
                qc.link(nc.vector.tensor_tensor(idx[:], own[:], far[:], ALU.add))

            def window_mask(grp, i):
                if i >= MB:
                    dve.wait_ge(looked, GW * grp + i - MB + 1)
                elif not isinstance(grp, int) or grp:
                    dve.wait_ge(looked, GW * grp)
                nc.vector.tensor_scalar(mask[:, i % MB], pos_own[:], rel[:, i:i + 1], None, ALU.is_equal).then_inc(mask_ready, 1)

            def weights(grp):
                qc = Chain(dve, prep, PREP * grp + 6)
                dve.wait_ge(looked, GW * (grp + 1))
                qc.link(nc.vector.tensor_tensor(w[:], slots[:, :, 0], look[:, :, 1], ALU.subtract))
                nc.vector.tensor_tensor(w_now[:], w[:], look[:, :, 0], ALU.add).then_inc(weights_ready, 1)
                qc.link(nc.vector.tensor_copy(rel_now[:], rel[:]))
                rows_now(grp, 0)

            def rows_now(grp, half):
                if not isinstance(grp, int) or grp:
                    for b in range(RB):
                        dve.wait_ge(gathered[b], 16 * (2 * (grp - 1) + half + 1))
                at = slice(RB * half, RB * half + RB)
                nc.vector.tensor_copy(idx_now[:, at], idx[:, at]).then_inc(idx_ready, 1)

            def spread(t, at):
                if beyond(t, RB // 2):
                    dve.wait_ge(agg_done, t + 1 - RB // 2)
                for i in (2 * at, 2 * at + 1):
                    half = slice(WN * (i % 2), WN * (i % 2) + WN)
                    nc.vector.tensor_scalar(att[:, i % RB, half], pos[:, 0:WN], rel_now[:, i:i + 1], w_now[:, i:i + 1],
                                            ALU.is_equal, ALU.mult).then_inc(att_ready, 1)

            def iteration(grp, j):
                t, at, _, ok = tile_at(grp, j, 0)
                b = at % 2
                col = slice(b, b + 1)
                lc = Chain(dve, chain, 3 * t)
                if ok:
                    dve.wait_ge(agg_done, t + 1)
                    dve.wait_ge(xb_ready, t + 1)
                    nc.vector.tensor_tensor(x[:, at, 512:D], x[:, at, 512:D], pa_tail[0:OT, :], ALU.add)\
                        .then_inc(tail_read, 1)
                    nc.vector.tensor_tensor(x[:, at, 0:512], x[:, at, 0:512], pa[b][0:OT, :], ALU.add)\
                        .then_inc(x2_ready, 1)
                    dve.wait_ge(x2_ready, t + 1)
                    for half in range(2):
                        lc.put(nc.vector.bn_stats(stats[:, b, half], x[:, at, half * (D // 2):(half + 1) * (D // 2)]))
                    lc.wait()
                    nc.vector.memset(spare[:], 0.0)
                    lc.link(nc.vector.bn_aggr(mv[:, b], stats[:, b].rearrange("p a b -> p (a b)")))
                    nc.vector.tensor_scalar(nm[:, col], mv[:, b, 0:1], -1.0, None, ALU.mult)
                    nc.vector.tensor_scalar(ve[:, col], mv[:, b, 1:2], EPS, None, ALU.add).then_inc(ve_ready, 1)
                    assert lc.n == 3, lc.n
                if next_group(grp):
                    if j == ROWS_AT:
                        slot_math(grp + 1)
                    for i in looks(j):
                        window_mask(grp + 1, i)
                t2, at2, _, ok2 = tile_at(grp, j, AHEAD)
                if ok2:
                    spread(t2, at2)
                if next_group(grp) and j == WEIGHTS_AT:
                    weights(grp + 1)
                if next_group(grp) and j == REST_AT:
                    rows_now(grp + 1, 1)
                tg, ag, _, okg = tile_at(grp, j, -3)
                gb = ag % 2
                if okg:
                    dve.wait_ge(u_ready, 2 * (tg + 1))
                    gc = Chain(dve, gelu, tg)
                    gc.link(nc.vector.tensor_scalar(u2[:, gb], u2[:, gb], 0.044715, 1.0, ALU.mult, ALU.add))
                    nc.vector.tensor_tensor(u2[:, gb], u2[:, gb], u[:, gb], ALU.mult).then_inc(t_ready, 1)
                tf, af, _, okf = tile_at(grp, j, -4)
                if okf:
                    dve.wait_ge(o_done, tf + 1)
                    nc.vector.tensor_tensor(x[:, af, 0:512], x[:, af, 0:512], po[0][0:OT, :], ALU.add)
                    nc.vector.tensor_tensor(x[:, af, 512:D], x[:, af, 512:D], po[1][0:OT, 0:D - 512], ALU.add)\
                        .then_inc(o_ready, 1)
                if okg:
                    dve.wait_ge(th_ready, tg + 1)
                    nc.vector.scalar_tensor_tensor(out=g[0:F, gb], in0=th[:, gb], scalar=1.0, in1=u[:, gb], op0=ALU.add,
                                                   op1=ALU.mult).then_inc(g_ready, 1)

            slot_math(0)
            for i in range(GW):
                window_mask(0, i)
            weights(0)
            rows_now(0, 1)
            schedule(dve, iteration)

        @block.scalar
        def _(act):
            act.wait_ge(init, 2)
            for i in range(GW // 2, GW):
                load_records(act, c, dr.rec2, slots, slots_in, i, i)
            act.wait_ge(w_ready, 2)

            def iteration(grp, j):
                tg, ag, _, okg = tile_at(grp, j, -3)
                if okg:
                    act.wait_ge(t_ready, tg + 1)
                    nc.scalar.activation(th[:, ag % 2], u2[:, ag % 2], ACT.Tanh, scale=GELU_C).then_inc(th_ready, 1)
                t, at, _, ok = tile_at(grp, j, -1)
                if ok:
                    act.wait_ge(turned, t + 1)
                    if beyond(t, 2):
                        act.wait_ge(h_done, t - 1)
                    for k in range(2):
                        nc.scalar.activation(xt[:, at % 2, 3 * k:3 * k + 3], pt[k][:, 0:3, 0:OT], ACT.Copy)\
                            .then_inc(xt_ready, 1)
                th_, ah_, _, okh = tile_at(grp, j, -2)
                if okh:
                    act.wait_ge(h_done, th_ + 1)
                    if beyond(th_, 2):
                        act.wait_ge(g_ready, th_ - 1)
                    hb = ah_ % 2
                    nc.scalar.activation(u[:, hb], hid, ACT.Identity, bias=b0[:]).then_inc(u_ready, 1)
                    nc.scalar.activation(u2[:, hb], hid, ACT.Square, bias=b0[:]).then_inc(u_ready, 1)

                t, at, _, ok = tile_at(grp, j, 0)
                if ok:
                    act.wait_ge(norm_ready, t + 1)
                    if beyond(t, 2):
                        act.wait_ge(turned, t - 1)
                    b = at % 2
                    nc.scalar.activation(xn[:, b], x[:, at], ACT.Identity, bias=shift[:, b:b + 1], scale=rstd[:, b:b + 1])\
                        .then_inc(xn_ready, 1)

            schedule(act, iteration)

        @block.tensor
        def _(pe):
            pe.wait_ge(w_ready, 2)
            for k in range(DC):
                pe.transpose(pt[k // 3][:, k % 3, 0:F], wfc[:, 128 * k:128 * k + 128], c.ident[0:F, 0:F])
            for k in range(DC):
                ins = pe.transpose(po[k // 4][0:F, 128 * (k % 4):128 * (k % 4) + 128], wpr[:, k], c.ident[:])
            ins.then_inc(turned_w, 1)

            def look_up(grp, i):
                pe.wait_ge(mask_ready, GW * grp + i + 1)
                pe.matmul(look[:, i], mask[:, i % MB], slots[:, i, 4:9:4], start=True, stop=True).then_inc(looked, 1)

            for i in range(GW):
                look_up(0, i)
            pe.wait_ge(w_ready, 3)
            pe.wait_ge(bias_in, 16)

            def iteration(grp, j):
                t, at, there, ok = tile_at(grp, j, 1)
                if ok:
                    pe.wait_ge(att_ready, 2 * (t + 1))
                    if beyond(t, 2):
                        pe.wait_ge(x2_ready, t - 1)
                    for i in (2 * at, 2 * at + 1):
                        pe.wait_ge(gathered[i % RB], 16 * (GW // RB) * there + 16 * (i // RB + 1))
                        go = dict(start=(i % 2 == 0), stop=(i % 2 == 1))
                        pe.matmul(pa[at % 2][:], att[:, i % RB], rows[:, i % RB, 0:512], **go)
                    if beyond(t, 1):
                        pe.wait_ge(tail_read, t)
                    for i in (2 * at, 2 * at + 1):
                        ins = pe.matmul(pa_tail[:], att[:, i % RB], rows[:, i % RB, 512:D], start=(i % 2 == 0),
                                        stop=(i % 2 == 1))
                    ins.then_inc(agg_done, 1)
                t, at, _, ok = tile_at(grp, j, -1)
                if ok:
                    pe.wait_ge(xn_ready, t + 1)
                    if beyond(t, 1):
                        pe.wait_ge(xt_ready, 2 * t)
                    for k in range(DC):
                        ins = pe.transpose(pt[k // 3][:, k % 3, 0:OT], xn[:, at % 2, 128 * k:128 * k + 128],
                                           c.ident[0:OT, 0:OT])
                    ins.then_inc(turned, 1)
                if next_group(grp) and j == WEIGHTS_AT:
                    pe.wait_ge(weights_ready, grp + 2)
                t, at, _, ok = tile_at(grp, j, -2)
                if ok:
                    pe.wait_ge(xt_ready, 2 * (t + 1))
                    if beyond(t, 1):
                        pe.wait_ge(u_ready, 2 * t)
                    for k in range(DC):
                        ins = pe.matmul(hid, w0[:, k], xt[:, at % 2, k], start=(k == 0), stop=(k == DC - 1))
                    ins.then_inc(h_done, 1)
                t, at, _, ok = tile_at(grp, j, -3)
                if ok:
                    pe.wait_ge(g_ready, t + 1)
                    if beyond(t, 1):
                        pe.wait_ge(o_ready, t)
                    pe.matmul(po[0][0:OT, :], g[:, at % 2], w1[:, 0:512], start=True, stop=True)
                    pe.matmul(po[1][0:OT, 0:D - 512], g[:, at % 2], w1[:, 512:D], start=True, stop=True).then_inc(o_done, 1)
                if next_group(grp) and looks(j):
                    pe.wait_ge(u_ready, 2 * (GT * grp + j - 1))
                    for i in looks(j):
                        look_up(grp + 1, i)

            schedule(pe, iteration)


class Names:
    pass


def build(nc, ins, out):
    io = {name.removeprefix("L0_gnn_").removeprefix("L0_ffn_"): ap for name, ap in ins.items()}
    dr, c = Names(), Names()
    dr.out = out
    dr.parts = nc.dram_tensor("parts", [N, 2 * D], F16).ap()
    dr.logit1, dr.logit2 = nc.dram_tensor("logit1", [N, 2 * HEADS], F32).ap(), nc.dram_tensor("logit2", [N, 2], F32).ap()
    dr.rec1, dr.rec2 = (nc.dram_tensor(f"rec{n}", [E + PAD, REC], F32).ap() for n in (1, 2))
    dr.h2, dr.x_more = nc.dram_tensor("h2", [N, D], F32).ap(), nc.dram_tensor("x_more", [N, D], F32).ap()
    with ExitStack() as ctx:
        persistent(nc, ctx, c)
        stage_constants(nc, c)
        stage_normalise(nc, c, io, dr)
        with ExitStack() as big:
            layer_weights(nc, big, c)
            stage_softmax(nc, c, io, dr.logit1, dr.rec1, HEADS, extra=Weights, tag="sm1")
            stage_layers(nc, c, io, dr)
        stage_softmax(nc, c, io, dr.logit2, dr.rec2, 1, tag="sm2")
        stage_extra_rows(nc, c, io, dr)
        stage_output(nc, c, io, dr)


def kernel(**inputs):
    import concourse.bacc as bacc
    from concourse.bass_utils import run_bass_kernel_spmd

    nc = bacc.Bacc("TRN2", target_bir_lowering=False, num_devices=1)
    arrays, ins = {}, {}
    for name, value in inputs.items():
        a = np.ascontiguousarray(value)
        arrays[f"in_{name}_dram"] = a
        ins[name] = nc.dram_tensor(f"in_{name}_dram", a.shape, mybir.dt.from_np(a.dtype), kind="ExternalInput").ap()
    out = nc.dram_tensor("out_0_dram", [N, D], F32, kind="ExternalOutput").ap()
    build(nc, ins, out)
    r = run_bass_kernel_spmd(nc, [arrays], core_ids=[0])
    return r.results[0]["out_0_dram"]
```
